# Optimizing a Trainium2 kernel written in Bass

```python
import numpy as np
import jax
import jax.numpy as jnp

def _softmax(x, axis=-1):
    return jax.nn.softmax(x, axis=axis)

def _gelu(x):
    return jax.nn.gelu(x, approximate=True)

def _silu(x):
    return jax.nn.silu(x)

def _sigmoid(x):
    return jax.nn.sigmoid(x)

def _layernorm(x, axis=-1, eps=1e-05):
    m = jnp.mean(x, axis=axis, keepdims=True)
    v = jnp.var(x, axis=axis, keepdims=True)
    return (x - m) / jnp.sqrt(v + eps)

def _scatter_add(tgt, idx, src, axis=0):
    return tgt.at[idx].add(src)

def _segment_sum(src, seg, n):
    return jax.ops.segment_sum(src, seg, n)
kernel_name = 'mk_gps_d1_gnn_r64_165ba9'

def setup_inputs(seed: int=0):
    np.random.seed(seed)
    _w = jnp.asarray

    def _rec_inputs():
        import jax
        import jax.numpy as jnp
        _gk = jax.random.key(seed)
        x = -0.0002117 + 1 * jax.random.normal(jax.random.fold_in(_gk, 1), (10000, 512), jnp.float32)
        src = jax.random.randint(jax.random.fold_in(_gk, 2), (2500,), 0, 10000, jnp.int32)
        dst = jax.random.randint(jax.random.fold_in(_gk, 3), (2500,), 0, 10000, jnp.int32)
        _o = jnp.argsort(dst, stable=True)
        src = src[_o]
        dst = dst[_o]
        edge_attr_64 = -5.3897e-05 + 0.999841 * jax.random.normal(jax.random.fold_in(_gk, 11), (2500, 64), jnp.float32)
        return (x, src, dst, edge_attr_64)
    x, src, dst, edge_attr_64 = _rec_inputs()

    def _L0_gnn_setup():
        import jax, jax.numpy as jnp
        import numpy as np
        N, E, H, ED = (50000, 6250, 512, 64)
        BN_EPS = 1e-05

        def _bn(h, g, b):
            mu = jnp.mean(h, axis=0)
            var = jnp.mean(jnp.square(h - mu), axis=0)
            return (h - mu) * jax.lax.rsqrt(var + BN_EPS) * g + b
        key = jax.random.key(seed)
        ks = jax.random.split(key, 8)
        s = lambda d: 1.0 / np.sqrt(d)
        return {'x': jax.random.normal(ks[0], (N, H), jnp.float32), 'edge_attr': jax.random.normal(ks[1], (E, ED), jnp.float32), 'edge_index': jax.random.randint(ks[2], (2, E), 0, N, jnp.int32), 'W_e': jax.random.normal(ks[3], (ED, H), jnp.float32) * s(ED), 'b_e': jnp.zeros((H,), jnp.float32), 'W1': jax.random.normal(ks[4], (H, 2 * H), jnp.float32) * s(H), 'b1': jnp.zeros((2 * H,), jnp.float32), 'g1': jnp.ones((2 * H,), jnp.float32), 'beta1': jnp.zeros((2 * H,), jnp.float32), 'W2': jax.random.normal(ks[5], (2 * H, H), jnp.float32) * s(2 * H), 'b2': jnp.zeros((H,), jnp.float32), 'g2': jnp.ones((H,), jnp.float32), 'beta2': jnp.zeros((H,), jnp.float32), 'eps': jnp.zeros((), jnp.float32)}
    _L0_gnn_all = _L0_gnn_setup()
    _L0_gnn_in = {k: v for k, v in _L0_gnn_all.items() if k in ('W_e', 'b_e', 'W1', 'b1', 'g1', 'beta1', 'W2', 'b2', 'g2', 'beta2', 'eps')}
    del _L0_gnn_all

    def _L0_mix_setup():
        import jax, jax.numpy as jnp
        import numpy as np
        DIM = 512
        NUM_HEADS = 8
        HEAD_DIM = DIM // NUM_HEADS
        EPS = 1e-06

        def _feature_map(x):
            return jax.nn.elu(x) + 1.0
        key = jax.random.key(seed)
        k_x, k_qkv, k_out, k_b = jax.random.split(key, 4)
        B, N = (8, 64)
        x = jax.random.normal(k_x, (B, N, DIM), dtype=jnp.float32)
        s_qkv = 1.0 / np.sqrt(DIM)
        W_qkv = jax.random.uniform(k_qkv, (DIM, 3 * DIM), minval=-s_qkv, maxval=s_qkv, dtype=jnp.float32)
        W_out = jax.random.uniform(k_out, (DIM, DIM), minval=-s_qkv, maxval=s_qkv, dtype=jnp.float32)
        b_out = jax.random.uniform(k_b, (DIM,), minval=-s_qkv, maxval=s_qkv, dtype=jnp.float32)
        return {'x': x, 'W_qkv': W_qkv, 'W_out': W_out, 'b_out': b_out}
    _L0_mix_all = _L0_mix_setup()
    _L0_mix_in = {k: v for k, v in _L0_mix_all.items() if k in ('W_qkv', 'W_out', 'b_out')}
    del _L0_mix_all

    def _L0_ffn_setup():
        import jax, jax.numpy as jnp
        import numpy as np
        EPS = 1e-05
        TOP_K = 2

        def layer_norm(x, g, b):
            m = x.mean(-1, keepdims=True)
            v = ((x - m) ** 2).mean(-1, keepdims=True)
            return (x - m) / jnp.sqrt(v + EPS) * g + b
        key = jax.random.key(seed)
        ks = jax.random.split(key, 8)
        B, S, D, E, H = (8, 512, 512, 8, 32)
        x = jax.random.normal(ks[0], (B, S, D), dtype=jnp.float32)
        Wg = jax.random.normal(ks[1], (D, E), dtype=jnp.float32) * 0.02
        W1 = jax.random.normal(ks[2], (E, D, H), dtype=jnp.float32) * 0.02
        b1 = jnp.zeros((E, H), dtype=jnp.float32)
        W2 = jax.random.normal(ks[3], (E, H, D), dtype=jnp.float32) * 0.02
        b2 = jnp.zeros((E, D), dtype=jnp.float32)
        ln_g = jnp.ones((D,), dtype=jnp.float32)
        ln_b = jnp.zeros((D,), dtype=jnp.float32)
        out_g = jnp.ones((D,), dtype=jnp.float32)
        out_b = jnp.zeros((D,), dtype=jnp.float32)
        return {'x': x, 'Wg': Wg, 'W1': W1, 'b1': b1, 'W2': W2, 'b2': b2, 'ln_g': ln_g, 'ln_b': ln_b, 'out_g': out_g, 'out_b': out_b}
    _L0_ffn_all = _L0_ffn_setup()
    _L0_ffn_in = {k: v for k, v in _L0_ffn_all.items() if k in ('Wg', 'W1', 'b1', 'W2', 'b2', 'ln_g', 'ln_b', 'out_g', 'out_b')}
    del _L0_ffn_all
    return {'x': x, 'src': src, 'dst': dst, 'edge_attr_64': edge_attr_64, 'L0_gnn_W_e': _L0_gnn_in['W_e'], 'L0_gnn_b_e': _L0_gnn_in['b_e'], 'L0_gnn_W1': _L0_gnn_in['W1'], 'L0_gnn_b1': _L0_gnn_in['b1'], 'L0_gnn_g1': _L0_gnn_in['g1'], 'L0_gnn_beta1': _L0_gnn_in['beta1'], 'L0_gnn_W2': _L0_gnn_in['W2'], 'L0_gnn_b2': _L0_gnn_in['b2'], 'L0_gnn_g2': _L0_gnn_in['g2'], 'L0_gnn_beta2': _L0_gnn_in['beta2'], 'L0_gnn_eps': _L0_gnn_in['eps'], 'L0_mix_W_qkv': _L0_mix_in['W_qkv'], 'L0_mix_W_out': _L0_mix_in['W_out'], 'L0_mix_b_out': _L0_mix_in['b_out'], 'L0_ffn_Wg': _L0_ffn_in['Wg'], 'L0_ffn_W1': _L0_ffn_in['W1'], 'L0_ffn_b1': _L0_ffn_in['b1'], 'L0_ffn_W2': _L0_ffn_in['W2'], 'L0_ffn_b2': _L0_ffn_in['b2'], 'L0_ffn_ln_g': _L0_ffn_in['ln_g'], 'L0_ffn_ln_b': _L0_ffn_in['ln_b'], 'L0_ffn_out_g': _L0_ffn_in['out_g'], 'L0_ffn_out_b': _L0_ffn_in['out_b']}

def reference(x, src, dst, edge_attr_64, L0_gnn_W_e, L0_gnn_b_e, L0_gnn_W1, L0_gnn_b1, L0_gnn_g1, L0_gnn_beta1, L0_gnn_W2, L0_gnn_b2, L0_gnn_g2, L0_gnn_beta2, L0_gnn_eps, L0_mix_W_qkv, L0_mix_W_out, L0_mix_b_out, L0_ffn_Wg, L0_ffn_W1, L0_ffn_b1, L0_ffn_W2, L0_ffn_b2, L0_ffn_ln_g, L0_ffn_ln_b, L0_ffn_out_g, L0_ffn_out_b):
    import jax
    import jax.numpy as jnp

    def _L0_gnn_ref(x, edge_attr, edge_index, W_e, b_e, W1, b1, g1, beta1, W2, b2, g2, beta2, eps):
        import jax, jax.numpy as jnp
        import numpy as np
        N, E, H, ED = (50000, 6250, 512, 64)
        BN_EPS = 1e-05

        def _bn(h, g, b):
            mu = jnp.mean(h, axis=0)
            var = jnp.mean(jnp.square(h - mu), axis=0)
            return (h - mu) * jax.lax.rsqrt(var + BN_EPS) * g + b
        src, dst = (edge_index[0], edge_index[1])
        msg = jax.nn.relu(x[src] + edge_attr @ W_e + b_e)
        aggr = jax.ops.segment_sum(msg, dst, num_segments=x.shape[0])
        h = (1.0 + eps) * x + aggr
        h = jax.nn.silu(_bn(h @ W1 + b1, g1, beta1))
        h = h @ W2 + b2
        return jax.nn.silu(_bn(h, g2, beta2))

    def _L0_mix_ref(x, W_qkv, W_out, b_out):
        import jax, jax.numpy as jnp
        import numpy as np
        DIM = 512
        NUM_HEADS = 8
        HEAD_DIM = DIM // NUM_HEADS
        EPS = 1e-06

        def _feature_map(x):
            return jax.nn.elu(x) + 1.0
        B, N, C = x.shape
        H, D = (NUM_HEADS, HEAD_DIM)
        qkv = x @ W_qkv
        qkv = qkv.reshape(B, N, 3, H, D).transpose(2, 0, 3, 1, 4)
        q, k, v = (qkv[0], qkv[1], qkv[2])
        q_phi = _feature_map(q)
        k_phi = _feature_map(k)
        KV = jnp.einsum('bhnd,bhne->bhde', k_phi, v)
        K_sum = k_phi.sum(axis=2)
        denom = jnp.einsum('bhnd,bhd->bhn', q_phi, K_sum)[..., None] + EPS
        out = jnp.einsum('bhnd,bhde->bhne', q_phi, KV) / denom
        out = out.transpose(0, 2, 1, 3).reshape(B, N, C)
        return out @ W_out + b_out

    def _L0_ffn_ref(x, Wg, W1, b1, W2, b2, ln_g, ln_b, out_g, out_b):
        import jax, jax.numpy as jnp
        import numpy as np
        EPS = 1e-05
        TOP_K = 2

        def layer_norm(x, g, b):
            m = x.mean(-1, keepdims=True)
            v = ((x - m) ** 2).mean(-1, keepdims=True)
            return (x - m) / jnp.sqrt(v + EPS) * g + b
        xn = layer_norm(x, ln_g, ln_b)
        logits = jnp.einsum('bsd,de->bse', xn, Wg)
        probs = jax.nn.softmax(logits, axis=-1)
        top_p, top_i = jax.lax.top_k(probs, TOP_K)
        conf = top_p / top_p.sum(-1, keepdims=True)
        h = jax.nn.gelu(jnp.einsum('bsd,edh->bseh', xn, W1) + b1)
        o = jnp.einsum('bseh,ehd->bsed', h, W2) + b2
        sel = jnp.take_along_axis(o, top_i[..., None], axis=2)
        combined = jnp.einsum('bskd,bsk->bsd', sel, conf)
        return layer_norm(x + combined, out_g, out_b)
    edge_index = jnp.stack([src, dst])
    xn = _layernorm(x, axis=-1)
    x = x + _L0_gnn_ref(xn, edge_attr_64, edge_index, L0_gnn_W_e, L0_gnn_b_e, L0_gnn_W1, L0_gnn_b1, L0_gnn_g1, L0_gnn_beta1, L0_gnn_W2, L0_gnn_b2, L0_gnn_g2, L0_gnn_beta2, L0_gnn_eps) + _L0_mix_ref(xn[None], L0_mix_W_qkv, L0_mix_W_out, L0_mix_b_out)[0]
    x = x + _L0_ffn_ref(_layernorm(x, axis=-1)[None], L0_ffn_Wg, L0_ffn_W1, L0_ffn_b1, L0_ffn_W2, L0_ffn_b2, L0_ffn_ln_g, L0_ffn_ln_b, L0_ffn_out_g, L0_ffn_out_b)[0]
    return x

_drawn_inputs = setup_inputs


def setup_inputs(seed=0):
    import zlib

    import numpy as np

    out = dict(_drawn_inputs(seed))
    spreads = {'L0_gnn_b_e': (0.0, 0.401),
     'L0_gnn_b1': (0.0, 2.0),
     'L0_gnn_g1': (1.0, 0.2),
     'L0_gnn_beta1': (0.0, 0.1),
     'L0_gnn_b2': (0.0, 2.0),
     'L0_gnn_g2': (1.0, 0.2),
     'L0_gnn_beta2': (0.0, 0.1),
     'L0_ffn_b1': (0.0, 0.8),
     'L0_ffn_b2': (0.0, 0.334),
     'L0_ffn_ln_g': (1.0, 0.6),
     'L0_ffn_ln_b': (0.0, 0.687),
     'L0_ffn_out_g': (1.0, 0.2),
     'L0_ffn_out_b': (0.0, 0.1)}
    factors = {'L0_mix_W_qkv': 8.0,
     'L0_mix_W_out': 8.0,
     'L0_mix_b_out': 2.694,
     'L0_ffn_W1': 5.647,
     'L0_ffn_W2': 5.308}
    for name, (base, spread) in spreads.items():
        noise = np.random.default_rng([zlib.crc32(name.encode()), seed]).standard_normal(out[name].shape)
        drawn = base * np.exp(spread * noise) if base else spread * noise
        out[name] = jnp.asarray(drawn.astype(out[name].dtype))
    for name, factor in factors.items():
        out[name] = (out[name] * factor).astype(out[name].dtype)
    return out
```

```python
from contextlib import ExitStack

import concourse.bass as bass
from concourse import mybir

F32 = mybir.dt.float32
F16 = mybir.dt.float16
I32 = mybir.dt.int32
U32 = mybir.dt.uint32
ALU = mybir.AluOpType
ACT = mybir.ActivationFunctionType
AX = mybir.AxisListType

N = 10000
E = 2500
D = 512
ED = 64
HEADS, HD = 8, 64
NE, EH = 8, 32
P = 128
RT = 125
NT = 4
CH = RT * NT
NCH = N // CH
KT = D // P
FH = NE * EH
F1 = FH + NE
CUT = 112
WS = 64.0
QS = 256.0
NS = 2.0 ** -13
LN_EPS = 1e-5
BN_EPS = 1e-5
ATT_EPS = 1e-6
assert N == CH * NCH and E == RT * NCH


def split3(nc, out, lhs_hi, lhs_lo, rhs_hi, rhs_lo, first, last):
    nc.tensor.matmul(out, lhs_hi, rhs_hi, start=first, stop=False, skip_group_check=True)
    nc.tensor.matmul(out, lhs_hi, rhs_lo, start=False, stop=False, skip_group_check=True)
    return nc.tensor.matmul(out, lhs_lo, rhs_hi, start=False, stop=last, skip_group_check=True)


def wait(eng, tick, sem, value):
    eng.wait_ge(sem, value)
    eng.sem_inc(tick, 1)


class Chunk:

    def __init__(self, i, slot):
        self.i, self.slot, self.at = i, slot, i * 2 + slot

    def prev(self):
        return Chunk(self.i, 0) if self.slot == 1 else Chunk(self.i - 1, 1)

    def next(self):
        return Chunk(self.i, 1) if self.slot == 0 else Chunk(self.i + 1, 0)

    def count(self, per, extra):
        return self.i * (2 * per) + (self.slot * per + extra)

    def uses(self, per, extra=0):
        return self.i * per + (per + extra)


def chunk_loop(eng, body):
    body(Chunk(0, 0), 2)
    body(Chunk(0, 1), 2)
    with eng.Fori(1, NCH // 2 - 1) as i:
        body(Chunk(i, 0), 2)
        body(Chunk(i, 1), 2)
    body(Chunk(NCH // 2 - 1, 0), 1)
    body(Chunk(NCH // 2 - 1, 1), 0)


def rows(t, c):
    first = t[bass.ds(c * CH, CUT * NT), :].rearrange("(p j) d -> p (j d)", j=NT)
    rest = t[bass.ds(c * CH + CUT * NT, CH - CUT * NT), :].rearrange("(p j) d -> p (j d)", j=NT)
    return first, rest


def dma_rows_in(eng, tile, t, c, sem):
    first, rest = rows(t, c)
    flat = tile.rearrange("p j d -> p (j d)")
    eng.dma_start(flat[0:CUT, :], first).then_inc(sem, 16)
    eng.dma_start(flat[CUT:RT, :], rest).then_inc(sem, 16)


def dma_rows_out(eng, t, c, tile, sem):
    first, rest = rows(t, c)
    flat = tile.rearrange("p j d -> p (j d)")
    eng.dma_start(first, flat[0:CUT, :]).then_inc(sem, 16)
    eng.dma_start(rest, flat[CUT:RT, :]).then_inc(sem, 16)


def need(eng, sem, value):
    if isinstance(value, int) and value <= 0:
        return
    eng.wait_ge(sem, value)


class Parts:
    pass


def setup(nc, g, a):
    SMALL = 23
    with ExitStack() as ctx:
        def sb(name, shape, dt=F32):
            return ctx.enter_context(nc.sbuf_tensor(name, shape, dt))

        def sem(name):
            return ctx.enter_context(nc.semaphore(name))

        qkv_f = sb("qkv_f", [P, KT, 3 * D])
        f1_f = sb("f1_f", [P, KT, F1])
        f1g_f = sb("f1g_f", [P, KT, F1])
        f2_f = sb("f2_f", [P, 2, D])
        eb2_f = sb("eb2_f", [NE, D])
        ea = sb("ea", [RT, NCH, ED])
        lng = sb("lng", [P, KT])
        lnb = sb("lnb", [P, KT])
        b1row = sb("b1row", [1, F1])
        borow = sb("borow", [1, D])
        b1rest = sb("b1rest", [1, F1])
        borest = sb("borest", [1, D])
        b1part = sb("b1part", [1, 3, F1], F16)
        bopart = sb("bopart", [1, 3, D], F16)
        eb2part = sb("eb2part", [NE, 2, D], F16)
        eps_b = sb("eps_b", [RT, 1])
        psT = ctx.enter_context(nc.psum_tensor("psT", [P, 5, 512], F32))
        psB = ctx.enter_context(nc.psum_tensor("psB", [P, 512], F32))

        qkv_in, f_in, small_in, ea_in = (sem(n) for n in ("qkv_in", "f_in", "small_in", "ea_in"))
        placed, zeroed, consts = (sem(n) for n in ("placed", "zeroed", "consts"))
        hi_done, folded, bias_done, rest_done, ea_turned, ea_copied, lo_done, eps_done = (
            sem(n) for n in ("hi_done", "folded", "bias_done", "rest_done", "ea_turned", "ea_copied",
                             "lo_done", "eps_done"))

        with nc.Block() as block:
            @block.sync
            def _(sp):
                sp.dma_start(qkv_f[:], a["L0_mix_W_qkv"].rearrange("(k p) n -> p k n", p=P)).then_inc(qkv_in, 16)
                sp.dma_start(ea[:], a["edge_attr_64"].rearrange("(t p) f -> p t f", p=RT)).then_inc(ea_in, 16)
                for k in range(KT):
                    sp.dma_start(f1_f[:, k, 0:FH].rearrange("p (e h) -> p e h", e=NE),
                                 a["L0_ffn_W1"][:, k * P:(k + 1) * P, :].rearrange("e p h -> p e h")).then_inc(f_in, 16)
                sp.dma_start(f1_f[:, :, FH:F1], a["L0_ffn_Wg"].rearrange("(k p) e -> p k e", p=P)).then_inc(f_in, 16)
                sp.dma_start(f2_f[:], a["L0_ffn_W2"].rearrange("e h d -> (e h) d").rearrange("(k p) d -> p k d", p=P)).then_inc(f_in, 16)

            @block.scalar
            def _(act):
                def small(dst, src):
                    act.dma_start(dst, src, allow_slow_non_contiguous=True).then_inc(small_in, 16)

                small(lng[:], a["L0_ffn_ln_g"].rearrange("(k p) -> p k", p=P))
                small(lnb[:], a["L0_ffn_ln_b"].rearrange("(k p) -> p k", p=P))
                small(b1row[:, 0:FH], a["L0_ffn_b1"].rearrange("e h -> (e h)").rearrange("(a n) -> a n", a=1))
                small(borow[:], a["L0_mix_b_out"].rearrange("(a n) -> a n", a=1))
                small(eb2_f[:], a["L0_ffn_b2"])
                small(eps_b[:], a["L0_gnn_eps"].partition_broadcast(RT))
                small(g.gb1[:], a["L0_gnn_b1"].rearrange("(m p) -> p m", p=P))
                small(g.g1[:], a["L0_gnn_g1"].rearrange("(m p) -> p m", p=P))
                small(g.beta1[:], a["L0_gnn_beta1"].rearrange("(m p) -> p m", p=P))
                small(g.gb2[:], a["L0_gnn_b2"].rearrange("(m p) -> p m", p=P))
                small(g.g2[:], a["L0_gnn_g2"].rearrange("(m p) -> p m", p=P))
                small(g.beta2[:], a["L0_gnn_beta2"].rearrange("(m p) -> p m", p=P))
                small(g.we[0:ED, :], a["L0_gnn_W_e"])
                small(g.we[ED:ED + 1, :], a["L0_gnn_b_e"].rearrange("(a n) -> a n", a=1))
                small(g.out_g[:], a["L0_ffn_out_g"].partition_broadcast(RT))
                small(g.out_b[:], a["L0_ffn_out_b"].partition_broadcast(RT))
                small(g.ident[:], a["c_ident"])
                small(g.ident_h[:], a["c_ident_h"])
                small(g.before[:], a["c_before"])
                small(g.head_mask[:], a["c_head_mask"])
                small(g.spread[:], a["c_spread"])
                small(g.trash[:], a["c_trash"])
                small(g.expert[:], a["c_expert"].partition_broadcast(RT))
                act.wait_ge(qkv_in, 16)
                nc.scalar.activation(g.wqkv_hi[:], qkv_f[:], ACT.Copy, scale=WS).then_inc(hi_done, 1)
                act.wait_ge(ea_turned, 1)
                nc.scalar.copy(g.ea_t[0:ED, :].rearrange("p (t n) -> p t n", t=5), psT[0:ED, :, 0:CH]).then_inc(ea_copied, 1)
                act.wait_ge(folded, KT)
                nc.scalar.activation(g.f1_hi[:], f1g_f[:], ACT.Copy, scale=WS).then_inc(hi_done, 1)
                act.wait_ge(f_in, 6 * 16)
                nc.scalar.activation(g.f2_hi[:], f2_f[:], ACT.Copy, scale=WS).then_inc(hi_done, 1)
                act.wait_ge(small_in, SMALL * 16)
                nc.scalar.activation(eb2part[:, 0, :], eb2_f[:], ACT.Copy, scale=WS).then_inc(hi_done, 1)

            @block.vector
            def _(dve):
                nc.vector.memset(g.ones_w[:], 0.0).then_inc(zeroed, 1)
                nc.vector.memset(g.ones_q[:], 0.0).then_inc(zeroed, 1)
                nc.vector.memset(g.f1_bias[:], 0.0).then_inc(zeroed, 1)
                nc.vector.memset(g.out_bias[:], 0.0).then_inc(zeroed, 1)
                nc.vector.memset(g.eb2[:], 0.0).then_inc(zeroed, 1)
                nc.vector.memset(g.ea_t[ED:ED + 1, :], 1.0).then_inc(zeroed, 1)
                nc.vector.memset(g.zeros[:], 0.0).then_inc(zeroed, 1)
                nc.vector.memset(g.minus_half[:], -0.5).then_inc(zeroed, 1)
                nc.vector.memset(g.half[:], 0.5).then_inc(zeroed, 1)
                nc.vector.memset(g.ones_col[:], 1.0).then_inc(zeroed, 1)
                nc.vector.memset(g.zeros_h[:], 0.0).then_inc(zeroed, 1)
                nc.vector.memset(g.k_sum[:], 0.0).then_inc(zeroed, 1)
                nc.vector.memset(b1row[:, FH:F1], 0.0).then_inc(zeroed, 1)
                dve.wait_ge(zeroed, 13)
                nc.vector.memset(g.ones_w[0:3, :], 1.0).then_inc(consts, 1)
                nc.vector.memset(g.ones_q[0:3, :], QS).then_inc(consts, 1)
                dve.wait_ge(f_in, 6 * 16)
                dve.wait_ge(small_in, SMALL * 16)
                for k in range(KT):
                    nc.vector.tensor_scalar(f1g_f[:, k, :], f1_f[:, k, :], lng[:, k:k + 1], None, ALU.mult).then_inc(folded, 1)
                nc.vector.tensor_scalar(g.one_eps[:], eps_b[:], 1.0, None, ALU.add).then_inc(eps_done, 1)
                parts = [(g.wqkv_lo, qkv_f, g.wqkv_hi),
                         (g.f1_lo, f1g_f, g.f1_hi), (g.f2_lo, f2_f, g.f2_hi)]
                for n, (lo, full, hi) in enumerate(parts):
                    dve.wait_ge(hi_done, n + 1)
                    nc.vector.scalar_tensor_tensor(lo[:], full[:], WS, hi[:], ALU.mult, ALU.subtract).then_inc(lo_done, 1)
                dve.wait_ge(hi_done, 4)
                nc.vector.scalar_tensor_tensor(eb2part[:, 1, :], eb2_f[:], WS, eb2part[:, 0, :],
                                               ALU.mult, ALU.subtract).then_inc(lo_done, 1)
                dve.wait_ge(bias_done, 1)
                nc.vector.tensor_tensor(b1row[:], b1row[:], psB[0:1, 0:F1], ALU.add).then_inc(rest_done, 1)
                dve.wait_ge(rest_done, 1)
                nc.vector.tensor_scalar(b1rest[:], b1row[:], WS, None, ALU.mult).then_inc(rest_done, 1)
                nc.vector.tensor_scalar(borest[:], borow[:], WS, None, ALU.mult).then_inc(rest_done, 1)
                n = 3
                for m in range(3):
                    for part, rest in ((b1part, b1rest), (bopart, borest)):
                        dve.wait_ge(rest_done, n)
                        nc.vector.tensor_copy(part[:, m, :], rest[:]).then_inc(rest_done, 1)
                        dve.wait_ge(rest_done, n + 1)
                        nc.vector.tensor_tensor(rest[:], rest[:], part[:, m, :], ALU.subtract).then_inc(rest_done, 1)
                        n += 2

            @block.gpsimd
            def _(pool):
                pool.wait_ge(zeroed, 13)
                pool.wait_ge(consts, 2)
                pool.wait_ge(rest_done, 15)
                pool.wait_ge(lo_done, 4)
                for m in range(3):
                    pool.dma_start(g.f1_bias[m:m + 1, :], b1part[:, m, :]).then_inc(placed, 16)
                    pool.dma_start(g.out_bias[m:m + 1, :], bopart[:, m, :]).then_inc(placed, 16)
                    pool.dma_start(g.eb2[NE * m:NE * (m + 1), :], eb2part[:, 0 if m < 2 else 1, :]).then_inc(placed, 16)
                pool.dma_start(g.h_rows[N:N + RT, :], g.zeros[0:RT, :]).then_inc(placed, 16)
                pool.wait_ge(placed, 10 * 16)

            @block.tensor
            def _(pe):
                pe.wait_ge(small_in, SMALL * 16)
                pe.wait_ge(ea_in, 16)
                for t in range(NCH):
                    turned = nc.tensor.transpose(psT[0:ED, t // 4, (t % 4) * RT:(t % 4 + 1) * RT],
                                                 ea[:, t, :], g.ident[0:RT, 0:RT])
                turned.then_inc(ea_turned, 1)
                pe.wait_ge(f_in, 6 * 16)
                pe.wait_ge(small_in, SMALL * 16)
                for k in range(KT):
                    b = nc.tensor.matmul(psB[0:1, 0:F1], lnb[:, k:k + 1], f1_f[:, k, :], start=(k == 0), stop=(k == KT - 1))
                b.then_inc(bias_done, 1)


def project(nc, g, a):
    TURN = 6
    MM = 12
    with ExitStack() as ctx:
        def sb(name, shape, dt=F32):
            return ctx.enter_context(nc.sbuf_tensor(name, shape, dt))

        def sem(name):
            return ctx.enter_context(nc.semaphore(name))

        def sems(*names):
            return [sem(n) for n in names]

        x_in = sb("x_in", [RT, 2, NT, D])
        xn = sb("xn", [RT, 2, NT, D])
        h0 = sb("h0", [RT, NT, D])
        xt_hi = sb("xt_hi", [P, 2, KT, CH], F16)
        xt_lo = sb("xt_lo", [P, 2, KT, CH], F16)
        stats = sb("stats", [RT, NT, 6])
        mv = sb("mv", [RT, NT, 2])
        var_eps = sb("var_eps", [RT, NT])
        rstd = sb("rstd", [RT, NT])
        e_x = sb("e_x", [P, 2, D])
        r_x = sb("r_x", [P, 2, D])
        k_f = sb("k_f", [RT, 2, D])
        k_hi = sb("k_hi", [RT, 2, D], F16)
        k_lo = sb("k_lo", [RT, 2, D], F16)
        v_hi = sb("v_hi", [RT, 2, D], F16)
        v_lo = sb("v_lo", [RT, 2, D], F16)
        q_f = sb("q_f", [P, 2, KT, CH])
        src_i = sb("src_i", [RT, 2], I32)
        dst_i = sb("dst_i", [RT, 2], I32)
        dst_row = sb("dst_row", [RT, 2, RT], I32)
        dst_f = sb("dst_f", [RT, 1])
        x_src = sb("x_src", [RT, 2, D])
        e_stats = sb("e_stats", [RT, 6])
        e_mv = sb("e_mv", [RT, 2])
        e_var = sb("e_var", [RT, 1])
        e_rstd = sb("e_rstd", [RT, 1])
        xn_src = sb("xn_src", [RT, D])
        ea_now = sb("ea_now", [ED + 1, RT])
        msg_in = sb("msg_in", [RT, D])
        msg = sb("msg", [RT, D])
        same = sb("same", [RT, RT])
        same_before = sb("same_before", [RT, RT])
        again = sb("again", [RT, 2])
        to_trash = sb("to_trash", [RT, 1])

        turn_ps = ctx.enter_context(nc.psum_tensor("turn_ps", [P, 2, 512], F32))
        mm_ps = ctx.enter_context(nc.psum_tensor("mm_ps", [P, 4, 512], F32))
        kv_ps = ctx.enter_context(nc.psum_tensor("kv_ps", [P, 512], F32))
        ks_ps = ctx.enter_context(nc.psum_tensor("ks_ps", [P, 512], F32))

        x_loaded = sems("x_loaded0", "x_loaded1")
        dst_loaded = sems("dst_loaded0", "dst_loaded1")
        src_loaded = sems("src_loaded0", "src_loaded1")
        gathered = sems("gathered0", "gathered1")
        q_stored = sems("q_stored0", "q_stored1")
        h_stored, stats_done, mv_done, var_done, rstd_done, xn_done, h0_done = sems(
            "h_stored", "stats_done", "mv_done", "var_done", "rstd_done", "xn_done", "h0_done")
        turned, turn_hi, turn_free, mm_done, act_mm_free, v_mm_free = sems(
            "turned", "turn_hi", "turn_free", "mm_done", "act_mm_free", "v_mm_free")
        v_hi_done, phi_done, k_hi_done, k_lo_done, kv_done, pool_tick, sp_tick, dve_tick = sems(
            "v_hi_done", "phi_done", "k_hi_done", "k_lo_done", "kv_done", "pool_tick", "sp_tick", "dve_tick")
        e_mv_done, e_var_done, e_rstd_done, edge_step, ea_ready, msg_in_done, msg_done = sems(
            "e_mv_done", "e_var_done", "e_rstd_done", "edge_step", "ea_ready", "msg_in_done", "msg_done")
        STEPS = 8
        src_tiles = a["src"].rearrange("(t p) -> t p", p=RT)
        dst_tiles = a["dst"].rearrange("(t p) -> t p", p=RT)

        with nc.Block() as block:
            @block.sync
            def _(sp):
                sp.sem_inc(q_stored[0], 16)
                sp.sem_inc(q_stored[1], 16)
                sp.sem_inc(h_stored, 32)

                def load(at, s):
                    dma_rows_in(sp, x_in[:, s], a["x"], at, x_loaded[s])
                    sp.dma_start(src_i[:, s:s + 1], src_tiles[bass.ds(at, 1), :].rearrange("a p -> p a"),
                                 allow_slow_non_contiguous=True).then_inc(src_loaded[s], 16)
                    sp.dma_start(dst_i[:, s:s + 1], dst_tiles[bass.ds(at, 1), :].rearrange("a p -> p a"),
                                 allow_slow_non_contiguous=True).then_inc(dst_loaded[s], 16)
                    sp.dma_start(dst_row[:, s, :], dst_tiles[bass.ds(at, 1), :].broadcast_to([RT, RT])).then_inc(dst_loaded[s], 16)

                load(0, 0)
                load(1, 1)

                def step(c, follow):
                    s = c.slot
                    if follow == 2:
                        wait(sp, sp_tick, xn_done, c.count(NT, NT))
                        wait(sp, sp_tick, gathered[s], c.uses(16))
                        wait(sp, sp_tick, edge_step, c.count(STEPS, 7))
                        load(c.at + 2, s)
                    wait(sp, sp_tick, h0_done, c.count(NT, 2 * NT))
                    dma_rows_out(sp, g.h_rows, c.at, h0[:], h_stored)
                    wait(sp, sp_tick, phi_done, c.count(2 * NT, 2 + 2 * NT))
                    sp.dma_start(g.q_t[bass.ds(c.at, 1), :, :].rearrange("a p n -> (a p) n"),
                                 q_f[:, s].rearrange("p k n -> p (k n)")).then_inc(q_stored[s], 16)

                chunk_loop(sp, step)
                for s in range(2):
                    sp.wait_ge(q_stored[s], 16 + 16 * NCH // 2)
                sp.wait_ge(h_stored, 32 + 32 * NCH)

            @block.gpsimd
            def _(pool):
                def gather(s):
                    pool.indirect_dma_start(x_src[:, s, :], None, a["x"],
                                            bass.IndirectOffsetOnAxis(ap=src_i[:, s:s + 1], axis=0),
                                            bounds_check=N - 1, oob_is_err=True).then_inc(gathered[s], 16)

                def row_rstd(c):
                    pool.wait_ge(mv_done, c.count(NT, NT))
                    pool.sem_inc(pool_tick, 1)
                    nc.gpsimd.tensor_scalar(var_eps[:], mv[:, :, 1], LN_EPS, None, ALU.add).then_inc(var_done, 1)
                    pool.wait_ge(var_done, c.count(1, 1))
                    nc.gpsimd.tensor_tensor(rstd[:], var_eps[:], g.minus_half[0:RT, 0:NT], ALU.pow).then_inc(rstd_done, 1)

                pool.sem_inc(h0_done, NT)
                for s in range(2):
                    pool.wait_ge(src_loaded[s], 16)
                    gather(s)
                row_rstd(Chunk(0, 0))

                def step(c, follow):
                    s = c.slot
                    if follow:
                        row_rstd(c.next())
                    pool.wait_ge(e_mv_done, c.count(1, 1))
                    pool.sem_inc(pool_tick, 1)
                    nc.gpsimd.tensor_scalar(e_var[:], e_mv[:, 1:2], LN_EPS, None, ALU.add).then_inc(e_var_done, 1)
                    pool.wait_ge(e_var_done, c.count(1, 1))
                    nc.gpsimd.tensor_tensor(e_rstd[:], e_var[:], g.minus_half[0:RT, 0:1], ALU.pow).then_inc(e_rstd_done, 1)
                    pool.wait_ge(turned, c.count(TURN, 5))
                    pool.sem_inc(pool_tick, 1)
                    nc.gpsimd.tensor_copy(ea_now[:], g.ea_t[:, bass.ds(c.at * RT, RT)]).then_inc(ea_ready, 1)
                    pool.wait_ge(h_stored, c.count(32, 32))
                    pool.wait_ge(xn_done, c.count(NT, NT))
                    pool.sem_inc(pool_tick, 1)
                    for j in range(NT):
                        nc.gpsimd.tensor_scalar(h0[:, j, :], xn[:, s, j, :], g.one_eps[:], None, ALU.mult).then_inc(h0_done, 1)
                    if follow == 2:
                        pool.wait_ge(src_loaded[s], c.uses(16, 16))
                        pool.wait_ge(edge_step, c.count(STEPS, 8))
                        pool.sem_inc(pool_tick, 1)
                        gather(s)

                chunk_loop(pool, step)

            @block.scalar
            def _(act):
                act.sem_inc(act_mm_free, 8)

                def phi_parts(c, u, bank):
                    b = u % 2
                    n = RT if u < NT else P
                    w = D if u < NT else CH
                    act.wait_ge(phi_done, c.count(8, u + 1))
                    nc.scalar.activation(e_x[0:n, b, 0:w], mm_ps[0:n, bank, 0:w], ACT.Exp, scale=1 / WS)
                    nc.scalar.activation(r_x[0:n, b, 0:w], mm_ps[0:n, bank, 0:w], ACT.Relu, scale=1 / WS).then_inc(act_mm_free, 1)

                def turn_high(index, slot, k):
                    act.wait_ge(turned, index)
                    nc.scalar.copy(xt_hi[:, slot, k, :], turn_ps[:, k % 2, 0:CH]).then_inc(turn_hi, 1)

                for k in range(KT):
                    turn_high(k + 1, 0, k)

                def step(c, follow):
                    for j in range(NT):
                        act.wait_ge(mm_done, c.count(MM, 2 * j + 1))
                        phi_parts(c, j, (2 * j) % 4)
                        act.wait_ge(mm_done, c.count(MM, 2 * j + 2))
                        act.wait_ge(kv_done, c.count(NT, j + 1))
                        nc.scalar.activation(v_hi[:, j % 2, :], mm_ps[0:RT, (2 * j + 1) % 4, :], ACT.Copy,
                                             scale=1 / WS).then_inc(v_hi_done, 1)
                        act.wait_ge(phi_done, c.count(8, 2 + j + 1))
                        nc.scalar.copy(k_hi[:, j % 2, :], k_f[:, j % 2, :]).then_inc(k_hi_done, 1)
                        if j and follow:
                            turn_high(c.count(TURN, TURN + j), c.next().slot, j - 1)
                    for m in range(KT):
                        act.wait_ge(mm_done, c.count(MM, 8 + m + 1))
                        phi_parts(c, NT + m, (8 + m) % 4)
                        if m == 0 and follow:
                            turn_high(c.count(TURN, TURN + 4), c.next().slot, 3)
                        if m == 1:
                            act.wait_ge(msg_in_done, c.count(1, 1))
                            act.wait_ge(turned, c.count(TURN, TURN))
                            nc.scalar.activation(msg[:], msg_in[:], ACT.Relu).then_inc(msg_done, 1)

                chunk_loop(act, step)

            @block.vector
            def _(dve):
                def row_stats(c):
                    dve.wait_ge(x_loaded[c.slot], c.uses(32))
                    for j in range(NT):
                        nc.vector.bn_stats(stats[:, j, :], x_in[:, c.slot, j, :]).then_inc(stats_done, 1)
                    dve.wait_ge(stats_done, c.count(NT, NT))
                    dve.sem_inc(dve_tick, 1)
                    nc.vector.bn_aggr(mv[:, 0, :], stats[:, 0, :]).then_inc(mv_done, 1)
                    for j in range(1, NT):
                        nc.vector.bn_aggr(mv[:, j, :], stats[:, j, :]).then_inc(mv_done, 1)

                def normalise(c):
                    dve.wait_ge(rstd_done, c.count(1, 1))
                    for j in range(NT):
                        nc.vector.tensor_scalar(xn[:, c.slot, j, :], x_in[:, c.slot, j, :], mv[:, j, 0:1],
                                                rstd[:, j:j + 1], ALU.subtract, ALU.mult).then_inc(xn_done, 1)

                def phi(c, u, out):
                    n = RT if u < NT else P
                    w = D if u < NT else CH
                    dve.wait_ge(act_mm_free, c.count(8, 8 + u + 1))
                    nc.vector.scalar_tensor_tensor(out, e_x[0:n, u % 2, 0:w], 1.0, r_x[0:n, u % 2, 0:w],
                                                   ALU.min, ALU.add).then_inc(phi_done, 1)

                def turn_low(index, slot, k, by=1):
                    dve.wait_ge(turn_hi, index)
                    nc.vector.tensor_tensor(xt_lo[:, slot, k, :], turn_ps[:, k % 2, 0:CH], xt_hi[:, slot, k, :],
                                            ALU.subtract).then_inc(turn_free, by)

                dve.sem_inc(phi_done, 2)
                first = Chunk(0, 0)
                row_stats(first)
                normalise(first)
                for k in range(KT):
                    turn_low(k + 1, 0, k, 1 if k < KT - 1 else 3)

                def step(c, follow):
                    s = c.slot
                    nxt = c.next()
                    if follow:
                        dve.wait_ge(xn_done, c.count(NT, NT))
                        row_stats(nxt)
                    dve.wait_ge(gathered[s], c.uses(16))
                    nc.vector.bn_stats(e_stats[:], x_src[:, s, :]).then_inc(edge_step, 1)
                    dve.wait_ge(edge_step, c.count(STEPS, 1))
                    dve.sem_inc(dve_tick, 1)
                    nc.vector.bn_aggr(e_mv[:], e_stats[:]).then_inc(e_mv_done, 1)
                    for j in range(NT):
                        phi(c, j, k_f[:, j % 2, :])
                        dve.wait_ge(v_hi_done, c.count(NT, j + 1))
                        nc.vector.scalar_tensor_tensor(v_lo[:, j % 2, :], mm_ps[0:RT, (2 * j + 1) % 4, :], 1 / WS,
                                                       v_hi[:, j % 2, :], ALU.mult, ALU.subtract).then_inc(v_mm_free, 1)
                        dve.wait_ge(k_hi_done, c.count(NT, j + 1))
                        nc.vector.tensor_tensor(k_lo[:, j % 2, :], k_f[:, j % 2, :], k_hi[:, j % 2, :],
                                                ALU.subtract).then_inc(k_lo_done, 1)
                        if j == 0:
                            if follow:
                                dve.wait_ge(h0_done, c.count(NT, NT))
                                normalise(nxt)
                        elif follow:
                            turn_low(c.count(KT, KT + j), nxt.slot, j - 1)
                        if j == 1:
                            dve.wait_ge(dst_loaded[s], c.uses(32))
                            nc.vector.tensor_copy(dst_f[:], dst_i[:, s:s + 1]).then_inc(edge_step, 1)
                            dve.wait_ge(edge_step, c.count(STEPS, 2))
                            dve.wait_ge(turned, c.count(TURN, TURN))
                            nc.vector.tensor_scalar(same[:], dst_row[:, s, :], dst_f[:], None, ALU.is_equal).then_inc(edge_step, 1)
                            nc.vector.tensor_tensor(to_trash[:], g.trash[:], dst_f[:], ALU.subtract)
                            dve.wait_ge(edge_step, c.count(STEPS, 3))
                            nc.vector.tensor_tensor(same_before[:], same[:], g.before[:], ALU.mult).then_inc(edge_step, 1)
                        if j == 2:
                            dve.wait_ge(edge_step, c.count(STEPS, 4))
                            nc.vector.tensor_reduce(again[:, 0:1], same_before[:], AX.X, ALU.add).then_inc(edge_step, 1)
                            dve.wait_ge(edge_step, c.count(STEPS, 5))
                            nc.vector.tensor_scalar(again[:, 1:2], again[:, 0:1], 1.0, None, ALU.min).then_inc(edge_step, 1)
                            dve.wait_ge(edge_step, c.count(STEPS, 6))
                            nc.vector.scalar_tensor_tensor(g.target[:, bass.ds(c.at, 1)], again[:, 1:2], to_trash[:],
                                                           dst_f[:], ALU.mult, ALU.add).then_inc(edge_step, 1)
                            dve.wait_ge(e_rstd_done, c.count(1, 1))
                            nc.vector.tensor_scalar(xn_src[:], x_src[:, s, :], e_mv[:, 0:1], e_rstd[:],
                                                    ALU.subtract, ALU.mult).then_inc(edge_step, 1)
                    dve.wait_ge(q_stored[s], c.uses(16))
                    for m in range(KT):
                        phi(c, NT + m, q_f[:, s, m, :])
                        if m == 0 and follow:
                            turn_low(c.count(KT, 2 * KT), nxt.slot, 3)
                        if m == 1:
                            dve.wait_ge(turned, c.count(TURN, TURN + (5 if follow else 1)))
                            dve.wait_ge(edge_step, c.count(STEPS, 8))
                            nc.vector.tensor_tensor(msg_in[:], turn_ps[0:RT, 0, :], xn_src[:], ALU.add).then_inc(msg_in_done, 1)
                    dve.wait_ge(turned, c.count(TURN, TURN + (6 if follow else 2)))
                    nc.vector.tensor_copy(g.totals[:, bass.ds(c.at, 1), :].rearrange("p a d -> p (a d)"),
                                          turn_ps[0:RT, 1, :]).then_inc(turn_free, 2)

                chunk_loop(dve, step)
                dve.wait_ge(kv_done, 4 + NT * NCH)
                for h in range(KT):
                    nc.vector.scalar_tensor_tensor(g.kv[:, h, :], kv_ps[:, h * P:(h + 1) * P], NS, g.head_mask[:],
                                                   ALU.mult, ALU.mult)
                flat = g.k_sum[:].rearrange("p k h -> p (k h)")
                step10 = 2 * KT + 2
                nc.vector.tensor_scalar(flat[0:HD, 0:KT * HEADS:step10], ks_ps[0:HD, 0:KT], NS, None, ALU.mult)
                nc.vector.tensor_scalar(flat[HD:P, 1:KT * HEADS:step10], ks_ps[HD:P, 0:KT], NS, None, ALU.mult)

            @block.tensor
            def _(pe):
                def transposes(slot, k, by=1):
                    for j in range(NT):
                        t = nc.tensor.transpose(turn_ps[:, k % 2, j * RT:(j + 1) * RT],
                                                xn[:, slot, j, k * P:(k + 1) * P], g.ident[0:RT, 0:RT])
                    t.then_inc(turned, by)

                nc.tensor.matmul(kv_ps[:], g.zeros_h[:, 0:P], g.zeros_h[:], start=True, stop=False).then_inc(kv_done, 1)
                nc.tensor.matmul(ks_ps[:, 0:KT], g.zeros_h[:, 0:P], g.zeros_h[:, 0:KT], start=True, stop=False).then_inc(kv_done, 1)
                pe.wait_ge(xn_done, NT)
                for k in range(KT):
                    if k >= 2:
                        pe.wait_ge(turn_free, k - 1)
                    transposes(0, k, 1 if k < KT - 1 else 3)

                def row_product(c, j, w0, bank):
                    s = c.slot
                    rows_ = slice(j * RT, (j + 1) * RT)
                    for k in range(KT):
                        last = split3(nc, mm_ps[0:RT, bank, :], xt_hi[:, s, k, rows_], xt_lo[:, s, k, rows_],
                                      g.wqkv_hi[:, k, w0:w0 + D], g.wqkv_lo[:, k, w0:w0 + D], k == 0, k == KT - 1)
                    last.then_inc(mm_done, 1)

                def sums(c, j):
                    pe.wait_ge(v_mm_free, c.count(NT, j + 1))
                    pe.wait_ge(k_lo_done, c.count(NT, j + 1))
                    b = j % 2
                    for h in range(KT):
                        hs = slice(h * P, (h + 1) * P)
                        split3(nc, kv_ps[:, hs], v_hi[:, b, hs], v_lo[:, b, hs], k_hi[:, b, hs], k_lo[:, b, hs], False, False)
                        nc.tensor.matmul(ks_ps[:, h:h + 1], k_hi[:, b, hs], g.ones_col[0:RT, :], start=False, stop=False, skip_group_check=True)
                        last = nc.tensor.matmul(ks_ps[:, h:h + 1], k_lo[:, b, hs], g.ones_col[0:RT, :], start=False, stop=False, skip_group_check=True)
                    last.then_inc(kv_done, 1)

                def step(c, follow):
                    s = c.slot
                    nxt = c.next()
                    pe.wait_ge(turn_free, c.count(TURN, 4))
                    for j in range(NT):
                        pe.wait_ge(act_mm_free, c.count(8, [5, 7, 9, 10][j]))
                        row_product(c, j, D, (2 * j) % 4)
                        if j < 2:
                            pe.wait_ge(act_mm_free, c.count(8, [6, 8][j]))
                        else:
                            pe.wait_ge(v_mm_free, c.count(NT, j - 1))
                        row_product(c, j, 2 * D, (2 * j + 1) % 4)
                        if j:
                            sums(c, j - 1)
                            if follow:
                                pe.wait_ge(xn_done, nxt.count(NT, NT))
                                pe.wait_ge(turn_free, c.count(TURN, TURN + j - 2))
                                transposes(nxt.slot, j - 1)
                    for m in range(KT):
                        if m % 2 == 0:
                            pe.wait_ge(act_mm_free, c.count(8, [11, None, 12][m]))
                        else:
                            pe.wait_ge(v_mm_free, c.count(NT, [None, 3, None, 4][m]))
                        for k in range(KT):
                            w = slice(m * P, (m + 1) * P)
                            last = split3(nc, mm_ps[:, m, 0:CH], g.wqkv_hi[:, k, w], g.wqkv_lo[:, k, w],
                                          xt_hi[:, s, k, :], xt_lo[:, s, k, :], k == 0, k == KT - 1)
                        last.then_inc(mm_done, 1)
                        if m == 0:
                            sums(c, NT - 1)
                            if follow:
                                pe.wait_ge(turn_free, c.count(TURN, TURN + 2))
                                transposes(nxt.slot, 3)
                        if m == 1:
                            pe.wait_ge(turn_free, c.count(TURN, TURN + (3 if follow else -1)))
                            pe.wait_ge(ea_ready, c.count(1, 1))
                            nc.tensor.matmul(turn_ps[0:RT, 0, :], ea_now[:], g.we[:], start=True, stop=True).then_inc(turned, 1)
                    pe.wait_ge(turn_free, c.count(TURN, TURN + (4 if follow else 0)))
                    pe.wait_ge(msg_done, c.count(1, 1))
                    nc.tensor.matmul(turn_ps[0:RT, 1, :], same[:], msg[:], start=True, stop=True).then_inc(turned, 1)

                chunk_loop(pe, step)
                nc.tensor.matmul(kv_ps[:], g.zeros_h[:, 0:P], g.zeros_h[:], start=False, stop=True).then_inc(kv_done, 1)
                nc.tensor.matmul(ks_ps[:, 0:KT], g.zeros_h[:, 0:P], g.zeros_h[:, 0:KT], start=False, stop=True).then_inc(kv_done, 1)


def attend(nc, g, a):
    with ExitStack() as ctx:
        def sb(name, shape, dt=F32):
            return ctx.enter_context(nc.sbuf_tensor("at_" + name, shape, dt))

        def sems(*names):
            return [ctx.enter_context(nc.semaphore("at_" + n)) for n in names]

        wo_f = sb("wo_f", [P, KT, D])
        m_hi = sb("m_hi", [P, KT, D], F16)
        m_lo = sb("m_lo", [P, KT, D], F16)
        q_in = sb("q_in", [P, 2, KT, CH])
        x_in = sb("x_in", [RT, 2, NT, D])
        den_e = sb("den_e", [RT, NT, HEADS])
        rden = sb("rden", [RT, NT, HEADS])
        rden_parts = sb("rden_parts", [RT, NT, P], F16)
        rden_t = sb("rden_t", [P, CH], F16)
        q_norm = sb("q_norm", [P, 2, CH])
        qn_hi = sb("qn_hi", [P, 2, KT, CH], F16)
        qn_lo = sb("qn_lo", [P, 2, KT, CH], F16)
        r_out = sb("r_out", [RT, 2, NT, D])
        den_ps = ctx.enter_context(nc.psum_tensor("den_ps", [P, 512], F32))
        rt_ps = ctx.enter_context(nc.psum_tensor("rt_ps", [P, 8, P], F16))
        spread_ps = ctx.enter_context(nc.psum_tensor("spread_ps", [P, 2, 512], F32))
        o_ps = ctx.enter_context(nc.psum_tensor("o_ps", [P, 4, 512], F32))

        w_in, q_in0, q_in1, x_in0, x_in1, r_st0, r_st1 = sems("w_in", "q_loaded0", "q_loaded1", "x_loaded0", "x_loaded1", "r_stored0", "r_stored1")
        q_loaded, x_loaded, r_stored = (q_in0, q_in1), (x_in0, x_in1), (r_st0, r_st1)
        m_mm, m_hi_done, m_lo_done = sems("m_mm", "m_hi_done", "m_lo_done")
        den_done, den_step, rden_done, rden_turned, rden_t_done = sems(
            "den_done", "den_step", "rden_done", "rden_turned", "rden_t_done")
        spread_done, qn_done, qn_hi_done, qn_lo_done, o_done, r_done, added, zero_done = sems(
            "spread_done", "qn_done", "qn_hi_done", "qn_lo_done", "o_done", "r_done", "added", "zero_done")
        sp_tick, dve_tick = sems("sp_tick", "dve_tick")

        with nc.Block() as block:
            @block.sync
            def _(sp):
                def load_q(at, s):
                    sp.dma_start(q_in[:, s].rearrange("p k n -> p (k n)"),
                                 g.q_t[bass.ds(at, 1), :, :].rearrange("a p n -> (a p) n")).then_inc(q_loaded[s], 16)

                sp.dma_start(wo_f[:], a["L0_mix_W_out"].rearrange("(k p) n -> p k n", p=P)).then_inc(w_in, 16)
                for s in range(2):
                    load_q(s, s)
                    dma_rows_in(sp, x_in[:, s], a["x"], s, x_loaded[s])
                sp.sem_inc(r_stored[0], 32)
                sp.sem_inc(r_stored[1], 32)

                def step(c, follow):
                    s = c.slot
                    if follow == 2:
                        wait(sp, sp_tick, qn_done, c.count(KT, KT))
                        load_q(c.at + 2, s)
                    wait(sp, sp_tick, r_done, c.count(NT, 2 * NT))
                    dma_rows_out(sp, g.r_rows, c.at, r_out[:, s], r_stored[s])
                    if follow == 2:
                        dma_rows_in(sp, x_in[:, s], a["x"], c.at + 2, x_loaded[s])

                chunk_loop(sp, step)
                for s in range(2):
                    sp.wait_ge(r_stored[s], 32 + 32 * NCH // 2)

            @block.gpsimd
            def _(pool):
                for t in range(NCH):
                    need(pool, added, 16 * t)
                    pool.indirect_dma_start(g.h_rows, bass.IndirectOffsetOnAxis(ap=g.target[:, t:t + 1], axis=0),
                                            g.totals[:, t, :], None, compute_op=ALU.add,
                                            bounds_check=N + RT - 1, oob_is_err=True).then_inc(added, 16)
                pool.wait_ge(added, 16 * NCH)

            @block.scalar
            def _(act):
                for k in range(KT):
                    act.wait_ge(m_mm, k + 1)
                    nc.scalar.activation(m_hi[:, k, :], o_ps[:, k, :], ACT.Copy, scale=WS).then_inc(m_hi_done, 1)

                def turn(c):
                    act.wait_ge(rden_turned, c.count(1, 1))
                    nc.scalar.copy(rden_t[:].rearrange("p (j n) -> p j n", j=NT), rt_ps[:, 0:NT, 0:RT]).then_inc(rden_t_done, 1)

                def high(c, k):
                    act.wait_ge(qn_done, c.count(KT, k + 1))
                    nc.scalar.copy(qn_hi[:, c.slot, k, :], q_norm[:, k % 2, :]).then_inc(qn_hi_done, 1)

                turn(Chunk(0, 0))
                for k in range(KT):
                    high(Chunk(0, 0), k)

                def step(c, follow):
                    if follow:
                        turn(c.next())
                        for k in range(KT):
                            high(c.next(), k)

                chunk_loop(act, step)

            @block.vector
            def _(dve):
                nc.vector.memset(rden_parts[:], 0.0).then_inc(zero_done, 1)
                for k in range(KT):
                    dve.wait_ge(m_hi_done, k + 1)
                    nc.vector.scalar_tensor_tensor(m_lo[:, k, :], o_ps[:, k, :], WS, m_hi[:, k, :],
                                                   ALU.mult, ALU.subtract).then_inc(m_lo_done, 1)
                dve.wait_ge(zero_done, 1)
                dve.sem_inc(r_done, NT)

                def reciprocals(c):
                    dve.wait_ge(den_done, c.count(1, 1))
                    flat = den_ps[0:RT, 0:NT * HEADS].rearrange("p (j h) -> p j h", j=NT)
                    nc.vector.tensor_scalar(den_e[:], flat, 1 / QS, ATT_EPS * NS / QS, ALU.mult, ALU.add).then_inc(den_step, 1)
                    dve.wait_ge(den_step, c.count(2, 1))
                    nc.vector.reciprocal(rden[:], den_e[:]).then_inc(den_step, 1)
                    dve.wait_ge(den_step, c.count(2, 2))
                    need(dve, rden_turned, c.count(1, 0))
                    nc.vector.tensor_copy(rden_parts[:, :, 0:HEADS], rden[:]).then_inc(rden_done, 1)
                    dve.wait_ge(rden_done, c.count(2, 1))
                    nc.vector.tensor_tensor(rden_parts[:, :, HEADS:2 * HEADS], rden[:], rden_parts[:, :, 0:HEADS],
                                            ALU.subtract).then_inc(rden_done, 1)

                def normalise(c, k):
                    dve.wait_ge(spread_done, c.count(KT, k + 1))
                    nc.vector.tensor_tensor(q_norm[:, k % 2, :], spread_ps[:, k % 2, 0:CH], q_in[:, c.slot, k, :],
                                            ALU.mult).then_inc(qn_done, 1)
                    dve.wait_ge(qn_hi_done, c.count(KT, k + 1))
                    nc.vector.tensor_tensor(qn_lo[:, c.slot, k, :], q_norm[:, k % 2, :], qn_hi[:, c.slot, k, :],
                                            ALU.subtract).then_inc(qn_lo_done, 1)

                reciprocals(Chunk(0, 0))
                for k in range(KT):
                    normalise(Chunk(0, 0), k)

                def step(c, follow):
                    s = c.slot
                    if follow:
                        reciprocals(c.next())
                    dve.wait_ge(x_loaded[s], c.uses(32))
                    dve.wait_ge(r_stored[s], c.uses(32))
                    for j in range(NT):
                        dve.wait_ge(o_done, c.count(NT, j + 1))
                        nc.vector.scalar_tensor_tensor(r_out[:, s, j, :], o_ps[0:RT, j, :], 1 / (WS * QS), x_in[:, s, j, :],
                                                       ALU.mult, ALU.add).then_inc(r_done, 1)
                        if follow:
                            normalise(c.next(), j)

                chunk_loop(dve, step)

            @block.tensor
            def _(pe):
                pe.wait_ge(w_in, 16)
                for k in range(KT):
                    nc.tensor.matmul(o_ps[:, k, :], g.kv[:, k, :], wo_f[:, k, :], start=True, stop=True).then_inc(m_mm, 1)

                def denominators(c):
                    pe.wait_ge(q_loaded[c.slot], c.uses(16))
                    need(pe, den_step, c.count(2, -1))
                    for j in range(NT):
                        for k in range(KT):
                            last = nc.tensor.matmul(den_ps[0:RT, j * HEADS:(j + 1) * HEADS], q_in[:, c.slot, k, j * RT:(j + 1) * RT],
                                                    g.k_sum[:, k, :], start=(k == 0), stop=(k == KT - 1))
                    last.then_inc(den_done, 1)

                def turn(c):
                    pe.wait_ge(rden_done, c.count(2, 2))
                    need(pe, rden_t_done, c.count(1, 0))
                    for j in range(NT):
                        t = nc.tensor.transpose(rt_ps[:, j, 0:RT], rden_parts[:, j, :], g.ident_h[0:RT, 0:RT])
                    t.then_inc(rden_turned, 1)

                def spread(c, k):
                    pe.wait_ge(rden_t_done, c.count(1, 1))
                    need(pe, qn_done, c.count(KT, k - 1))
                    nc.tensor.matmul(spread_ps[:, k % 2, 0:CH], g.spread[:, k * P:(k + 1) * P], rden_t[:],
                                     start=True, stop=True).then_inc(spread_done, 1)

                first = Chunk(0, 0)
                denominators(first)
                turn(first)
                for k in range(KT):
                    spread(first, k)
                pe.wait_ge(m_lo_done, KT)

                def step(c, follow):
                    s = c.slot
                    if follow:
                        denominators(c.next())
                    pe.wait_ge(qn_lo_done, c.count(KT, KT))
                    for j in range(NT):
                        pe.wait_ge(r_done, c.count(NT, j + 1))
                        for k in range(KT):
                            js = slice(j * RT, (j + 1) * RT)
                            split3(nc, o_ps[0:RT, j, :], qn_hi[:, s, k, js], qn_lo[:, s, k, js],
                                   m_hi[:, k, :], m_lo[:, k, :], k == 0, False)
                        nc.tensor.matmul(o_ps[0:RT, j, :], g.ones_q[:], g.out_bias[:], start=False, stop=True,
                                         skip_group_check=True).then_inc(o_done, 1)
                        if follow:
                            if j == 0:
                                turn(c.next())
                            spread(c.next(), j)

                chunk_loop(pe, step)


def gnn_weights(nc, g, a):
    with ExitStack() as ctx:
        w1_f = ctx.enter_context(nc.sbuf_tensor("w1_f", [P, KT, 2 * D], F32))
        w2_f = ctx.enter_context(nc.sbuf_tensor("w2_f", [P, 2 * KT, D], F32))
        w1_in, w2_in, w_hi, w_lo = (ctx.enter_context(nc.semaphore(n)) for n in ("w1_in", "w2_in", "w_hi", "w_lo"))
        weights = ((g.w1_hi, g.w1_lo, w1_f, w1_in, "L0_gnn_W1"), (g.w2_hi, g.w2_lo, w2_f, w2_in, "L0_gnn_W2"))

        with nc.Block() as block:
            @block.sync
            def _(sp):
                for _, _, full, loaded, name in weights:
                    sp.dma_start(full[:], a[name].rearrange("(k p) n -> p k n", p=P)).then_inc(loaded, 16)

            @block.scalar
            def _(act):
                for hi, _, full, loaded, _ in weights:
                    act.wait_ge(loaded, 16)
                    nc.scalar.activation(hi[:], full[:], ACT.Copy, scale=WS).then_inc(w_hi, 1)

            @block.vector
            def _(dve):
                for n, (hi, lo, full, _, _) in enumerate(weights):
                    dve.wait_ge(w_hi, n + 1)
                    nc.vector.scalar_tensor_tensor(lo[:], full[:], WS, hi[:], ALU.mult, ALU.subtract).then_inc(w_lo, 1)


def batch_norm(nc, dve, pool_ready, pool_done, step, stats, mv, var_eps, rstd, gain, shift, scale, offset, tiles):
    for m in range(tiles):
        nc.vector.bn_aggr(mv[:, m, :], stats[:, m, :, :].rearrange("p c s -> p (c s)")).then_inc(step, 1)
    dve.wait_ge(step, tiles)
    nc.vector.tensor_scalar(var_eps[:, 0:tiles], mv[:, :, 1], BN_EPS, None, ALU.add).then_inc(pool_ready, 1)
    dve.wait_ge(pool_done, 1)
    nc.vector.tensor_tensor(scale[:, 0:tiles], gain[:, 0:tiles], rstd[:, 0:tiles], ALU.mult).then_inc(step, 1)
    dve.wait_ge(step, tiles + 1)
    nc.vector.tensor_tensor(var_eps[:, 0:tiles], mv[:, :, 0], scale[:, 0:tiles], ALU.mult).then_inc(step, 1)
    dve.wait_ge(step, tiles + 2)
    nc.vector.tensor_tensor(offset[:, 0:tiles], shift[:, 0:tiles], var_eps[:, 0:tiles], ALU.subtract).then_inc(step, 1)


def gnn_up(nc, g, a):
    MT = 2 * KT
    with ExitStack() as ctx:
        def sb(name, shape, dt=F32):
            return ctx.enter_context(nc.sbuf_tensor("up_" + name, shape, dt))

        def sems(*names):
            return [ctx.enter_context(nc.semaphore("up_" + n)) for n in names]

        h_in = sb("h_in", [RT, 2, NT, D])
        ht_hi = sb("ht_hi", [P, 2, KT, CH], F16)
        ht_lo = sb("ht_lo", [P, 2, KT, CH], F16)
        h1 = sb("h1", [P, 2, MT, CH])
        stats = sb("stats", [P, MT, NCH, 6])
        mv = sb("mv", [P, MT, 2])
        var_eps = sb("var_eps", [P, MT])
        rstd = sb("rstd", [P, MT])
        turn_ps = ctx.enter_context(nc.psum_tensor("up_turn_ps", [P, KT, 512], F32))
        mm_ps = ctx.enter_context(nc.psum_tensor("up_mm_ps", [P, 4, 512], F32))
        h_in0, h_in1, st0, st1 = sems("h_loaded0", "h_loaded1", "h1_stored0", "h1_stored1")
        h_loaded, h1_stored = (h_in0, h_in1), (st0, st1)
        turned, turn_hi, turn_lo, mm_done, h1_done, stats_done, var_done, rstd_done, bn_step, sp_tick, dve_tick = sems(
            "turned", "turn_hi", "turn_lo", "mm_done", "h1_done", "stats_done", "var_done", "rstd_done",
            "bn_step", "sp_tick", "dve_tick")

        with nc.Block() as block:
            @block.sync
            def _(sp):
                for s in range(2):
                    dma_rows_in(sp, h_in[:, s], g.h_rows, s, h_loaded[s])
                    sp.sem_inc(h1_stored[s], 16)

                def step(c, follow):
                    s = c.slot
                    if follow == 2:
                        wait(sp, sp_tick, turned, c.count(KT, KT))
                        dma_rows_in(sp, h_in[:, s], g.h_rows, c.at + 2, h_loaded[s])
                    wait(sp, sp_tick, h1_done, c.count(MT, 2 * MT))
                    sp.dma_start(g.h1_t[bass.ds(c.at, 1), :, :].rearrange("a p n -> (a p) n"),
                                 h1[:, s].rearrange("p m n -> p (m n)")).then_inc(h1_stored[s], 16)

                chunk_loop(sp, step)
                for s in range(2):
                    sp.wait_ge(h1_stored[s], 16 + 16 * NCH // 2)

            @block.scalar
            def _(act):
                def turn_high(c, k):
                    act.wait_ge(turned, c.count(KT, k + 1))
                    nc.scalar.copy(ht_hi[:, c.slot, k, :], turn_ps[:, k, 0:CH]).then_inc(turn_hi, 1)

                act.sem_inc(h1_done, MT)
                for k in range(KT):
                    turn_high(Chunk(0, 0), k)

                def step(c, follow):
                    s = c.slot
                    act.wait_ge(h1_stored[s], c.uses(16))
                    need(act, stats_done, c.count(MT, 0))
                    for m in range(MT):
                        act.wait_ge(mm_done, c.count(MT, m + 1))
                        nc.scalar.activation(h1[:, s, m, :], mm_ps[:, m % 4, 0:CH], ACT.Identity, bias=g.gb1[:, m:m + 1],
                                             scale=1 / WS).then_inc(h1_done, 1)
                        if follow and 1 <= m < 1 + KT:
                            turn_high(c.next(), m - 1)

                chunk_loop(act, step)

            @block.vector
            def _(dve):
                def turn_low(c, k):
                    dve.wait_ge(turn_hi, c.count(KT, k + 1))
                    nc.vector.tensor_tensor(ht_lo[:, c.slot, k, :], turn_ps[:, k, 0:CH], ht_hi[:, c.slot, k, :],
                                            ALU.subtract).then_inc(turn_lo, 1)

                for k in range(KT):
                    turn_low(Chunk(0, 0), k)

                def step(c, follow):
                    s = c.slot
                    for m in range(MT):
                        dve.wait_ge(h1_done, c.count(MT, MT + m + 1))
                        nc.vector.bn_stats(stats[:, m, bass.ds(c.at, 1), :].rearrange("p a s -> p (a s)"),
                                           h1[:, s, m, :]).then_inc(stats_done, 1)
                        if follow and 1 <= m < 1 + KT:
                            turn_low(c.next(), m - 1)

                chunk_loop(dve, step)
                dve.wait_ge(stats_done, MT * NCH)
                batch_norm(nc, dve, var_done, rstd_done, bn_step, stats, mv, var_eps, rstd, g.g1, g.beta1,
                           g.scale1, g.offset1, MT)

            @block.gpsimd
            def _(pool):
                pool.wait_ge(var_done, 1)
                nc.gpsimd.tensor_tensor(rstd[:], var_eps[:], g.minus_half[:, 0:MT], ALU.pow).then_inc(rstd_done, 1)

            @block.tensor
            def _(pe):
                def transposes(c, k):
                    for j in range(NT):
                        t = nc.tensor.transpose(turn_ps[:, k, j * RT:(j + 1) * RT], h_in[:, c.slot, j, k * P:(k + 1) * P],
                                                g.ident[0:RT, 0:RT])
                    t.then_inc(turned, 1)

                pe.wait_ge(h_loaded[0], 32)
                for k in range(KT):
                    transposes(Chunk(0, 0), k)

                def step(c, follow):
                    s = c.slot
                    pe.wait_ge(turn_lo, c.count(KT, KT))
                    for m in range(MT):
                        pe.wait_ge(h1_done, c.count(MT, m + 5))
                        w = slice(m * P, (m + 1) * P)
                        for k in range(KT):
                            last = split3(nc, mm_ps[:, m % 4, 0:CH], g.w1_hi[:, k, w], g.w1_lo[:, k, w],
                                          ht_hi[:, s, k, :], ht_lo[:, s, k, :], k == 0, k == KT - 1)
                        last.then_inc(mm_done, 1)
                        if follow and 1 <= m < 1 + KT:
                            if m == 1:
                                pe.wait_ge(h_loaded[c.next().slot], c.next().uses(32))
                            transposes(c.next(), m - 1)

                chunk_loop(pe, step)


def gnn_down(nc, g, a):
    K8 = 2 * KT
    AHEAD = 3
    with ExitStack() as ctx:
        def sb(name, shape, dt=F32):
            return ctx.enter_context(nc.sbuf_tensor("dn_" + name, shape, dt))

        def sems(*names):
            return [ctx.enter_context(nc.semaphore("dn_" + n)) for n in names]

        h1_in = sb("h1_in", [P, 2, K8, CH])
        act_f = sb("act_f", [P, 2, CH])
        act_hi = sb("act_hi", [P, 4, CH], F16)
        act_lo = sb("act_lo", [P, 4, CH], F16)
        h2 = sb("h2", [P, 2, KT, CH])
        stats = sb("stats", [P, KT, NCH, 6])
        mv = sb("mv", [P, KT, 2])
        var_eps = sb("var_eps", [P, KT])
        rstd = sb("rstd", [P, KT])
        mm_ps = ctx.enter_context(nc.psum_tensor("dn_mm_ps", [P, 2, KT, 512], F32))
        l0, l1, st0, st1 = sems("loaded0", "loaded1", "stored0", "stored1")
        loaded, stored = (l0, l1), (st0, st1)
        silu_done, hi_done, lo_done, k_done, mm_done, h2_done, stats_done, var_done, rstd_done, bn_step, sp_tick = sems(
            "silu_done", "hi_done", "lo_done", "k_done", "mm_done", "h2_done", "stats_done", "var_done", "rstd_done",
            "bn_step", "sp_tick")

        with nc.Block() as block:
            @block.sync
            def _(sp):
                def load(at, s):
                    sp.dma_start(h1_in[:, s].rearrange("p k n -> p (k n)"),
                                 g.h1_t[bass.ds(at, 1), :, :].rearrange("a p n -> (a p) n")).then_inc(loaded[s], 16)

                for s in range(2):
                    load(s, s)
                    sp.sem_inc(stored[s], 16)

                def step(c, follow):
                    s = c.slot
                    if follow == 2:
                        wait(sp, sp_tick, silu_done, c.count(K8, K8))
                        load(c.at + 2, s)
                    wait(sp, sp_tick, h2_done, c.count(KT, KT))
                    sp.dma_start(g.h2_t[bass.ds(c.at, 1), :, :].rearrange("a p n -> (a p) n"),
                                 h2[:, s].rearrange("p m n -> p (m n)")).then_inc(stored[s], 16)

                chunk_loop(sp, step)
                for s in range(2):
                    sp.wait_ge(stored[s], 16 + 16 * NCH // 2)

            @block.scalar
            def _(act):
                def activate(c, k):
                    act.wait_ge(lo_done, c.count(K8, k + 1))
                    nc.scalar.activation(act_f[:, k % 2, :], h1_in[:, c.slot, k, :], ACT.Silu, bias=g.offset1[:, k:k + 1],
                                         scale=g.scale1[:, k:k + 1]).then_inc(silu_done, 1)
                    act.wait_ge(silu_done, c.count(K8, k + 1))
                    if k == 3:
                        need(act, mm_done, c.count(KT, 0))
                    else:
                        need(act, k_done, c.count(K8 - 1, k if k < 3 else k - 1))
                    nc.scalar.copy(act_hi[:, k % 4, :], act_f[:, k % 2, :]).then_inc(hi_done, 1)

                def read_out(c, m):
                    act.wait_ge(mm_done, c.count(KT, m + 1))
                    nc.scalar.activation(h2[:, c.slot, m, :], mm_ps[:, c.slot, m, 0:CH], ACT.Identity,
                                         bias=g.gb2[:, m:m + 1], scale=1 / WS).then_inc(h2_done, 1)

                act.wait_ge(loaded[0], 16)
                for k in range(AHEAD):
                    activate(Chunk(0, 0), k)

                def step(c, follow):
                    for k in range(AHEAD, K8):
                        activate(c, k)
                    if follow:
                        act.wait_ge(loaded[c.next().slot], c.next().uses(16))
                        for k in range(AHEAD):
                            activate(c.next(), k)
                    act.wait_ge(stored[c.slot], c.uses(16))
                    need(act, stats_done, c.count(KT, 0))
                    for m in range(KT):
                        read_out(c, m)

                chunk_loop(act, step)

            @block.vector
            def _(dve):
                dve.sem_inc(lo_done, 2)

                def low(c, k):
                    dve.wait_ge(hi_done, c.count(K8, k + 1))
                    nc.vector.tensor_tensor(act_lo[:, k % 4, :], act_f[:, k % 2, :], act_hi[:, k % 4, :],
                                            ALU.subtract).then_inc(lo_done, 1)

                for k in range(AHEAD):
                    low(Chunk(0, 0), k)

                def step(c, follow):
                    for k in range(AHEAD, K8):
                        low(c, k)
                    if follow:
                        for k in range(AHEAD):
                            low(c.next(), k)
                    for m in range(KT):
                        dve.wait_ge(h2_done, c.count(KT, m + 1))
                        nc.vector.bn_stats(stats[:, m, bass.ds(c.at, 1), :].rearrange("p a s -> p (a s)"),
                                           h2[:, c.slot, m, :]).then_inc(stats_done, 1)

                chunk_loop(dve, step)
                dve.wait_ge(stats_done, KT * NCH)
                batch_norm(nc, dve, var_done, rstd_done, bn_step, stats, mv, var_eps, rstd, g.g2, g.beta2,
                           g.scale2, g.offset2, KT)

            @block.gpsimd
            def _(pool):
                pool.wait_ge(var_done, 1)
                nc.gpsimd.tensor_tensor(rstd[:], var_eps[:], g.minus_half[:, 0:KT], ALU.pow).then_inc(rstd_done, 1)

            @block.tensor
            def _(pe):
                pe.sem_inc(k_done, 2)

                def step(c, follow):
                    for k in range(K8):
                        pe.wait_ge(lo_done, c.count(K8, 2 + k + 1))
                        if k == 0:
                            need(pe, h2_done, c.count(KT, -KT))
                        for m in range(KT):
                            w = slice(m * P, (m + 1) * P)
                            last = split3(nc, mm_ps[:, c.slot, m, 0:CH], g.w2_hi[:, k, w], g.w2_lo[:, k, w],
                                          act_hi[:, k % 4, :], act_lo[:, k % 4, :], k == 0, k == K8 - 1)
                            if k == K8 - 1:
                                last.then_inc(mm_done, 1)
                            elif m == KT - 1:
                                last.then_inc(k_done, 1)

                chunk_loop(pe, step)


def feed(nc, g, a, out):
    with ExitStack() as ctx:
        def sb(name, shape, dt=F32):
            return ctx.enter_context(nc.sbuf_tensor("ff_" + name, shape, dt))

        def sems(*names):
            return [ctx.enter_context(nc.semaphore("ff_" + n)) for n in names]

        h2_in = sb("h2_in", [P, 2, KT, CH])
        r_in = sb("r_in", [RT, 2, NT, D])
        z = sb("z", [P, KT, CH])
        y = sb("y", [RT, 2, NT, D])
        y_b = sb("y_b", [RT, 2, NT, D])
        n2 = sb("n2", [RT, 2, NT, D])
        nt_hi = sb("nt_hi", [P, NT, KT * RT], F16)
        nt_lo = sb("nt_lo", [P, NT, KT * RT], F16)
        gelu = sb("gelu", [RT, NT, FH])
        share_h = sb("share_h", [RT, NT, FH])
        gt_hi = sb("gt_hi", [P, 2, 4 * RT], F16)
        gt_lo = sb("gt_lo", [P, 2, 4 * RT], F16)
        u = sb("u", [RT, NT, D])
        ug = sb("ug", [RT, NT, D])
        o = sb("o", [RT, 2, NT, D])
        y_stats = sb("y_stats", [RT, NT, 6])
        y_mv = sb("y_mv", [RT, NT, 2])
        u_stats = sb("u_stats", [RT, NT, 6])
        u_mv = sb("u_mv", [RT, NT, 2])
        small = sb("small", [RT, 12, NT])
        inv2 = sb("inv2", [RT, 2, NT])
        var2 = sb("var2", [RT, 2, NT])
        u_var = sb("u_var", [RT, NT])
        u_rstd = sb("u_rstd", [RT, NT])
        logits = sb("logits", [RT, NT, NE])
        top = sb("top", [RT, NT, 8])
        top_i = sb("top_i", [RT, NT, 8], U32)
        top_f = sb("top_f", [RT, NT, 2])
        gap = sb("gap", [RT, NT])
        e_gap = sb("e_gap", [RT, NT])
        e_one = sb("e_one", [RT, NT])
        share = sb("share", [RT, 2, NT])
        is_top = sb("is_top", [RT, 2, NT, NE])
        by_top = sb("by_top", [RT, 2, NT, NE])
        shares = sb("shares", [RT, NT, NE])
        share_hi = sb("share_hi", [RT, NT, NE], F16)
        share_parts = sb("share_parts", [RT, NT, P])
        share_t = sb("share_t", [P, NT, RT], F16)
        z_ps = ctx.enter_context(nc.psum_tensor("ff_z_ps", [P, 2, 512], F32))
        turn_ps = ctx.enter_context(nc.psum_tensor("ff_turn_ps", [P, 2, 512], F32))
        f_ps = ctx.enter_context(nc.psum_tensor("ff_f_ps", [P, 2, 512], F32))
        u_ps = ctx.enter_context(nc.psum_tensor("ff_u_ps", [P, 2, 512], F32))

        h0_, h1_, r0_, r1_, o0_, o1_ = sems("h2_loaded0", "h2_loaded1", "r_loaded0", "r_loaded1", "stored0", "stored1")
        h2_loaded, r_loaded, stored = (h0_, h1_), (r0_, r1_), (o0_, o1_)
        z_done, z_turned, y_done, y_stats_done, y_mv_done, s1_step, n2_done, n2_turned, nt_hi_done, nt_lo_done = sems(
            "z_done", "z_turned", "y_done", "y_stats_done", "y_mv_done", "s1_step", "n2_done", "n2_turned", "nt_hi_done", "nt_lo_done")
        f_done, gelu_done, logits_done, s2_step, gap_done, e_gap_done, share_step, share_h_done, inv2_done, y_b_done = sems(
            "f_done", "gelu_done", "logits_done", "s2_step", "gap_done", "e_gap_done", "share_step", "share_h_done", "inv2_done", "y_b_done")
        g_turned, s_turned, gt_hi_done, gt_lo_done, share_t_done, u_mm, u_done, u_stats_done, u_mv_done, u_step, ug_done, o_done = sems(
            "g_turned", "s_turned", "gt_hi_done", "gt_lo_done", "share_t_done", "u_mm", "u_done", "u_stats_done", "u_mv_done",
            "u_step", "ug_done", "o_done")
        sp_tick, pool_tick, dve_tick, zeroed, inv2_step, parts_done = sems(
            "sp_tick", "pool_tick", "dve_tick", "zeroed", "inv2_step", "parts_done")
        S1 = 9
        S2 = 10

        def stages(eng, step):
            chunk = [None] * 3 + [Chunk(n // 2, n % 2) for n in range(NCH)] + [None] * 3
            for n in range(4):
                step(chunk[n + 3], chunk[n + 2], chunk[n + 1], chunk[n], True)
            with eng.Fori(2, NCH // 2 - 1) as i:
                for s in range(2):
                    A = Chunk(i, s)
                    B = A.prev()
                    C = B.prev()
                    step(A, B, C, C.prev(), True)
            for n in range(NCH - 2, NCH + 3):
                step(chunk[n + 3], chunk[n + 2], chunk[n + 1], chunk[n], n < NCH - 1)

        def ticked(eng, tick):
            def wait_for(sem, value):
                if isinstance(value, int):
                    need(eng, sem, value)
                else:
                    wait(eng, tick, sem, value)
            return wait_for

        with nc.Block() as block:
            @block.sync
            def _(sp):
                wait_for = ticked(sp, sp_tick)

                def load_h2(c):
                    sp.dma_start(h2_in[:, c.slot].rearrange("p k n -> p (k n)"),
                                 g.h2_t[bass.ds(c.at, 1), :, :].rearrange("a p n -> (a p) n")).then_inc(h2_loaded[c.slot], 16)

                def load_r(c):
                    dma_rows_in(sp, r_in[:, c.slot], g.r_rows, c.at, r_loaded[c.slot])

                sp.sem_inc(stored[0], 32)
                sp.sem_inc(stored[1], 32)
                load_h2(Chunk(0, 0))
                load_r(Chunk(0, 0))

                def step(A, B, C, D, more):
                    if more:
                        n = A.next()
                        wait_for(z_done, A.count(KT, 0))
                        load_h2(n)
                        wait_for(y_done, A.count(NT, 0))
                        load_r(n)
                    if D is not None:
                        wait_for(o_done, D.count(NT, NT))
                        dma_rows_out(sp, out, D.at, o[:, D.slot], stored[D.slot])

                stages(sp, step)
                for s in range(2):
                    sp.wait_ge(stored[s], 32 + 32 * NCH // 2)

            @block.gpsimd
            def _(pool):
                wait_for = ticked(pool, pool_tick)

                def step(A, B, C, D, more):
                    if B is not None:
                        wait_for(u_done, B.count(NT, -NT))
                        nc.gpsimd.tensor_tensor(small[:, 8, :], var2[:, B.slot, :], g.half[0:RT, 0:NT], ALU.pow).then_inc(inv2_step, 1)
                        wait_for(inv2_step, B.count(1, 1))
                        nc.gpsimd.tensor_scalar(inv2[:, B.slot, :], small[:, 8, :], WS, None, ALU.mult).then_inc(inv2_done, 1)
                        wait_for(y_done, B.count(NT, NT))
                        for j in range(NT):
                            wait_for(o_done, B.count(NT, j + 1 - 2 * NT))
                            nc.gpsimd.tensor_tensor(y_b[:, B.slot, j, :], y[:, B.slot, j, :], g.out_b[:], ALU.add).then_inc(y_b_done, 1)
                    if A is not None:
                        var_eps, r1, square, v2, r2, rr, mr, nb = (small[:, n, :] for n in range(8))
                        wait_for(n2_done, A.count(NT, 0))
                        wait_for(y_mv_done, A.count(NT, NT))
                        nc.gpsimd.tensor_scalar(var_eps, y_mv[:, :, 1], LN_EPS, None, ALU.add).then_inc(s1_step, 1)
                        wait_for(s1_step, A.count(S1, 1))
                        nc.gpsimd.tensor_tensor(r1, var_eps, g.minus_half[0:RT, 0:NT], ALU.pow).then_inc(s1_step, 1)
                        wait_for(s1_step, A.count(S1, 2))
                        nc.gpsimd.tensor_tensor(square, r1, r1, ALU.mult).then_inc(s1_step, 1)
                        wait_for(s1_step, A.count(S1, 3))
                        nc.gpsimd.tensor_tensor(v2, square, y_mv[:, :, 1], ALU.mult).then_inc(s1_step, 1)
                        wait_for(s1_step, A.count(S1, 4))
                        nc.gpsimd.tensor_scalar(var2[:, A.slot, :], v2, LN_EPS, None, ALU.add).then_inc(s1_step, 1)
                        wait_for(s1_step, A.count(S1, 5))
                        nc.gpsimd.tensor_tensor(r2, var2[:, A.slot, :], g.minus_half[0:RT, 0:NT], ALU.pow).then_inc(s1_step, 1)
                        wait_for(s1_step, A.count(S1, 6))
                        nc.gpsimd.tensor_tensor(rr, r1, r2, ALU.mult).then_inc(s1_step, 1)
                        wait_for(s1_step, A.count(S1, 7))
                        nc.gpsimd.tensor_tensor(mr, y_mv[:, :, 0], rr, ALU.mult).then_inc(s1_step, 1)
                        wait_for(s1_step, A.count(S1, 8))
                        nc.gpsimd.tensor_scalar(nb, mr, -1.0, None, ALU.mult).then_inc(s1_step, 1)
                    if C is not None:
                        wait_for(o_done, C.count(NT, 0))
                        wait_for(u_mv_done, C.count(NT, NT))
                        nc.gpsimd.tensor_scalar(u_var[:], u_mv[:, :, 1], LN_EPS * WS * WS, None, ALU.add).then_inc(u_step, 1)
                        wait_for(u_step, C.count(2, 1))
                        nc.gpsimd.tensor_tensor(u_rstd[:], u_var[:], g.minus_half[0:RT, 0:NT], ALU.pow).then_inc(u_step, 1)

                stages(pool, step)

            @block.scalar
            def _(act):
                def silu(c):
                    act.wait_ge(h2_loaded[c.slot], c.uses(16))
                    need(act, z_turned, c.count(NT, 0))
                    for k in range(KT):
                        nc.scalar.activation(z[:, k, :], h2_in[:, c.slot, k, :], ACT.Silu, bias=g.offset2[:, k:k + 1],
                                             scale=g.scale2[:, k:k + 1]).then_inc(z_done, 1)

                silu(Chunk(0, 0))

                def step(A, B, C, D, more):
                    def gelu_of(j):
                        act.wait_ge(f_done, B.count(NT, j + 1))
                        nc.scalar.activation(gelu[:, j, :], f_ps[0:RT, j % 2, 0:FH], ACT.Gelu_apprx_tanh,
                                             scale=1 / WS).then_inc(gelu_done, 1)

                    def turned_high(pair):
                        act.wait_ge(g_turned, C.count(2, pair + 1))
                        nc.scalar.copy(gt_hi[:, pair, :], turn_ps[:, pair, 0:4 * RT]).then_inc(gt_hi_done, 1)

                    if B is not None:
                        need(act, f_done, B.count(NT, 0))
                        for j in range(NT):
                            act.wait_ge(n2_turned, B.count(NT, j + 1))
                            nc.scalar.copy(nt_hi[:, j, :], turn_ps[:, j % 2, 0:KT * RT]).then_inc(nt_hi_done, 1)
                        need(act, share_h_done, B.count(NT, 0))
                        gelu_of(0)
                        gelu_of(1)
                    if C is not None:
                        need(act, u_mm, C.count(NT, 0))
                        turned_high(0)
                    if B is not None:
                        gelu_of(2)
                    if C is not None:
                        turned_high(1)
                        act.wait_ge(s_turned, C.count(1, 1))
                        nc.scalar.copy(share_t[:].rearrange("p j n -> p (j n)"), turn_ps[:, 0, 0:NT * RT]).then_inc(share_t_done, 1)
                    if B is not None:
                        gelu_of(3)
                    if more:
                        silu(A.next())
                    if B is not None:
                        act.wait_ge(gap_done, B.count(1, 1))
                        nc.scalar.activation(e_gap[:], gap[:], ACT.Exp).then_inc(e_gap_done, 1)
                    if A is not None:
                        act.wait_ge(s1_step, A.count(S1, S1))
                        for j in range(NT):
                            need(act, u_done, A.count(NT, j + 1 - 2 * NT))
                            nc.scalar.activation(n2[:, A.slot, j, :], y[:, A.slot, j, :], ACT.Identity,
                                                 bias=small[:, 7, j:j + 1], scale=small[:, 5, j:j + 1]).then_inc(n2_done, 1)

                stages(act, step)

            @block.vector
            def _(dve):
                nc.vector.memset(share_parts[:], 0.0).then_inc(zeroed, 1)
                dve.wait_ge(zeroed, 1)
                wait_for = ticked(dve, dve_tick)

                def head_shares(t, k):
                    return t.unsqueeze(2).to_broadcast([RT, NT, k])

                def step(A, B, C, D, more):
                    S = 9

                    def y_sum(j):
                        need(dve, y_b_done, A.count(NT, j + 1 - 2 * NT))
                        dve.wait_ge(z_turned, A.count(NT, j + 1))
                        nc.vector.tensor_tensor(y[:, A.slot, j, :], z_ps[0:RT, j % 2, :], r_in[:, A.slot, j, :],
                                                ALU.add).then_inc(y_done, 1)

                    def y_stat(j):
                        dve.wait_ge(y_done, A.count(NT, j + 1))
                        nc.vector.bn_stats(y_stats[:, j, :], y[:, A.slot, j, :]).then_inc(y_stats_done, 1)

                    def n2_low(j):
                        dve.wait_ge(nt_hi_done, B.count(NT, j + 1))
                        nc.vector.tensor_tensor(nt_lo[:, j, :], turn_ps[:, j % 2, 0:KT * RT], nt_hi[:, j, :],
                                                ALU.subtract).then_inc(nt_lo_done, 1)

                    def g_low(pair):
                        dve.wait_ge(gt_hi_done, C.count(2, pair + 1))
                        nc.vector.tensor_tensor(gt_lo[:, pair, :], turn_ps[:, pair, 0:4 * RT], gt_hi[:, pair, :],
                                                ALU.subtract).then_inc(gt_lo_done, 1)

                    def logits_of(j):
                        dve.wait_ge(gelu_done, B.count(NT, j + 1))
                        nc.vector.tensor_scalar(logits[:, j, :], f_ps[0:RT, j % 2, FH:F1], 1 / WS, None,
                                                ALU.mult).then_inc(logits_done, 1)

                    def u_sum(j):
                        dve.wait_ge(u_mm, C.count(NT, j + 1))
                        nc.vector.scalar_tensor_tensor(u[:, j, :], n2[:, C.slot, j, :], inv2[:, C.slot, j:j + 1], u_ps[0:RT, j % 2, :],
                                                       ALU.mult, ALU.add).then_inc(u_done, 1)

                    def u_stat(j):
                        dve.wait_ge(u_done, C.count(NT, j + 1))
                        nc.vector.bn_stats(u_stats[:, j, :], u[:, j, :]).then_inc(u_stats_done, 1)

                    def u_gain(j):
                        nc.vector.scalar_tensor_tensor(ug[:, j, :], u[:, j, :], u_mv[:, j, 0:1], g.out_g[:],
                                                       ALU.subtract, ALU.mult).then_inc(ug_done, 1)

                    def finish(j):
                        dve.wait_ge(ug_done, D.count(NT, j + 1))
                        nc.vector.scalar_tensor_tensor(o[:, D.slot, j, :], ug[:, j, :], u_rstd[:, j:j + 1], y_b[:, D.slot, j, :],
                                                       ALU.mult, ALU.add).then_inc(o_done, 1)

                    if A is not None:
                        dve.wait_ge(r_loaded[A.slot], A.uses(32))
                        y_sum(0)
                        y_sum(1)
                    if D is not None:
                        dve.wait_ge(u_mv_done, D.count(NT, NT))
                        u_gain(0)
                    if A is not None:
                        y_sum(2)
                        y_sum(3)
                    if D is not None:
                        u_gain(1)
                    if B is not None:
                        n2_low(0)
                        n2_low(1)
                    if D is not None:
                        u_gain(2)
                    if B is not None:
                        n2_low(2)
                    if D is not None:
                        u_gain(3)
                    if B is not None:
                        n2_low(3)
                        logits_of(0)
                    if A is not None:
                        y_stat(0)
                        y_stat(1)
                    if B is not None:
                        logits_of(1)
                    if C is not None:
                        g_low(0)
                    if A is not None:
                        y_stat(2)
                        y_stat(3)
                        wait_for(s1_step, A.count(S1, 0))
                        wait_for(y_stats_done, A.count(NT, NT))
                        for j in range(NT):
                            nc.vector.bn_aggr(y_mv[:, j, :], y_stats[:, j, :]).then_inc(y_mv_done, 1)
                    if D is not None:
                        wait_for(u_step, D.count(2, 2))
                        wait_for(y_b_done, D.count(NT, NT))
                        wait_for(stored[D.slot], D.uses(32))
                        finish(0)
                    if B is not None:
                        logits_of(2)
                    if C is not None:
                        g_low(1)
                    if D is not None:
                        finish(1)
                        finish(2)
                        finish(3)
                    if B is not None:
                        logits_of(3)
                        wait_for(logits_done, B.count(NT, NT))
                        for j in range(NT):
                            nc.vector.max(top[:, j, :], logits[:, j, :]).then_inc(s2_step, 1)
                        wait_for(s2_step, B.count(S2, NT))
                        nc.vector.tensor_tensor(gap[:], top[:, :, 1], top[:, :, 0], ALU.subtract).then_inc(gap_done, 1)
                        for j in range(NT):
                            nc.vector.max_index(top_i[:, j, :], top[:, j, :], logits[:, j, :]).then_inc(s2_step, 1)
                    if C is not None:
                        wait_for(inv2_done, C.count(1, 1))
                        u_sum(0)
                    if B is not None:
                        wait_for(s2_step, B.count(S2, 2 * NT))
                        nc.vector.tensor_copy(top_f[:], top_i[:, :, 0:2]).then_inc(s2_step, 2)
                    if C is not None:
                        u_stat(0)
                        u_sum(1)
                    if B is not None:
                        for t in range(2):
                            wait_for(s2_step, B.count(S2, S2))
                            nc.vector.tensor_tensor(is_top[:, t], g.expert[:], head_shares(top_f[:, :, t], NE),
                                                    ALU.is_equal).then_inc(share_step, 1)
                        wait_for(e_gap_done, B.count(1, 1))
                        nc.vector.tensor_scalar(e_one[:], e_gap[:], 1.0, None, ALU.add).then_inc(share_step, 1)
                    if C is not None:
                        u_stat(1)
                    if B is not None:
                        wait_for(share_step, B.count(S, 3))
                        nc.vector.reciprocal(share[:, 0, :], e_one[:]).then_inc(share_step, 1)
                    if C is not None:
                        u_sum(2)
                    if B is not None:
                        wait_for(share_step, B.count(S, 4))
                        nc.vector.tensor_tensor(share[:, 1, :], e_gap[:], share[:, 0, :], ALU.mult).then_inc(share_step, 1)
                    if C is not None:
                        u_stat(2)
                    if B is not None:
                        wait_for(share_step, B.count(S, 5))
                        for t in range(2):
                            nc.vector.tensor_tensor(by_top[:, t], is_top[:, t], head_shares(share[:, t, :], NE),
                                                    ALU.mult).then_inc(share_step, 1)
                    if C is not None:
                        u_sum(3)
                    if B is not None:
                        wait_for(share_step, B.count(S, 7))
                        nc.vector.tensor_tensor(shares[:], by_top[:, 0], by_top[:, 1], ALU.add).then_inc(share_step, 1)
                    if C is not None:
                        u_stat(3)
                    if B is not None:
                        wait_for(share_step, B.count(S, 8))
                        nc.vector.tensor_copy(share_hi[:], shares[:]).then_inc(share_step, 1)
                        wait_for(g_turned, B.count(2, 0))
                        for j in range(NT):
                            dve.wait_ge(gelu_done, B.count(NT, j + 1))
                            nc.vector.tensor_tensor(share_h[:, j, :].rearrange("p (e h) -> p e h", e=NE),
                                                    gelu[:, j, :].rearrange("p (e h) -> p e h", e=NE),
                                                    shares[:, j, :].unsqueeze(2).to_broadcast([RT, NE, EH]),
                                                    ALU.mult).then_inc(share_h_done, 1)
                    if C is not None:
                        wait_for(u_step, C.count(2, 0))
                        wait_for(u_stats_done, C.count(NT, NT))
                        for j in range(NT):
                            nc.vector.bn_aggr(u_mv[:, j, :], u_stats[:, j, :]).then_inc(u_mv_done, 1)
                    if B is not None:
                        wait_for(s_turned, B.count(1, 0))
                        wait_for(share_step, B.count(S, 9))
                        nc.vector.tensor_copy(share_parts[:, :, 0:NE], share_hi[:]).then_inc(parts_done, 1)
                        nc.vector.tensor_tensor(share_parts[:, :, NE:2 * NE], shares[:], share_hi[:],
                                                ALU.subtract).then_inc(parts_done, 1)
                        nc.vector.tensor_copy(share_parts[:, :, 2 * NE:3 * NE], share_hi[:]).then_inc(parts_done, 1)

                stages(dve, step)

            @block.tensor
            def _(pe):
                def step(A, B, C, D, more):
                    def turn_n2(j):
                        if j == 0:
                            need(pe, share_t_done, B.count(1, -1))
                        elif j == 1:
                            need(pe, gt_lo_done, B.count(2, -2))
                        else:
                            pe.wait_ge(nt_lo_done, B.count(NT, j - 1))
                        pe.wait_ge(n2_done, B.count(NT, j + 1))
                        for k in range(KT):
                            t = nc.tensor.transpose(turn_ps[:, j % 2, k * RT:(k + 1) * RT], n2[:, B.slot, j, k * P:(k + 1) * P],
                                                    g.ident[0:RT, 0:RT])
                        t.then_inc(n2_turned, 1)

                    def turn_hidden(pair):
                        if B is not None:
                            pe.wait_ge(nt_lo_done, B.count(NT, pair + 3))
                        elif pair == 0:
                            need(pe, share_t_done, C.count(1, 0))
                        else:
                            need(pe, gt_lo_done, C.count(2, 0))
                        for j in (2 * pair, 2 * pair + 1):
                            pe.wait_ge(share_h_done, C.count(NT, j + 1))
                            for b in range(2):
                                at = (j % 2 * 2 + b) * RT
                                t = nc.tensor.transpose(turn_ps[:, pair, at:at + RT], share_h[:, j, b * P:(b + 1) * P],
                                                        g.ident[0:RT, 0:RT])
                        t.then_inc(g_turned, 1)

                    def turn_shares():
                        pe.wait_ge(gt_lo_done, C.count(2, 1))
                        pe.wait_ge(parts_done, C.count(3, 3))
                        for j in range(NT):
                            t = nc.tensor.transpose(turn_ps[:, 0, j * RT:(j + 1) * RT], share_parts[:, j, :], g.ident[0:RT, 0:RT])
                        t.then_inc(s_turned, 1)

                    def hidden(j):
                        pe.wait_ge(nt_lo_done, B.count(NT, j + 1))
                        need(pe, logits_done, B.count(NT, j - 1))
                        for k in range(KT):
                            ks = slice(k * RT, (k + 1) * RT)
                            split3(nc, f_ps[0:RT, j % 2, 0:F1], nt_hi[:, j, ks], nt_lo[:, j, ks],
                                   g.f1_hi[:, k, :], g.f1_lo[:, k, :], k == 0, False)
                        nc.tensor.matmul(f_ps[0:RT, j % 2, 0:F1], g.ones_w[:], g.f1_bias[:], start=False, stop=True,
                                         skip_group_check=True).then_inc(f_done, 1)

                    def output(j):
                        pe.wait_ge(gt_lo_done, C.count(2, j // 2 + 1))
                        need(pe, u_done, C.count(NT, j - 1))
                        for b in range(2):
                            at = (j % 2 * 2 + b) * RT
                            split3(nc, u_ps[0:RT, j % 2, :], gt_hi[:, j // 2, at:at + RT], gt_lo[:, j // 2, at:at + RT],
                                   g.f2_hi[:, b, :], g.f2_lo[:, b, :], b == 0, False)
                        nc.tensor.matmul(u_ps[0:RT, j % 2, :], share_t[:, j, :], g.eb2[:], start=False, stop=True,
                                         skip_group_check=True).then_inc(u_mm, 1)

                    if A is not None:
                        pe.wait_ge(z_done, A.count(KT, KT))
                        for j in range(NT):
                            need(pe, y_done, A.count(NT, j - 1))
                            for k in range(KT):
                                t = nc.tensor.transpose(z_ps[0:RT, j % 2, k * P:(k + 1) * P], z[:, k, j * RT:(j + 1) * RT], g.ident[:])
                            t.then_inc(z_turned, 1)
                    if B is not None:
                        turn_n2(0)
                        turn_n2(1)
                        turn_n2(2)
                        hidden(0)
                        turn_n2(3)
                        hidden(1)
                    if C is not None:
                        turn_hidden(0)
                    if B is not None:
                        hidden(2)
                    if C is not None:
                        turn_hidden(1)
                        turn_shares()
                    if B is not None:
                        hidden(3)
                    if C is not None:
                        pe.wait_ge(share_t_done, C.count(1, 1))
                        for j in range(NT):
                            output(j)

                stages(pe, step)


def build(nc, a, out):
    with ExitStack() as ctx:
        g = Parts()

        def keep(name, shape, dt=F32):
            return ctx.enter_context(nc.sbuf_tensor(name, shape, dt))

        g.h_rows = nc.dram_tensor("h_rows", [N + RT, D], F32, kind="Internal").ap()
        g.q_t = nc.dram_tensor("q_t", [NCH, P, KT * CH], F32, kind="Internal").ap()
        g.r_rows = nc.dram_tensor("r_rows", [N, D], F32, kind="Internal").ap()
        g.h1_t = nc.dram_tensor("h1_t", [NCH, P, 2 * KT * CH], F32, kind="Internal").ap()
        g.h2_t = nc.dram_tensor("h2_t", [NCH, P, KT * CH], F32, kind="Internal").ap()
        g.ident = keep("ident", [P, P])
        g.ident_h = keep("ident_h", [P, P], F16)
        g.before = keep("before", [RT, RT])
        g.head_mask = keep("head_mask", [P, P])
        g.spread = keep("spread", [P, D], F16)
        g.trash = keep("trash", [RT, 1])
        g.expert = keep("expert", [RT, NT, NE])
        g.minus_half = keep("minus_half", [P, 2 * KT])
        g.half = keep("half", [P, 2 * KT])
        g.zeros = keep("zeros", [P, D])
        g.zeros_h = keep("zeros_h", [P, D], F16)
        g.ones_col = keep("ones_col", [P, 1], F16)
        g.ones_w = keep("ones_w", [P, RT], F16)
        g.ones_q = keep("ones_q", [P, RT], F16)
        g.one_eps = keep("one_eps", [RT, 1])
        g.gb1, g.g1, g.beta1 = (keep(n, [P, 2 * KT]) for n in ("gb1", "g1", "beta1"))
        g.gb2, g.g2, g.beta2 = (keep(n, [P, KT]) for n in ("gb2", "g2", "beta2"))
        g.we = keep("we", [ED + 1, D])
        g.out_g, g.out_b = (keep(n, [RT, D]) for n in ("out_g", "out_b"))
        g.f1_hi, g.f1_lo = (keep(n, [P, KT, F1], F16) for n in ("f1_hi", "f1_lo"))
        g.f2_hi, g.f2_lo = (keep(n, [P, 2, D], F16) for n in ("f2_hi", "f2_lo"))
        g.f1_bias = keep("f1_bias", [P, F1], F16)
        g.out_bias = keep("out_bias", [P, D], F16)
        g.eb2 = keep("eb2", [P, D], F16)
        g.scale1, g.offset1 = (keep(n, [P, 2 * KT]) for n in ("scale1", "offset1"))
        g.scale2, g.offset2 = (keep(n, [P, KT]) for n in ("scale2", "offset2"))
        with ExitStack() as messages:
            g.kv = messages.enter_context(nc.sbuf_tensor("kv", [P, KT, P], F32))
            g.k_sum = messages.enter_context(nc.sbuf_tensor("k_sum", [P, KT, HEADS], F32))
            g.totals = messages.enter_context(nc.sbuf_tensor("totals", [RT, NCH, D], F32))
            g.target = messages.enter_context(nc.sbuf_tensor("target", [RT, NCH], I32))
            with ExitStack() as first:
                g.ea_t = first.enter_context(nc.sbuf_tensor("ea_t", [ED + 1, E], F32))
                g.wqkv_hi, g.wqkv_lo = (first.enter_context(nc.sbuf_tensor(n, [P, KT, 3 * D], F16))
                                        for n in ("wqkv_hi", "wqkv_lo"))
                setup(nc, g, a)
                project(nc, g, a)
            attend(nc, g, a)
        with ExitStack() as gnn:
            g.w1_hi, g.w1_lo = (gnn.enter_context(nc.sbuf_tensor(n, [P, KT, 2 * D], F16)) for n in ("w1_hi", "w1_lo"))
            g.w2_hi, g.w2_lo = (gnn.enter_context(nc.sbuf_tensor(n, [P, 2 * KT, D], F16)) for n in ("w2_hi", "w2_lo"))
            gnn_weights(nc, g, a)
            gnn_up(nc, g, a)
            gnn_down(nc, g, a)
        feed(nc, g, a, out)


def constants():
    import numpy as np

    ident = np.eye(P, dtype=np.float32)
    p = np.arange(P)
    before = (p[:RT, None] < p[None, :RT]).astype(np.float32).T.copy()
    spread = np.zeros((P, D), np.float16)
    for m in range(3):
        spread[m * HEADS:(m + 1) * HEADS] = np.kron(np.eye(HEADS), np.ones((1, HD)))
    return {
        "c_ident": ident,
        "c_ident_h": ident.astype(np.float16),
        "c_before": before,
        "c_head_mask": np.kron(np.eye(2), np.ones((HD, HD))).astype(np.float32),
        "c_spread": spread,
        "c_trash": (N + p[:RT, None]).astype(np.float32),
        "c_expert": np.tile(np.arange(NE, dtype=np.float32), (NT, 1)),
    }


def kernel(**inputs):
    import numpy as np
    import concourse.bacc as bacc
    from concourse.bass_utils import run_bass_kernel_spmd

    nc = bacc.Bacc("TRN2", target_bir_lowering=False, num_devices=1)
    arrays, a = {}, {}
    for name, value in [*inputs.items(), *constants().items()]:
        v = np.ascontiguousarray(value)
        if name == "L0_gnn_eps":
            v = v.reshape(1)
        arrays[f"in_{name}"] = v
        a[name] = nc.dram_tensor(f"in_{name}", v.shape, mybir.dt.from_np(v.dtype), kind="ExternalInput").ap()
    out = nc.dram_tensor("out", [N, D], F32, kind="ExternalOutput").ap()
    build(nc, a, out)
    r = run_bass_kernel_spmd(nc, [arrays], core_ids=[0])
    return r.results[0]["out"]
```

```python
from contextlib import ExitStack

import concourse.bass as bass
from concourse import mybir

F32 = mybir.dt.float32
F16 = mybir.dt.float16
I32 = mybir.dt.int32
U32 = mybir.dt.uint32
ALU = mybir.AluOpType
ACT = mybir.ActivationFunctionType
AX = mybir.AxisListType

N = 10000
E = 2500
D = 512
ED = 64
HEADS, HD = 8, 64
NE, EH = 8, 32
P = 128
RT = 125
NT = 4
CH = RT * NT
NCH = N // CH
KT = D // P
FH = NE * EH
F1 = FH + NE
TWICE = 32 + HEADS
CUT = 112
WS = 64.0
QS = 256.0
NS = 2.0 ** -13
LN_EPS = 1e-5
BN_EPS = 1e-5
ATT_EPS = 1e-6
QKV_ORDER = (slice(D, 2 * D), slice(2 * D, 3 * D), slice(0, D))
SMALL = 7
assert N == CH * NCH and E == RT * NCH


def split3(nc, out, lhs_hi, lhs_lo, rhs_hi, rhs_lo, first, last):
    nc.tensor.matmul(out, lhs_hi, rhs_hi, start=first, stop=False, skip_group_check=True)
    nc.tensor.matmul(out, lhs_hi, rhs_lo, start=False, stop=False, skip_group_check=True)
    return nc.tensor.matmul(out, lhs_lo, rhs_hi, start=False, stop=last, skip_group_check=True)


def wait(eng, tick, sem, value):
    eng.wait_ge(sem, value)
    eng.sem_inc(tick, 1)


class Chunk:

    def __init__(self, i, slot):
        self.i, self.slot, self.at = i, slot, i * 2 + slot

        self.first = isinstance(i, int) and i == 0 and slot == 0

    def prev(self):
        return Chunk(self.i, 0) if self.slot == 1 else Chunk(self.i - 1, 1)

    def next(self):
        return Chunk(self.i, 1) if self.slot == 0 else Chunk(self.i + 1, 0)

    def count(self, per, extra):
        return self.i * (2 * per) + (self.slot * per + extra)

    def uses(self, per, extra=0):
        return self.i * per + (per + extra)


def chunk_loop(eng, body):
    body(Chunk(0, 0), 2)
    body(Chunk(0, 1), 2)
    with eng.Fori(1, NCH // 2 - 1) as i:
        body(Chunk(i, 0), 2)
        body(Chunk(i, 1), 2)
    body(Chunk(NCH // 2 - 1, 0), 1)
    body(Chunk(NCH // 2 - 1, 1), 0)


def rows(t, c):
    first = t[bass.ds(c * CH, CUT * NT), :].rearrange("(p j) d -> p (j d)", j=NT)
    rest = t[bass.ds(c * CH + CUT * NT, CH - CUT * NT), :].rearrange("(p j) d -> p (j d)", j=NT)
    return first, rest


def dma_rows_in(eng, tile, t, c, sem):
    first, rest = rows(t, c)
    flat = tile.rearrange("p j d -> p (j d)")
    eng.dma_start(flat[0:CUT, :], first).then_inc(sem, 16)
    eng.dma_start(flat[CUT:RT, :], rest).then_inc(sem, 16)


def dma_rows_out(eng, t, c, tile, sem):
    first, rest = rows(t, c)
    flat = tile.rearrange("p j d -> p (j d)")
    eng.dma_start(first, flat[0:CUT, :]).then_inc(sem, 16)
    eng.dma_start(rest, flat[CUT:RT, :]).then_inc(sem, 16)


def load_features(eng, tile, t, c, sem):
    eng.dma_start(tile.rearrange("p k n -> p (k n)"), t[bass.ds(c, 1), :, :].rearrange("a p n -> (a p) n")).then_inc(sem, 16)


def need(eng, sem, value):
    if isinstance(value, int) and value <= 0:
        return
    eng.wait_ge(sem, value)


class Parts:
    pass


def load_qkv(eng, g, a, part):
    eng.dma_start(g.qkv_f[:, part], a["L0_mix_W_qkv"][:, QKV_ORDER[part]].rearrange("(k p) n -> p k n", p=P)
                  ).then_inc(g.qkv_loaded[part], 16)


def setup(nc, g, a):
    with ExitStack() as ctx:
        zeroed, pool_zeroed = (ctx.enter_context(nc.semaphore(n)) for n in ("zeroed", "pool_zeroed"))

        with nc.Block() as block:
            @block.sync
            def _(sp):
                dma_rows_in(sp, g.rows_in[:, 0], a["x"], 0, g.px_loaded[0])
                load_qkv(sp, g, a, 0)
                sp.dma_start(g.ea, a["edge_attr_64"].rearrange("(t p) f -> p t f", p=RT)).then_inc(g.ea_in, 16)

            @block.scalar
            def _(act):
                def small(dst, src):
                    act.dma_start(dst, src, allow_slow_non_contiguous=True).then_inc(g.small_in, 16)

                small(g.ident[:], a["c_ident"])
                small(g.eps[:], a["L0_gnn_eps"].partition_broadcast(RT))
                small(g.we[0:ED, :], a["L0_gnn_W_e"])
                small(g.we[ED:ED + 1, :], a["L0_gnn_b_e"].rearrange("(a n) -> a n", a=1))
                small(g.before[:], a["c_before"])
                small(g.trash[:], a["c_trash"])
                small(g.head_mask[:], a["c_head_mask"])

            @block.vector
            def _(dve):
                nc.vector.memset(g.minus_half[:], -0.5).then_inc(zeroed, 1)
                nc.vector.memset(g.half[:], 0.5).then_inc(zeroed, 1)
                nc.vector.memset(g.zeros_h[:], 0.0).then_inc(zeroed, 1)
                nc.vector.memset(g.ones_col[:], 1.0).then_inc(zeroed, 1)
                nc.vector.memset(g.zeros[:], 0.0).then_inc(zeroed, 1)
                nc.vector.memset(g.ones_w[:], 0.0).then_inc(zeroed, 1)
                nc.vector.memset(g.ones_q[:], 0.0).then_inc(zeroed, 1)
                dve.wait_ge(zeroed, 7)
                nc.vector.memset(g.ones_w[0:3, :], 1.0).then_inc(zeroed, 1)
                nc.vector.memset(g.ones_q[0:3, :], QS).then_inc(zeroed, 1)

            @block.gpsimd
            def _(pool):
                nc.gpsimd.memset(g.f1_bias[:], 0.0).then_inc(pool_zeroed, 1)
                nc.gpsimd.memset(g.out_bias[:], 0.0).then_inc(pool_zeroed, 1)
                nc.gpsimd.memset(g.eb2[:], 0.0).then_inc(pool_zeroed, 1)
                nc.gpsimd.memset(g.k_sum[:], 0.0).then_inc(pool_zeroed, 1)
                pool.wait_ge(pool_zeroed, 4)
                nc.gpsimd.memset(g.ea_t[ED:ED + 1, :], 1.0).then_inc(pool_zeroed, 1)


def project(nc, g, a):
    TURN = 6
    MM = 12
    with ExitStack() as ctx:
        def sb(name, shape, dt=F32):
            return ctx.enter_context(nc.sbuf_tensor(name, shape, dt))

        def sem(name):
            return ctx.enter_context(nc.semaphore(name))

        def sems(*names):
            return [sem(n) for n in names]

        x_in = g.rows_in
        xn = sb("xn", [RT, 2, NT, D])
        h0 = sb("h0", [RT, NT, D])
        xt_hi = sb("xt_hi", [P, 2, KT, CH], F16)
        xt_lo = sb("xt_lo", [P, 2, KT, CH], F16)
        stats = sb("stats", [RT, NT, 6])
        mv = sb("mv", [RT, NT, 2])
        var_eps = sb("var_eps", [RT, NT])
        rstd = sb("rstd", [RT, NT])
        e_x = sb("e_x", [P, 2, D])
        r_x = sb("r_x", [P, 2, D])
        k_f = sb("k_f", [RT, 2, D])
        k_hi = sb("k_hi", [RT, 2, D], F16)
        k_lo = sb("k_lo", [RT, 2, D], F16)
        v_hi = sb("v_hi", [RT, 2, D], F16)
        v_lo = sb("v_lo", [RT, 2, D], F16)
        q_f = g.feat_in
        src_i = sb("src_i", [RT, 2], I32)
        dst_i = sb("dst_i", [RT, 2], I32)
        dst_row = sb("dst_row", [RT, 2, RT], I32)
        dst_f = sb("dst_f", [RT, 1])
        x_src = sb("x_src", [RT, 2, D])
        e_stats = sb("e_stats", [RT, 6])
        e_mv = sb("e_mv", [RT, 2])
        e_var = sb("e_var", [RT, 1])
        e_rstd = sb("e_rstd", [RT, 1])
        xn_src = sb("xn_src", [RT, D])
        ea_now = sb("ea_now", [ED + 1, RT])
        msg_in = sb("msg_in", [RT, D])
        msg = sb("msg", [RT, D])
        same = sb("same", [RT, RT])
        same_before = sb("same_before", [RT, RT])
        again = sb("again", [RT, 2])
        to_trash = sb("to_trash", [RT, 1])

        turn_ps = ctx.enter_context(nc.psum_tensor("turn_ps", [P, 2, 512], F32))
        mm_ps = ctx.enter_context(nc.psum_tensor("mm_ps", [P, 4, 512], F32))
        kv_ps = ctx.enter_context(nc.psum_tensor("kv_ps", [P, 512], F32))
        ks_ps = ctx.enter_context(nc.psum_tensor("ks_ps", [P, 512], F32))

        x_loaded = g.px_loaded
        dst_loaded = sems("dst_loaded0", "dst_loaded1")
        src_loaded = sems("src_loaded0", "src_loaded1")
        gathered = sems("gathered0", "gathered1")
        q_stored = sems("q_stored0", "q_stored1")
        ea_turned, ea_copied, w_hi_done, w_lo_done, spare_zeroed, eps_done = sems(
            "ea_turned", "ea_copied", "w_hi_done", "w_lo_done", "spare_zeroed", "eps_done")
        h_stored, stats_done, mv_done, var_done, rstd_done, xn_done, h0_done = sems(
            "h_stored", "stats_done", "mv_done", "var_done", "rstd_done", "xn_done", "h0_done")
        turned, turn_hi, turn_free, mm_done, act_mm_free, v_mm_free = sems(
            "turned", "turn_hi", "turn_free", "mm_done", "act_mm_free", "v_mm_free")
        v_hi_done, phi_done, k_hi_done, k_lo_done, kv_done = sems(
            "v_hi_done", "phi_done", "k_hi_done", "k_lo_done", "kv_done")
        e_mv_done, e_var_done, e_rstd_done, edge_step, ea_ready, msg_in_done, msg_done = sems(
            "e_mv_done", "e_var_done", "e_rstd_done", "edge_step", "ea_ready", "msg_in_done", "msg_done")
        STEPS = 8
        src_tiles = a["src"].rearrange("(t p) -> t p", p=RT)
        dst_tiles = a["dst"].rearrange("(t p) -> t p", p=RT)

        with nc.Block() as block:
            @block.sync
            def _(sp):
                sp.sem_inc(q_stored[0], 16)
                sp.sem_inc(q_stored[1], 16)
                sp.sem_inc(h_stored, 32)

                def load_edges(at, s):
                    sp.dma_start(src_i[:, s:s + 1], src_tiles[bass.ds(at, 1), :].rearrange("a p -> p a"),
                                 allow_slow_non_contiguous=True).then_inc(src_loaded[s], 16)
                    sp.dma_start(dst_i[:, s:s + 1], dst_tiles[bass.ds(at, 1), :].rearrange("a p -> p a"),
                                 allow_slow_non_contiguous=True).then_inc(dst_loaded[s], 16)
                    sp.dma_start(dst_row[:, s, :], dst_tiles[bass.ds(at, 1), :].broadcast_to([RT, RT])).then_inc(dst_loaded[s], 16)

                sp.wait_ge(g.small_in, SMALL * 16)
                for part in (1, 2):
                    load_qkv(sp, g, a, part)
                load_edges(0, 0)
                load_edges(1, 1)
                dma_rows_in(sp, x_in[:, 1], a["x"], 1, x_loaded[1])

                def small(dst, src):
                    sp.dma_start(dst, src, allow_slow_non_contiguous=True).then_inc(g.small_in, 16)

                small(g.gb1[:], a["L0_gnn_b1"].rearrange("(m p) -> p m", p=P))
                small(g.g1[:], a["L0_gnn_g1"].rearrange("(m p) -> p m", p=P))
                small(g.beta1[:], a["L0_gnn_beta1"].rearrange("(m p) -> p m", p=P))
                small(g.gb2[:], a["L0_gnn_b2"].rearrange("(m p) -> p m", p=P))
                small(g.g2[:], a["L0_gnn_g2"].rearrange("(m p) -> p m", p=P))
                small(g.beta2[:], a["L0_gnn_beta2"].rearrange("(m p) -> p m", p=P))
                small(g.out_g[:], a["L0_ffn_out_g"].partition_broadcast(RT))
                small(g.out_b[:], a["L0_ffn_out_b"].partition_broadcast(RT))
                small(g.ident_h[:], a["c_ident_h"])
                small(g.spread[:], a["c_spread"])
                small(g.expert[:], a["c_expert"].partition_broadcast(RT))

                def step(c, follow):
                    s = c.slot
                    if follow == 2:
                        wait(sp, g.sp_tick, xn_done, c.count(NT, NT))
                        wait(sp, g.sp_tick, gathered[s], c.uses(16))
                        wait(sp, g.sp_tick, edge_step, c.count(STEPS, 7))
                        dma_rows_in(sp, x_in[:, s], a["x"], c.at + 2, x_loaded[s])
                        load_edges(c.at + 2, s)
                    else:
                        sp.wait_ge(xn_done, c.count(NT, NT))
                        dma_rows_in(sp, g.rows_in[:, s], a["x"], s, g.x_loaded[s])
                    if follow == 0:
                        sp.wait_ge(q_stored[0], 16 + 16 * NCH // 2)
                        load_features(sp, g.feat_in[:, 0], g.q_t, 0, g.q_loaded[0])
                    wait(sp, g.sp_tick, h0_done, c.count(NT, 2 * NT))
                    dma_rows_out(sp, g.h_rows, c.at, h0[:], h_stored)
                    wait(sp, g.sp_tick, phi_done, c.count(2 * NT, 2 + 2 * NT))
                    sp.dma_start(g.q_t[bass.ds(c.at, 1), :, :].rearrange("a p n -> (a p) n"),
                                 q_f[:, s].rearrange("p k n -> p (k n)")).then_inc(q_stored[s], 16)

                chunk_loop(sp, step)
                sp.wait_ge(q_stored[1], 16 + 16 * NCH // 2)
                load_features(sp, g.feat_in[:, 1], g.q_t, 1, g.q_loaded[1])
                sp.wait_ge(h_stored, 32 + 32 * NCH)
                sp.wait_ge(g.small_in, 16 * (SMALL + 11))

            @block.gpsimd
            def _(pool):
                def gather(s):
                    pool.indirect_dma_start(x_src[:, s, :], None, a["x"],
                                            bass.IndirectOffsetOnAxis(ap=src_i[:, s:s + 1], axis=0),
                                            bounds_check=N - 1, oob_is_err=True).then_inc(gathered[s], 16)

                def row_rstd(c):
                    pool.wait_ge(mv_done, c.count(NT, NT))
                    pool.sem_inc(g.pool_tick, 1)
                    nc.gpsimd.tensor_scalar(var_eps[:], mv[:, :, 1], LN_EPS, None, ALU.add).then_inc(var_done, 1)
                    pool.wait_ge(var_done, c.count(1, 1))
                    nc.gpsimd.tensor_tensor(rstd[:], var_eps[:], g.minus_half[0:RT, 0:NT], ALU.pow).then_inc(rstd_done, 1)

                pool.sem_inc(h0_done, NT)
                pool.dma_start(g.h_rows[N:N + RT, :], g.zeros[:]).then_inc(spare_zeroed, 16)
                row_rstd(Chunk(0, 0))
                pool.wait_ge(eps_done, 1)
                for s in range(2):
                    pool.wait_ge(src_loaded[s], 16)
                    gather(s)

                def step(c, follow):
                    s = c.slot
                    if follow:
                        row_rstd(c.next())
                    pool.wait_ge(e_mv_done, c.count(1, 1))
                    pool.sem_inc(g.pool_tick, 1)
                    nc.gpsimd.tensor_scalar(e_var[:], e_mv[:, 1:2], LN_EPS, None, ALU.add).then_inc(e_var_done, 1)
                    pool.wait_ge(e_var_done, c.count(1, 1))
                    nc.gpsimd.tensor_tensor(e_rstd[:], e_var[:], g.minus_half[0:RT, 0:1], ALU.pow).then_inc(e_rstd_done, 1)
                    pool.wait_ge(turned, c.count(TURN, 5))
                    pool.sem_inc(g.pool_tick, 1)
                    nc.gpsimd.tensor_copy(ea_now[:], g.ea_t[:, bass.ds(c.at * RT, RT)]).then_inc(ea_ready, 1)
                    pool.wait_ge(h_stored, c.count(32, 32))
                    pool.wait_ge(xn_done, c.count(NT, NT))
                    pool.sem_inc(g.pool_tick, 1)
                    for j in range(NT):
                        nc.gpsimd.tensor_scalar(h0[:, j, :], xn[:, s, j, :], g.one_eps[:], None, ALU.mult).then_inc(h0_done, 1)
                    if follow == 2:
                        pool.wait_ge(src_loaded[s], c.uses(16, 16))
                        pool.wait_ge(edge_step, c.count(STEPS, 8))
                        pool.sem_inc(g.pool_tick, 1)
                        gather(s)

                chunk_loop(pool, step)
                pool.wait_ge(spare_zeroed, 16)

            @block.scalar
            def _(act):
                act.sem_inc(act_mm_free, 8)

                def phi_parts(c, u, bank):
                    b = u % 2
                    n = RT if u < NT else P
                    w = D if u < NT else CH
                    act.wait_ge(phi_done, c.count(8, u + 1))
                    nc.scalar.activation(e_x[0:n, b, 0:w], mm_ps[0:n, bank, 0:w], ACT.Exp, scale=1 / WS)
                    nc.scalar.activation(r_x[0:n, b, 0:w], mm_ps[0:n, bank, 0:w], ACT.Relu, scale=1 / WS).then_inc(act_mm_free, 1)

                def turn_high(index, slot, k):
                    act.wait_ge(turned, index)
                    nc.scalar.copy(xt_hi[:, slot, k, :], turn_ps[:, k % 2, 0:CH]).then_inc(turn_hi, 1)

                def weight_high(part):
                    act.wait_ge(g.qkv_loaded[part], 16)
                    nc.scalar.activation(g.wqkv_hi[:, :, QKV_ORDER[part]], g.qkv_f[:, part], ACT.Copy,
                                         scale=WS).then_inc(w_hi_done, 1)

                weight_high(0)
                for group in range(5):
                    act.wait_ge(ea_turned, group + 1)
                    nc.scalar.copy(g.ea_t[0:ED, group * CH:(group + 1) * CH], mm_ps[0:ED, group % 4, 0:CH]).then_inc(ea_copied, 1)
                for k in range(KT):
                    turn_high(k + 1, 0, k)
                weight_high(1)
                weight_high(2)

                def step(c, follow):
                    for j in range(NT):
                        act.wait_ge(mm_done, c.count(MM, 2 * j + 1))
                        phi_parts(c, j, (2 * j) % 4)
                        act.wait_ge(mm_done, c.count(MM, 2 * j + 2))
                        act.wait_ge(kv_done, c.count(NT, j + 1))
                        nc.scalar.activation(v_hi[:, j % 2, :], mm_ps[0:RT, (2 * j + 1) % 4, :], ACT.Copy,
                                             scale=1 / WS).then_inc(v_hi_done, 1)
                        act.wait_ge(phi_done, c.count(8, 2 + j + 1))
                        nc.scalar.copy(k_hi[:, j % 2, :], k_f[:, j % 2, :]).then_inc(k_hi_done, 1)
                        if j and follow:
                            turn_high(c.count(TURN, TURN + j), c.next().slot, j - 1)
                    for m in range(KT):
                        act.wait_ge(mm_done, c.count(MM, 8 + m + 1))
                        phi_parts(c, NT + m, (8 + m) % 4)
                        if m == 0 and follow:
                            turn_high(c.count(TURN, TURN + 4), c.next().slot, 3)
                        if m == 1:
                            act.wait_ge(msg_in_done, c.count(1, 1))
                            act.wait_ge(turned, c.count(TURN, TURN))
                            nc.scalar.activation(msg[:], msg_in[:], ACT.Relu).then_inc(msg_done, 1)

                chunk_loop(act, step)

            @block.vector
            def _(dve):
                def row_stats(c):
                    dve.wait_ge(x_loaded[c.slot], c.uses(32))
                    for j in range(NT):
                        nc.vector.bn_stats(stats[:, j, :], x_in[:, c.slot, j, :]).then_inc(stats_done, 1)
                    dve.wait_ge(stats_done, c.count(NT, NT))
                    dve.sem_inc(g.dve_tick, 1)
                    nc.vector.bn_aggr(mv[:, 0, :], stats[:, 0, :]).then_inc(mv_done, 1)
                    for j in range(1, NT):
                        nc.vector.bn_aggr(mv[:, j, :], stats[:, j, :]).then_inc(mv_done, 1)

                def normalise(c):
                    dve.wait_ge(rstd_done, c.count(1, 1))
                    for j in range(NT):
                        nc.vector.tensor_scalar(xn[:, c.slot, j, :], x_in[:, c.slot, j, :], mv[:, j, 0:1],
                                                rstd[:, j:j + 1], ALU.subtract, ALU.mult).then_inc(xn_done, 1)

                def phi(c, u, out):
                    n = RT if u < NT else P
                    w = D if u < NT else CH
                    dve.wait_ge(act_mm_free, c.count(8, 8 + u + 1))
                    nc.vector.scalar_tensor_tensor(out, e_x[0:n, u % 2, 0:w], 1.0, r_x[0:n, u % 2, 0:w],
                                                   ALU.min, ALU.add).then_inc(phi_done, 1)

                def turn_low(index, slot, k, by=1):
                    dve.wait_ge(turn_hi, index)
                    nc.vector.tensor_tensor(xt_lo[:, slot, k, :], turn_ps[:, k % 2, 0:CH], xt_hi[:, slot, k, :],
                                            ALU.subtract).then_inc(turn_free, by)

                dve.sem_inc(phi_done, 2)
                first = Chunk(0, 0)
                row_stats(first)
                normalise(first)
                dve.wait_ge(g.small_in, SMALL * 16)
                nc.vector.tensor_scalar(g.one_eps[:], g.eps[:], 1.0, None, ALU.add).then_inc(eps_done, 1)

                def weight_low(part):
                    dve.wait_ge(w_hi_done, part + 1)
                    nc.vector.scalar_tensor_tensor(g.wqkv_lo[:, :, QKV_ORDER[part]], g.qkv_f[:, part], WS,
                                                   g.wqkv_hi[:, :, QKV_ORDER[part]], ALU.mult, ALU.subtract).then_inc(w_lo_done, 1)

                weight_low(0)
                for k in range(KT):
                    turn_low(k + 1, 0, k, 1 if k < KT - 1 else 3)
                weight_low(1)
                weight_low(2)

                def step(c, follow):
                    s = c.slot
                    nxt = c.next()
                    if follow:
                        dve.wait_ge(xn_done, c.count(NT, NT))
                        row_stats(nxt)
                    dve.wait_ge(gathered[s], c.uses(16))
                    nc.vector.bn_stats(e_stats[:], x_src[:, s, :]).then_inc(edge_step, 1)
                    dve.wait_ge(edge_step, c.count(STEPS, 1))
                    dve.sem_inc(g.dve_tick, 1)
                    nc.vector.bn_aggr(e_mv[:], e_stats[:]).then_inc(e_mv_done, 1)
                    for j in range(NT):
                        phi(c, j, k_f[:, j % 2, :])
                        dve.wait_ge(v_hi_done, c.count(NT, j + 1))
                        nc.vector.scalar_tensor_tensor(v_lo[:, j % 2, :], mm_ps[0:RT, (2 * j + 1) % 4, :], 1 / WS,
                                                       v_hi[:, j % 2, :], ALU.mult, ALU.subtract).then_inc(v_mm_free, 1)
                        dve.wait_ge(k_hi_done, c.count(NT, j + 1))
                        nc.vector.tensor_tensor(k_lo[:, j % 2, :], k_f[:, j % 2, :], k_hi[:, j % 2, :],
                                                ALU.subtract).then_inc(k_lo_done, 1)
                        if j == 0:
                            if follow:
                                dve.wait_ge(h0_done, c.count(NT, NT))
                                normalise(nxt)
                        elif follow:
                            turn_low(c.count(KT, KT + j), nxt.slot, j - 1)
                        if j == 1:
                            dve.wait_ge(dst_loaded[s], c.uses(32))
                            nc.vector.tensor_copy(dst_f[:], dst_i[:, s:s + 1]).then_inc(edge_step, 1)
                            dve.wait_ge(edge_step, c.count(STEPS, 2))
                            dve.wait_ge(turned, c.count(TURN, TURN))
                            nc.vector.tensor_scalar(same[:], dst_row[:, s, :], dst_f[:], None, ALU.is_equal).then_inc(edge_step, 1)
                            nc.vector.tensor_tensor(to_trash[:], g.trash[:], dst_f[:], ALU.subtract)
                            dve.wait_ge(edge_step, c.count(STEPS, 3))
                            nc.vector.tensor_tensor(same_before[:], same[:], g.before[:], ALU.mult).then_inc(edge_step, 1)
                        if j == 2:
                            dve.wait_ge(edge_step, c.count(STEPS, 4))
                            nc.vector.tensor_reduce(again[:, 0:1], same_before[:], AX.X, ALU.add).then_inc(edge_step, 1)
                            dve.wait_ge(edge_step, c.count(STEPS, 5))
                            nc.vector.tensor_scalar(again[:, 1:2], again[:, 0:1], 1.0, None, ALU.min).then_inc(edge_step, 1)
                            dve.wait_ge(edge_step, c.count(STEPS, 6))
                            nc.vector.scalar_tensor_tensor(g.target[:, bass.ds(c.at, 1)], again[:, 1:2], to_trash[:],
                                                           dst_f[:], ALU.mult, ALU.add).then_inc(edge_step, 1)
                            dve.wait_ge(e_rstd_done, c.count(1, 1))
                            nc.vector.tensor_scalar(xn_src[:], x_src[:, s, :], e_mv[:, 0:1], e_rstd[:],
                                                    ALU.subtract, ALU.mult).then_inc(edge_step, 1)
                    dve.wait_ge(q_stored[s], c.uses(16))
                    for m in range(KT):
                        phi(c, NT + m, q_f[:, s, m, :])
                        if m == 0 and follow:
                            turn_low(c.count(KT, 2 * KT), nxt.slot, 3)
                        if m == 1:
                            dve.wait_ge(turned, c.count(TURN, TURN + (5 if follow else 1)))
                            dve.wait_ge(edge_step, c.count(STEPS, 8))
                            nc.vector.tensor_tensor(msg_in[:], turn_ps[0:RT, 0, :], xn_src[:], ALU.add).then_inc(msg_in_done, 1)
                    dve.wait_ge(turned, c.count(TURN, TURN + (6 if follow else 2)))
                    nc.vector.tensor_copy(g.totals[0:RT, bass.ds(c.at, 1), :].rearrange("p a d -> p (a d)"),
                                          turn_ps[0:RT, 1, :]).then_inc(turn_free, 2)

                chunk_loop(dve, step)
                dve.wait_ge(kv_done, 4 + NT * NCH)
                for h in range(KT):
                    nc.vector.scalar_tensor_tensor(g.kv[:, h, :], kv_ps[:, h * P:(h + 1) * P], NS, g.head_mask[:],
                                                   ALU.mult, ALU.mult)
                flat = g.k_sum[:].rearrange("p k h -> p (k h)")
                step = TWICE + 2
                for at in (0, TWICE - HEADS):
                    nc.vector.tensor_scalar(flat[0:HD, at:KT * TWICE:step], ks_ps[0:HD, 0:KT], NS, None, ALU.mult)
                    nc.vector.tensor_scalar(flat[HD:P, at + 1:KT * TWICE:step], ks_ps[HD:P, 0:KT], NS, None, ALU.mult)

            @block.tensor
            def _(pe):
                def transposes(slot, k, by=1):
                    for j in range(NT):
                        t = nc.tensor.transpose(turn_ps[:, k % 2, j * RT:(j + 1) * RT],
                                                xn[:, slot, j, k * P:(k + 1) * P], g.ident[0:RT, 0:RT])
                    t.then_inc(turned, by)

                pe.wait_ge(g.small_in, SMALL * 16)
                pe.wait_ge(g.ea_in, 16)
                for t in range(NCH):
                    if t == 16:
                        pe.wait_ge(ea_copied, 1)
                    e = nc.tensor.transpose(mm_ps[0:ED, t // 4 % 4, (t % 4) * RT:(t % 4 + 1) * RT], g.ea[:, t, :],
                                            g.ident[0:RT, 0:RT])
                    if t % 4 == 3:
                        e.then_inc(ea_turned, 1)
                nc.tensor.matmul(kv_ps[:], g.zeros_h[:, 0:P], g.zeros_h[:], start=True, stop=False).then_inc(kv_done, 1)
                nc.tensor.matmul(ks_ps[:, 0:KT], g.zeros_h[:, 0:P], g.zeros_h[:, 0:KT], start=True, stop=False).then_inc(kv_done, 1)
                pe.wait_ge(xn_done, NT)
                for k in range(KT):
                    if k >= 2:
                        pe.wait_ge(turn_free, k - 1)
                    transposes(0, k, 1 if k < KT - 1 else 3)

                def row_product(c, j, w0, bank):
                    s = c.slot
                    rows_ = slice(j * RT, (j + 1) * RT)
                    for k in range(KT):
                        last = split3(nc, mm_ps[0:RT, bank, :], xt_hi[:, s, k, rows_], xt_lo[:, s, k, rows_],
                                      g.wqkv_hi[:, k, w0:w0 + D], g.wqkv_lo[:, k, w0:w0 + D], k == 0, k == KT - 1)
                    last.then_inc(mm_done, 1)

                def sums(c, j):
                    pe.wait_ge(v_mm_free, c.count(NT, j + 1))
                    pe.wait_ge(k_lo_done, c.count(NT, j + 1))
                    b = j % 2
                    for h in range(KT):
                        hs = slice(h * P, (h + 1) * P)
                        split3(nc, kv_ps[:, hs], v_hi[:, b, hs], v_lo[:, b, hs], k_hi[:, b, hs], k_lo[:, b, hs], False, False)
                        nc.tensor.matmul(ks_ps[:, h:h + 1], k_hi[:, b, hs], g.ones_col[0:RT, :], start=False, stop=False, skip_group_check=True)
                        last = nc.tensor.matmul(ks_ps[:, h:h + 1], k_lo[:, b, hs], g.ones_col[0:RT, :], start=False, stop=False, skip_group_check=True)
                    last.then_inc(kv_done, 1)

                def step(c, follow):
                    s = c.slot
                    nxt = c.next()
                    pe.wait_ge(turn_free, c.count(TURN, 4))
                    if c.first:
                        pe.wait_ge(ea_copied, 5)
                    for j in range(NT):
                        pe.wait_ge(act_mm_free, c.count(8, [5, 7, 9, 10][j]))
                        if c.first and j == 0:
                            pe.wait_ge(w_lo_done, 1)
                        row_product(c, j, D, (2 * j) % 4)
                        if j < 2:
                            pe.wait_ge(act_mm_free, c.count(8, [6, 8][j]))
                        else:
                            pe.wait_ge(v_mm_free, c.count(NT, j - 1))
                        if c.first and j == 0:
                            pe.wait_ge(w_lo_done, 2)
                        row_product(c, j, 2 * D, (2 * j + 1) % 4)
                        if j:
                            sums(c, j - 1)
                            if follow:
                                pe.wait_ge(xn_done, nxt.count(NT, NT))
                                pe.wait_ge(turn_free, c.count(TURN, TURN + j - 2))
                                transposes(nxt.slot, j - 1)
                    if c.first:
                        pe.wait_ge(w_lo_done, 3)
                    for m in range(KT):
                        if m % 2 == 0:
                            pe.wait_ge(act_mm_free, c.count(8, [11, None, 12][m]))
                        else:
                            pe.wait_ge(v_mm_free, c.count(NT, [None, 3, None, 4][m]))
                        for k in range(KT):
                            w = slice(m * P, (m + 1) * P)
                            last = split3(nc, mm_ps[:, m, 0:CH], g.wqkv_hi[:, k, w], g.wqkv_lo[:, k, w],
                                          xt_hi[:, s, k, :], xt_lo[:, s, k, :], k == 0, k == KT - 1)
                        last.then_inc(mm_done, 1)
                        if m == 0:
                            sums(c, NT - 1)
                            if follow:
                                pe.wait_ge(turn_free, c.count(TURN, TURN + 2))
                                transposes(nxt.slot, 3)
                        if m == 1:
                            pe.wait_ge(turn_free, c.count(TURN, TURN + (3 if follow else -1)))
                            pe.wait_ge(ea_ready, c.count(1, 1))
                            nc.tensor.matmul(turn_ps[0:RT, 0, :], ea_now[:], g.we[:], start=True, stop=True).then_inc(turned, 1)
                    pe.wait_ge(turn_free, c.count(TURN, TURN + (4 if follow else 0)))
                    pe.wait_ge(msg_done, c.count(1, 1))
                    nc.tensor.matmul(turn_ps[0:RT, 1, :], same[:], msg[:], start=True, stop=True).then_inc(turned, 1)

                chunk_loop(pe, step)
                nc.tensor.matmul(kv_ps[:], g.zeros_h[:, 0:P], g.zeros_h[:], start=False, stop=True).then_inc(kv_done, 1)
                nc.tensor.matmul(ks_ps[:, 0:KT], g.zeros_h[:, 0:P], g.zeros_h[:, 0:KT], start=False, stop=True).then_inc(kv_done, 1)


def three_parts(nc, pool, rest, full, parts, step, wait_steps):
    step(nc.gpsimd.tensor_scalar(rest[:], full[:], WS, None, ALU.mult))
    for m in range(3):
        wait_steps()
        step(nc.gpsimd.tensor_copy(parts[:, m, :], rest[:]))
        wait_steps()
        step(nc.gpsimd.tensor_tensor(rest[:], rest[:], parts[:, m, :], ALU.subtract))


def attend(nc, g, a):
    with ExitStack() as ctx:
        def sb(name, shape, dt=F32):
            return ctx.enter_context(nc.sbuf_tensor("at_" + name, shape, dt))

        def sems(*names):
            return [ctx.enter_context(nc.semaphore("at_" + n)) for n in names]

        wo_f = sb("wo_f", [P, KT, D])
        m_hi = sb("m_hi", [P, KT, D], F16)
        m_lo = sb("m_lo", [P, KT, D], F16)
        q_in, x_in = g.feat_in, g.rows_in
        rden = sb("rden", [TWICE, CH])
        rden_hi = sb("rden_hi", [TWICE, CH], F16)
        rden_t = sb("rden_t", [P, CH], F16)
        q_norm = sb("q_norm", [P, 2, CH])
        qn_hi = sb("qn_hi", [P, 2, KT, CH], F16)
        qn_lo = sb("qn_lo", [P, 2, KT, CH], F16)
        r_out = sb("r_out", [RT, 2, NT, D])
        f1_f = sb("f1_f", [P, KT, F1])
        stage = sb("stage", [P, KT * F1 + 2 * D])
        eb2_f = sb("eb2_f", [NE, D])
        eb2_part = sb("eb2_part", [NE, 2, D], F16)
        ln_g = sb("ln_g", [P, KT])
        ln_b = sb("ln_b", [P, KT])
        bo_row = sb("bo_row", [1, D])
        bo_part = sb("bo_part", [1, 3, D], F16)
        den_ps = ctx.enter_context(nc.psum_tensor("den_ps", [P, 512], F32))
        spread_ps = ctx.enter_context(nc.psum_tensor("spread_ps", [P, 2, 512], F32))
        o_ps = ctx.enter_context(nc.psum_tensor("o_ps", [P, 4, 512], F32))

        r_st0, r_st1 = sems("r_stored0", "r_stored1")
        bo_in, f_in, bo_placed, placed, part_step, lnb_done = sems("bo_in", "f_in", "bo_placed", "placed", "part_step", "lnb_done")
        q_loaded, x_loaded, r_stored = g.q_loaded, g.x_loaded, (r_st0, r_st1)
        m_mm, m_hi_done, m_lo_done = sems("m_mm", "m_hi_done", "m_lo_done")
        den_done, den_step, rden_done = sems(
            "den_done", "den_step", "rden_done")
        spread_done, qn_done, qn_hi_done, qn_lo_done, o_done, r_done, added, zero_done = sems(
            "spread_done", "qn_done", "qn_hi_done", "qn_lo_done", "o_done", "r_done", "added", "zero_done")

        f1_g = stage[:, 0:KT * F1].rearrange("p (k n) -> p k n", k=KT)
        f2_f = stage[:, KT * F1:].rearrange("p (k n) -> p k n", k=2)
        half = stage[:, 0:KT * D]
        w1 = a["L0_gnn_W1"].rearrange("(k p) n -> p k n", p=P)
        w2 = a["L0_gnn_W2"].rearrange("(k p) n -> p k n", p=P)

        with nc.Block() as block:
            @block.sync
            def _(sp):
                sp.dma_start(wo_f[:], a["L0_mix_W_out"].rearrange("(k p) n -> p k n", p=P)).then_inc(g.qkv_loaded[0], 16)
                sp.dma_start(bo_row[:], a["L0_mix_b_out"].rearrange("(a n) -> a n", a=1)).then_inc(bo_in, 16)
                for k in range(KT):
                    sp.dma_start(f1_f[:, k, 0:FH].rearrange("p (e h) -> p e h", e=NE),
                                 a["L0_ffn_W1"][:, k * P:(k + 1) * P, :].rearrange("e p h -> p e h")).then_inc(f_in, 16)
                sp.dma_start(f1_f[:, :, FH:F1], a["L0_ffn_Wg"].rearrange("(k p) e -> p k e", p=P)).then_inc(f_in, 16)
                sp.dma_start(f2_f, a["L0_ffn_W2"].rearrange("e h d -> (e h) d").rearrange("(k p) d -> p k d", p=P)).then_inc(f_in, 16)
                sp.dma_start(eb2_f[:], a["L0_ffn_b2"]).then_inc(f_in, 16)
                sp.dma_start(g.b1_row[:, 0:FH], a["L0_ffn_b1"].rearrange("e h -> (e h)").rearrange("(a n) -> a n", a=1)).then_inc(f_in, 16)
                for dst, name in ((ln_g, "L0_ffn_ln_g"), (ln_b, "L0_ffn_ln_b")):
                    sp.dma_start(dst[:], a[name].rearrange("(k p) -> p k", p=P), allow_slow_non_contiguous=True).then_inc(f_in, 16)
                sp.sem_inc(r_stored[0], 32)
                sp.sem_inc(r_stored[1], 32)

                def step(c, follow):
                    s = c.slot
                    if follow == 2:
                        wait(sp, g.sp_tick, qn_done, c.count(KT, KT))
                        load_features(sp, q_in[:, s], g.q_t, c.at + 2, q_loaded[s])
                    wait(sp, g.sp_tick, r_done, c.count(NT, 2 * NT))
                    if follow < 2:
                        sp.wait_ge(added, 16 * NCH)
                        dma_rows_in(sp, g.rows_in[:, s], g.h_rows, s, g.h_loaded[s])
                    dma_rows_out(sp, g.r_rows, c.at, r_out[:, s], r_stored[s])
                    if follow == 2:
                        dma_rows_in(sp, x_in[:, s], a["x"], c.at + 2, x_loaded[s])

                chunk_loop(sp, step)
                for s in range(2):
                    sp.wait_ge(r_stored[s], 32 + 32 * NCH // 2)

            @block.gpsimd
            def _(pool):
                steps = 0
                halves = 0

                def step(instruction):
                    nonlocal steps
                    instruction.then_inc(part_step, 1)
                    steps += 1

                def two_parts(hi, lo, full):
                    pool.wait_ge(part_step, steps)
                    step(nc.gpsimd.tensor_copy(hi, full))
                    pool.wait_ge(part_step, steps)
                    step(nc.gpsimd.tensor_tensor(lo, full, hi, ALU.subtract))

                pool.wait_ge(bo_in, 16)
                three_parts(nc, pool, bo_row, bo_row, bo_part, step, lambda: pool.wait_ge(part_step, steps))
                pool.wait_ge(part_step, steps)
                for m in range(3):
                    pool.dma_start(g.out_bias[m:m + 1, :], bo_part[:, m, :]).then_inc(bo_placed, 16)
                for t in range(NCH):
                    need(pool, added, 16 * t)
                    pool.indirect_dma_start(g.h_rows, bass.IndirectOffsetOnAxis(ap=g.target[:, t:t + 1], axis=0),
                                            g.totals[0:RT, t, :], None, compute_op=ALU.add,
                                            bounds_check=N + RT - 1, oob_is_err=True).then_inc(added, 16)
                    if t == 0:
                        pool.wait_ge(f_in, 16 * 10)
                    if t < KT:
                        step(nc.gpsimd.tensor_scalar(f1_g[:, t, :], f1_f[:, t, :], ln_g[:, t:t + 1], WS, ALU.mult, ALU.mult))
                        two_parts(g.f1_hi[:, t, :], g.f1_lo[:, t, :], f1_g[:, t, :])
                    elif t < KT + 2:
                        b = t - KT
                        step(nc.gpsimd.tensor_scalar(f2_f[:, b, :], f2_f[:, b, :], WS, None, ALU.mult))
                        two_parts(g.f2_hi[:, b, :], g.f2_lo[:, b, :], f2_f[:, b, :])
                    elif t == KT + 2:
                        step(nc.gpsimd.tensor_scalar(eb2_f[:], eb2_f[:], WS, None, ALU.mult))
                        two_parts(eb2_part[:, 0, :], eb2_part[:, 1, :], eb2_f[:])
                        pool.wait_ge(part_step, steps)
                        for m in range(3):
                            pool.dma_start(g.eb2[NE * m:NE * (m + 1), :], eb2_part[:, 0 if m < 2 else 1, :]).then_inc(placed, 16)
                    elif t < KT + 3 + 12:
                        n = t - (KT + 3)
                        w, k, per = (w1, n, KT // 2) if n < KT else (w2, n - KT, KT)
                        if k % per == 0:
                            pool.wait_ge(part_step, steps)
                            pool.dma_start(half.rearrange("p (k n) -> p k n", k=per), w[:, k:k + per, :]).then_inc(g.w_in, 16)
                            halves += 1
                            pool.wait_ge(g.w_in, 16 * halves)
                        full = half.rearrange("p (k n) -> p k n", k=per)[:, k % per, :]
                        hi, lo = (g.w1_hi, g.w1_lo) if n < KT else (g.w2_hi, g.w2_lo)
                        step(nc.gpsimd.tensor_scalar(full, full, WS, None, ALU.mult))
                        two_parts(hi[:, k, :], lo[:, k, :], full)
                pool.wait_ge(placed, 3 * 16)
                pool.wait_ge(added, 16 * NCH)

            @block.scalar
            def _(act):
                def high(c, k):
                    act.wait_ge(qn_done, c.count(KT, k + 1))
                    nc.scalar.copy(qn_hi[:, c.slot, k, :], q_norm[:, k % 2, :]).then_inc(qn_hi_done, 1)

                def product_high(k):
                    act.wait_ge(m_mm, k + 1)
                    nc.scalar.activation(m_hi[:, k, :], o_ps[:, k, :], ACT.Copy, scale=WS).then_inc(m_hi_done, 1)

                for k in range(KT):
                    product_high(k)
                for k in range(KT):
                    high(Chunk(0, 0), k)

                def step(c, follow):
                    if follow:
                        for k in range(KT):
                            high(c.next(), k)

                chunk_loop(act, step)

            @block.vector
            def _(dve):
                nc.vector.memset(g.b1_row[:, FH:F1], 0.0).then_inc(zero_done, 1)
                nc.vector.memset(rden_t[:], 0.0).then_inc(zero_done, 1)
                dve.wait_ge(zero_done, 2)
                dve.sem_inc(r_done, NT)

                def reciprocals(c):
                    dve.wait_ge(den_done, c.count(1, 1))
                    nc.vector.tensor_scalar(rden[:], den_ps[0:TWICE, 0:CH], 1 / QS, ATT_EPS * NS / QS, ALU.mult, ALU.add).then_inc(den_step, 1)
                    dve.wait_ge(den_step, c.count(3, 1))
                    nc.vector.reciprocal(rden[:], rden[:]).then_inc(den_step, 1)
                    dve.wait_ge(den_step, c.count(3, 2))
                    need(dve, spread_done, c.count(KT, 0))
                    nc.vector.tensor_copy(rden_t[0:HEADS, :], rden[0:HEADS, :]).then_inc(rden_done, 1)
                    nc.vector.tensor_copy(rden_hi[TWICE - HEADS:TWICE, :], rden[TWICE - HEADS:TWICE, :]).then_inc(den_step, 1)
                    dve.wait_ge(den_step, c.count(3, 3))
                    nc.vector.tensor_tensor(rden_t[TWICE - HEADS:TWICE, :], rden[TWICE - HEADS:TWICE, :],
                                            rden_hi[TWICE - HEADS:TWICE, :], ALU.subtract).then_inc(rden_done, 1)

                def normalise(c, pair):
                    for k in pair:
                        need(dve, qn_lo_done, c.count(KT, k - 1))
                        dve.wait_ge(spread_done, c.count(KT, k + 1))
                        nc.vector.tensor_tensor(q_norm[:, k % 2, :], spread_ps[:, k % 2, 0:CH], q_in[:, c.slot, k, :],
                                                ALU.mult).then_inc(qn_done, 1)
                    for k in pair:
                        dve.wait_ge(qn_hi_done, c.count(KT, k + 1))
                        nc.vector.tensor_tensor(qn_lo[:, c.slot, k, :], q_norm[:, k % 2, :], qn_hi[:, c.slot, k, :],
                                                ALU.subtract).then_inc(qn_lo_done, 1)

                reciprocals(Chunk(0, 0))
                for k in range(KT):
                    dve.wait_ge(m_hi_done, k + 1)
                    nc.vector.scalar_tensor_tensor(m_lo[:, k, :], o_ps[:, k, :], WS, m_hi[:, k, :],
                                                   ALU.mult, ALU.subtract).then_inc(m_lo_done, 1)
                normalise(Chunk(0, 0), (0, 1))
                normalise(Chunk(0, 0), (2, 3))

                def step(c, follow):
                    s = c.slot
                    if follow:
                        reciprocals(c.next())
                    dve.wait_ge(x_loaded[s], c.uses(32))
                    dve.wait_ge(r_stored[s], c.uses(32))
                    for j in range(NT):
                        dve.wait_ge(o_done, c.count(NT, j + 1))
                        nc.vector.scalar_tensor_tensor(r_out[:, s, j, :], o_ps[0:RT, j, :], 1 / (WS * QS), x_in[:, s, j, :],
                                                       ALU.mult, ALU.add).then_inc(r_done, 1)
                        if follow and j == 2:
                            normalise(c.next(), (0, 1))
                    if follow:
                        normalise(c.next(), (2, 3))

                chunk_loop(dve, step)
                dve.wait_ge(lnb_done, 1)
                nc.vector.tensor_tensor(g.b1_sum[:], g.b1_row[:], den_ps[0:1, 0:F1], ALU.add)

            @block.tensor
            def _(pe):
                def denominators(c):
                    pe.wait_ge(q_loaded[c.slot], c.uses(16))
                    need(pe, den_step, c.count(3, -2))
                    for k in range(KT):
                        last = nc.tensor.matmul(den_ps[0:TWICE, 0:CH], g.k_sum[:, k, :], q_in[:, c.slot, k, :],
                                                start=(k == 0), stop=(k == KT - 1))
                    last.then_inc(den_done, 1)

                def spread(c, k):
                    pe.wait_ge(rden_done, c.count(2, 2))
                    need(pe, qn_done, c.count(KT, k - 1))
                    nc.tensor.matmul(spread_ps[:, k % 2, 0:CH], g.spread[:, k * P:(k + 1) * P], rden_t[:],
                                     start=True, stop=True).then_inc(spread_done, 1)

                first = Chunk(0, 0)
                denominators(first)
                pe.wait_ge(g.qkv_loaded[0], 32)
                for k in range(KT):
                    nc.tensor.matmul(o_ps[:, k, :], g.kv[:, k, :], wo_f[:, k, :], start=True, stop=True).then_inc(m_mm, 1)
                for k in range(KT):
                    spread(first, k)
                pe.wait_ge(m_lo_done, KT)

                def step(c, follow):
                    s = c.slot
                    if follow:
                        denominators(c.next())
                    pe.wait_ge(qn_lo_done, c.count(KT, KT))
                    for j in range(NT):
                        pe.wait_ge(r_done, c.count(NT, j + 1))
                        for k in range(KT):
                            js = slice(j * RT, (j + 1) * RT)
                            split3(nc, o_ps[0:RT, j, :], qn_hi[:, s, k, js], qn_lo[:, s, k, js],
                                   m_hi[:, k, :], m_lo[:, k, :], k == 0, False)
                        if c.first and j == 0:
                            pe.wait_ge(bo_placed, 3 * 16)
                        nc.tensor.matmul(o_ps[0:RT, j, :], g.ones_q[:], g.out_bias[:], start=False, stop=True,
                                         skip_group_check=True).then_inc(o_done, 1)
                        if follow and j == 2:
                            spread(c.next(), 0)
                            spread(c.next(), 1)
                    if follow:
                        spread(c.next(), 2)
                        spread(c.next(), 3)

                chunk_loop(pe, step)
                pe.wait_ge(f_in, 16 * 10)
                for k in range(KT):
                    b = nc.tensor.matmul(den_ps[0:1, 0:F1], ln_b[:, k:k + 1], f1_f[:, k, :], start=(k == 0), stop=(k == KT - 1))
                b.then_inc(lnb_done, 1)


def batch_norm(nc, dve, pool_ready, pool_done, step, stats, mv, var_eps, rstd, gain, shift, scale, offset, tiles):
    for m in range(tiles):
        nc.vector.bn_aggr(mv[:, m, :], stats[:, m, :, :].rearrange("p c s -> p (c s)")).then_inc(step, 1)
    dve.wait_ge(step, tiles)
    nc.vector.tensor_scalar(var_eps[:, 0:tiles], mv[:, :, 1], BN_EPS, None, ALU.add).then_inc(pool_ready, 1)
    dve.wait_ge(pool_done, 1)
    nc.vector.tensor_tensor(scale[:, 0:tiles], gain[:, 0:tiles], rstd[:, 0:tiles], ALU.mult).then_inc(step, 1)
    dve.wait_ge(step, tiles + 1)
    nc.vector.tensor_tensor(var_eps[:, 0:tiles], mv[:, :, 0], scale[:, 0:tiles], ALU.mult).then_inc(step, 1)
    dve.wait_ge(step, tiles + 2)
    nc.vector.tensor_tensor(offset[:, 0:tiles], shift[:, 0:tiles], var_eps[:, 0:tiles], ALU.subtract).then_inc(step, 1)


def gnn_up(nc, g, a):
    MT = 2 * KT
    with ExitStack() as ctx:
        def sb(name, shape, dt=F32):
            return ctx.enter_context(nc.sbuf_tensor("up_" + name, shape, dt))

        def sems(*names):
            return [ctx.enter_context(nc.semaphore("up_" + n)) for n in names]

        h_in = g.rows_in
        b1_rest = sb("b1_rest", [1, F1])
        b1_part = sb("b1_part", [1, 3, F1], F16)
        ht_hi = sb("ht_hi", [P, 2, KT, CH], F16)
        ht_lo = sb("ht_lo", [P, 2, KT, CH], F16)
        h1 = sb("h1", [P, 2, MT, CH])
        stats = sb("stats", [P, MT, NCH, 6])
        mv = sb("mv", [P, MT, 2])
        var_eps = sb("var_eps", [P, MT])
        rstd = sb("rstd", [P, MT])
        turn_ps = ctx.enter_context(nc.psum_tensor("up_turn_ps", [P, KT, 512], F32))
        mm_ps = ctx.enter_context(nc.psum_tensor("up_mm_ps", [P, 4, 512], F32))
        part_step, placed = sems("part_step", "placed")
        st0, st1 = sems("h1_stored0", "h1_stored1")
        h_loaded, h1_stored = g.h_loaded, (st0, st1)
        turned, turn_hi, turn_lo, mm_done, h1_done, stats_done, var_done, rstd_done, bn_step = sems(
            "turned", "turn_hi", "turn_lo", "mm_done", "h1_done", "stats_done", "var_done", "rstd_done",
            "bn_step")

        with nc.Block() as block:
            @block.sync
            def _(sp):
                for s in range(2):
                    sp.sem_inc(h1_stored[s], 16)

                def step(c, follow):
                    s = c.slot
                    if follow == 2:
                        wait(sp, g.sp_tick, turned, c.count(KT, KT))
                        dma_rows_in(sp, h_in[:, s], g.h_rows, c.at + 2, h_loaded[s])
                    if follow == 1:
                        sp.wait_ge(h1_stored[0], 16 + 16 * (NCH // 2 - 1))
                        load_features(sp, g.feat_in.rearrange("p s k n -> p (s k) n"), g.h1_t, 0, g.h1_loaded[0])
                    wait(sp, g.sp_tick, h1_done, c.count(MT, 2 * MT))
                    sp.dma_start(g.h1_t[bass.ds(c.at, 1), :, :].rearrange("a p n -> (a p) n"),
                                 h1[:, s].rearrange("p m n -> p (m n)")).then_inc(h1_stored[s], 16)

                chunk_loop(sp, step)
                for s in range(2):
                    sp.wait_ge(h1_stored[s], 16 + 16 * NCH // 2)

            @block.scalar
            def _(act):
                def turn_high(c, k):
                    act.wait_ge(turned, c.count(KT, k + 1))
                    nc.scalar.copy(ht_hi[:, c.slot, k, :], turn_ps[:, k, 0:CH]).then_inc(turn_hi, 1)

                act.sem_inc(h1_done, MT)
                for k in range(KT):
                    turn_high(Chunk(0, 0), k)

                def step(c, follow):
                    s = c.slot
                    act.wait_ge(h1_stored[s], c.uses(16))
                    need(act, stats_done, c.count(MT, 0))
                    for m in range(MT):
                        act.wait_ge(mm_done, c.count(MT, m + 1))
                        nc.scalar.activation(h1[:, s, m, :], mm_ps[:, m % 4, 0:CH], ACT.Identity, bias=g.gb1[:, m:m + 1],
                                             scale=1 / WS).then_inc(h1_done, 1)
                        if follow and 1 <= m < 1 + KT:
                            turn_high(c.next(), m - 1)

                chunk_loop(act, step)

            @block.vector
            def _(dve):
                def turn_low(c, k):
                    dve.wait_ge(turn_hi, c.count(KT, k + 1))
                    nc.vector.tensor_tensor(ht_lo[:, c.slot, k, :], turn_ps[:, k, 0:CH], ht_hi[:, c.slot, k, :],
                                            ALU.subtract).then_inc(turn_lo, 1)

                for k in range(KT):
                    turn_low(Chunk(0, 0), k)

                def step(c, follow):
                    s = c.slot
                    for m in range(MT):
                        dve.wait_ge(h1_done, c.count(MT, MT + m + 1))
                        nc.vector.bn_stats(stats[:, m, bass.ds(c.at, 1), :].rearrange("p a s -> p (a s)"),
                                           h1[:, s, m, :]).then_inc(stats_done, 1)
                        if follow and 1 <= m < 1 + KT:
                            turn_low(c.next(), m - 1)

                chunk_loop(dve, step)
                dve.wait_ge(stats_done, MT * NCH)
                batch_norm(nc, dve, var_done, rstd_done, bn_step, stats, mv, var_eps, rstd, g.g1, g.beta1,
                           g.scale1, g.offset1, MT)

            @block.gpsimd
            def _(pool):
                steps = 0

                def step(instruction):
                    nonlocal steps
                    instruction.then_inc(part_step, 1)
                    steps += 1

                three_parts(nc, pool, b1_rest, g.b1_sum, b1_part, step, lambda: pool.wait_ge(part_step, steps))
                pool.wait_ge(part_step, steps)
                for m in range(3):
                    pool.dma_start(g.f1_bias[m:m + 1, :], b1_part[:, m, :]).then_inc(placed, 16)
                pool.wait_ge(placed, 3 * 16)
                pool.wait_ge(var_done, 1)
                nc.gpsimd.tensor_tensor(rstd[:], var_eps[:], g.minus_half[:, 0:MT], ALU.pow).then_inc(rstd_done, 1)

            @block.tensor
            def _(pe):
                def transposes(c, k):
                    for j in range(NT):
                        t = nc.tensor.transpose(turn_ps[:, k, j * RT:(j + 1) * RT], h_in[:, c.slot, j, k * P:(k + 1) * P],
                                                g.ident[0:RT, 0:RT])
                    t.then_inc(turned, 1)

                pe.wait_ge(h_loaded[0], 32)
                for k in range(KT):
                    transposes(Chunk(0, 0), k)

                def step(c, follow):
                    s = c.slot
                    pe.wait_ge(turn_lo, c.count(KT, KT))
                    for m in range(MT):
                        pe.wait_ge(h1_done, c.count(MT, m + 5))
                        w = slice(m * P, (m + 1) * P)
                        for k in range(KT):
                            last = split3(nc, mm_ps[:, m % 4, 0:CH], g.w1_hi[:, k, w], g.w1_lo[:, k, w],
                                          ht_hi[:, s, k, :], ht_lo[:, s, k, :], k == 0, k == KT - 1)
                        last.then_inc(mm_done, 1)
                        if follow and 1 <= m < 1 + KT:
                            if m == 1:
                                pe.wait_ge(h_loaded[c.next().slot], c.next().uses(32))
                            transposes(c.next(), m - 1)

                chunk_loop(pe, step)


def gnn_down(nc, g, a):
    K8 = 2 * KT
    AHEAD = 3
    with ExitStack() as ctx:
        def sb(name, shape, dt=F32):
            return ctx.enter_context(nc.sbuf_tensor("dn_" + name, shape, dt))

        def sems(*names):
            return [ctx.enter_context(nc.semaphore("dn_" + n)) for n in names]

        h1_in = (g.feat_in.rearrange("p s k n -> p (s k) n"), sb("h1_in", [P, K8, CH])[:])
        act_f = sb("act_f", [P, 2, CH])
        act_hi = sb("act_hi", [P, 4, CH], F16)
        act_lo = sb("act_lo", [P, 4, CH], F16)
        h2 = sb("h2", [P, 2, KT, CH])
        stats = sb("stats", [P, KT, NCH, 6])
        mv = sb("mv", [P, KT, 2])
        var_eps = sb("var_eps", [P, KT])
        rstd = sb("rstd", [P, KT])
        mm_ps = ctx.enter_context(nc.psum_tensor("dn_mm_ps", [P, 2, KT, 512], F32))
        st0, st1 = sems("stored0", "stored1")
        loaded, stored = g.h1_loaded, (st0, st1)
        silu_done, hi_done, lo_done, k_done, mm_done, h2_done, stats_done, var_done, rstd_done, bn_step = sems(
            "silu_done", "hi_done", "lo_done", "k_done", "mm_done", "h2_done", "stats_done", "var_done", "rstd_done",
            "bn_step")

        with nc.Block() as block:
            @block.sync
            def _(sp):
                load_features(sp, h1_in[1], g.h1_t, 1, loaded[1])
                dma_rows_in(sp, g.rows_in[:, 0], g.r_rows, 0, g.r_loaded[0])
                for s in range(2):
                    sp.sem_inc(stored[s], 16)

                def step(c, follow):
                    s = c.slot
                    if follow == 2:
                        wait(sp, g.sp_tick, silu_done, c.count(K8, K8))
                        load_features(sp, h1_in[s], g.h1_t, c.at + 2, loaded[s])
                    if follow == 1:
                        sp.wait_ge(silu_done, c.count(K8, K8))
                        sp.wait_ge(stored[0], 16 + 16 * (NCH // 2 - 1))
                        load_features(sp, g.feat_in[:, 0], g.h2_t, 0, g.h2_loaded[0])
                    wait(sp, g.sp_tick, h2_done, c.count(KT, KT))
                    sp.dma_start(g.h2_t[bass.ds(c.at, 1), :, :].rearrange("a p n -> (a p) n"),
                                 h2[:, s].rearrange("p m n -> p (m n)")).then_inc(stored[s], 16)

                chunk_loop(sp, step)
                for s in range(2):
                    sp.wait_ge(stored[s], 16 + 16 * NCH // 2)

            @block.scalar
            def _(act):
                def activate(c, k):
                    act.wait_ge(lo_done, c.count(K8, k + 1))
                    nc.scalar.activation(act_f[:, k % 2, :], h1_in[c.slot][:, k, :], ACT.Silu, bias=g.offset1[:, k:k + 1],
                                         scale=g.scale1[:, k:k + 1]).then_inc(silu_done, 1)
                    act.wait_ge(silu_done, c.count(K8, k + 1))
                    if k == 3:
                        need(act, mm_done, c.count(KT, 0))
                    else:
                        need(act, k_done, c.count(K8 - 1, k if k < 3 else k - 1))
                    nc.scalar.copy(act_hi[:, k % 4, :], act_f[:, k % 2, :]).then_inc(hi_done, 1)

                def read_out(c, m):
                    act.wait_ge(mm_done, c.count(KT, m + 1))
                    nc.scalar.activation(h2[:, c.slot, m, :], mm_ps[:, c.slot, m, 0:CH], ACT.Identity,
                                         bias=g.gb2[:, m:m + 1], scale=1 / WS).then_inc(h2_done, 1)

                act.wait_ge(loaded[0], 16)
                for k in range(AHEAD):
                    activate(Chunk(0, 0), k)

                def step(c, follow):
                    for k in range(AHEAD, K8):
                        activate(c, k)
                    if follow:
                        act.wait_ge(loaded[c.next().slot], c.next().uses(16))
                        for k in range(AHEAD):
                            activate(c.next(), k)
                    act.wait_ge(stored[c.slot], c.uses(16))
                    need(act, stats_done, c.count(KT, 0))
                    for m in range(KT):
                        read_out(c, m)

                chunk_loop(act, step)

            @block.vector
            def _(dve):
                dve.sem_inc(lo_done, 2)

                def low(c, k):
                    dve.wait_ge(hi_done, c.count(K8, k + 1))
                    nc.vector.tensor_tensor(act_lo[:, k % 4, :], act_f[:, k % 2, :], act_hi[:, k % 4, :],
                                            ALU.subtract).then_inc(lo_done, 1)

                for k in range(AHEAD):
                    low(Chunk(0, 0), k)

                def step(c, follow):
                    for k in range(AHEAD, K8):
                        low(c, k)
                    if follow:
                        for k in range(AHEAD):
                            low(c.next(), k)
                    for m in range(KT):
                        dve.wait_ge(h2_done, c.count(KT, m + 1))
                        nc.vector.bn_stats(stats[:, m, bass.ds(c.at, 1), :].rearrange("p a s -> p (a s)"),
                                           h2[:, c.slot, m, :]).then_inc(stats_done, 1)

                chunk_loop(dve, step)
                dve.wait_ge(stats_done, KT * NCH)
                batch_norm(nc, dve, var_done, rstd_done, bn_step, stats, mv, var_eps, rstd, g.g2, g.beta2,
                           g.scale2, g.offset2, KT)

            @block.gpsimd
            def _(pool):
                pool.wait_ge(var_done, 1)
                nc.gpsimd.tensor_tensor(rstd[:], var_eps[:], g.minus_half[:, 0:KT], ALU.pow).then_inc(rstd_done, 1)

            @block.tensor
            def _(pe):
                pe.sem_inc(k_done, 2)

                def step(c, follow):
                    for k in range(K8):
                        pe.wait_ge(lo_done, c.count(K8, 2 + k + 1))
                        if k == 0:
                            need(pe, h2_done, c.count(KT, -KT))
                        for m in range(KT):
                            w = slice(m * P, (m + 1) * P)
                            last = split3(nc, mm_ps[:, c.slot, m, 0:CH], g.w2_hi[:, k, w], g.w2_lo[:, k, w],
                                          act_hi[:, k % 4, :], act_lo[:, k % 4, :], k == 0, k == K8 - 1)
                            if k == K8 - 1:
                                last.then_inc(mm_done, 1)
                            elif m == KT - 1:
                                last.then_inc(k_done, 1)

                chunk_loop(pe, step)


def feed(nc, g, a, out):
    with ExitStack() as ctx:
        def sb(name, shape, dt=F32):
            return ctx.enter_context(nc.sbuf_tensor("ff_" + name, shape, dt))

        def sems(*names):
            return [ctx.enter_context(nc.semaphore("ff_" + n)) for n in names]

        h2_in, r_in = g.feat_in, g.rows_in
        z = sb("z", [P, KT, CH])
        y = sb("y", [RT, 2, NT, D])
        y_b = sb("y_b", [RT, 2, NT, D])
        n2 = sb("n2", [RT, 2, NT, D])
        nt_hi = sb("nt_hi", [P, NT, KT * RT], F16)
        nt_lo = sb("nt_lo", [P, NT, KT * RT], F16)
        gelu = sb("gelu", [RT, NT, FH])
        share_h = sb("share_h", [RT, NT, FH])
        gt_hi = sb("gt_hi", [P, 2, 4 * RT], F16)
        gt_lo = sb("gt_lo", [P, 2, 4 * RT], F16)
        u = sb("u", [RT, NT, D])
        u_n = sb("u_n", [RT, NT, D])
        ug = sb("ug", [RT, NT, D])
        o = sb("o", [RT, 2, NT, D])
        y_stats = sb("y_stats", [RT, NT, 6])
        y_mv = sb("y_mv", [RT, NT, 2])
        u_stats = sb("u_stats", [RT, NT, 6])
        u_mv = sb("u_mv", [RT, NT, 2])
        small = sb("small", [RT, 12, NT])
        inv2 = sb("inv2", [RT, 2, NT])
        var2 = sb("var2", [RT, 2, NT])
        u_var = sb("u_var", [RT, NT])
        u_rstd = sb("u_rstd", [RT, NT])
        logits = sb("logits", [RT, NT, NE])
        top = sb("top", [RT, NT, 8])
        top_i = sb("top_i", [RT, NT, 8], U32)
        top_f = sb("top_f", [RT, NT, 2])
        gap = sb("gap", [RT, NT])
        e_gap = sb("e_gap", [RT, NT])
        e_one = sb("e_one", [RT, NT])
        share = sb("share", [RT, 2, NT])
        is_top = sb("is_top", [RT, 2, NT, NE])
        by_top = sb("by_top", [RT, 2, NT, NE])
        shares = sb("shares", [RT, NT, NE])
        share_hi = sb("share_hi", [RT, NT, NE], F16)
        share_parts = sb("share_parts", [RT, NT, P])
        share_t = sb("share_t", [P, NT, RT], F16)
        z_ps = ctx.enter_context(nc.psum_tensor("ff_z_ps", [P, 2, 512], F32))
        turn_ps = ctx.enter_context(nc.psum_tensor("ff_turn_ps", [P, 2, 512], F32))
        f_ps = ctx.enter_context(nc.psum_tensor("ff_f_ps", [P, 2, 512], F32))
        u_ps = ctx.enter_context(nc.psum_tensor("ff_u_ps", [P, 2, 512], F32))

        h2_loaded, r_loaded, stored = g.h2_loaded, g.r_loaded, sems("stored0", "stored1")
        z_done, z_turned, y_done, y_stats_done, y_mv_done, s1_step, n2_done, n2_turned, nt_hi_done, nt_lo_done = sems(
            "z_done", "z_turned", "y_done", "y_stats_done", "y_mv_done", "s1_step", "n2_done", "n2_turned", "nt_hi_done", "nt_lo_done")
        f_done, gelu_done, logits_done, s2_step, gap_done, e_gap_done, share_step, share_h_done, inv2_done, y_b_done = sems(
            "f_done", "gelu_done", "logits_done", "s2_step", "gap_done", "e_gap_done", "share_step", "share_h_done", "inv2_done", "y_b_done")
        g_turned, s_turned, gt_hi_done, gt_lo_done, share_t_done, u_mm, u_done, u_stats_done, u_mv_done, u_step, un_done, ug_done, o_done = sems(
            "g_turned", "s_turned", "gt_hi_done", "gt_lo_done", "share_t_done", "u_mm", "u_done", "u_stats_done", "u_mv_done",
            "u_step", "un_done", "ug_done", "o_done")
        zeroed, inv2_step, parts_done = sems(
            "zeroed", "inv2_step", "parts_done")
        S1 = 9
        S2 = 10

        def stages(eng, step):
            chunk = [None] * 3 + [Chunk(n // 2, n % 2) for n in range(NCH)] + [None] * 3
            for n in range(4):
                step(chunk[n + 3], chunk[n + 2], chunk[n + 1], chunk[n], True)
            with eng.Fori(2, NCH // 2 - 1) as i:
                for s in range(2):
                    A = Chunk(i, s)
                    B = A.prev()
                    C = B.prev()
                    step(A, B, C, C.prev(), True)
            for n in range(NCH - 2, NCH + 3):
                step(chunk[n + 3], chunk[n + 2], chunk[n + 1], chunk[n], n < NCH - 1)

        def ticked(eng, tick):
            def wait_for(sem, value):
                if isinstance(value, int):
                    need(eng, sem, value)
                else:
                    wait(eng, tick, sem, value)
            return wait_for

        with nc.Block() as block:
            @block.sync
            def _(sp):
                wait_for = ticked(sp, g.sp_tick)

                sp.sem_inc(stored[0], 32)
                sp.sem_inc(stored[1], 32)

                def step(A, B, C, D, more):
                    if more:
                        n = A.next()
                        wait_for(z_done, A.count(KT, 0))
                        load_features(sp, h2_in[:, n.slot], g.h2_t, n.at, h2_loaded[n.slot])
                        wait_for(y_done, A.count(NT, 0))
                        dma_rows_in(sp, r_in[:, n.slot], g.r_rows, n.at, r_loaded[n.slot])
                    if D is not None:
                        wait_for(o_done, D.count(NT, NT))
                        dma_rows_out(sp, out, D.at, o[:, D.slot], stored[D.slot])

                stages(sp, step)
                for s in range(2):
                    sp.wait_ge(stored[s], 32 + 32 * NCH // 2)

            @block.gpsimd
            def _(pool):
                wait_for = ticked(pool, g.pool_tick)

                def step(A, B, C, D, more):
                    if D is not None:
                        wait_for(o_done, D.count(NT, 0))
                        for j in range(NT):
                            wait_for(un_done, D.count(NT, j + 1))
                            nc.gpsimd.tensor_tensor(ug[:, j, :], u_n[:, j, :], g.out_g[:], ALU.mult).then_inc(ug_done, 1)
                    if B is not None:
                        wait_for(u_done, B.count(NT, -NT))
                        nc.gpsimd.tensor_tensor(small[:, 8, :], var2[:, B.slot, :], g.half[0:RT, 0:NT], ALU.pow).then_inc(inv2_step, 1)
                        wait_for(inv2_step, B.count(1, 1))
                        nc.gpsimd.tensor_scalar(inv2[:, B.slot, :], small[:, 8, :], WS, None, ALU.mult).then_inc(inv2_done, 1)
                        wait_for(y_done, B.count(NT, NT))
                        for j in range(NT):
                            wait_for(o_done, B.count(NT, j + 1 - 2 * NT))
                            nc.gpsimd.tensor_tensor(y_b[:, B.slot, j, :], y[:, B.slot, j, :], g.out_b[:], ALU.add).then_inc(y_b_done, 1)
                    if A is not None:
                        var_eps, r1, square, v2, r2, rr, mr, nb = (small[:, n, :] for n in range(8))
                        wait_for(n2_done, A.count(NT, 0))
                        wait_for(y_mv_done, A.count(NT, NT))
                        nc.gpsimd.tensor_scalar(var_eps, y_mv[:, :, 1], LN_EPS, None, ALU.add).then_inc(s1_step, 1)
                        wait_for(s1_step, A.count(S1, 1))
                        nc.gpsimd.tensor_tensor(r1, var_eps, g.minus_half[0:RT, 0:NT], ALU.pow).then_inc(s1_step, 1)
                        wait_for(s1_step, A.count(S1, 2))
                        nc.gpsimd.tensor_tensor(square, r1, r1, ALU.mult).then_inc(s1_step, 1)
                        wait_for(s1_step, A.count(S1, 3))
                        nc.gpsimd.tensor_tensor(v2, square, y_mv[:, :, 1], ALU.mult).then_inc(s1_step, 1)
                        wait_for(s1_step, A.count(S1, 4))
                        nc.gpsimd.tensor_scalar(var2[:, A.slot, :], v2, LN_EPS, None, ALU.add).then_inc(s1_step, 1)
                        wait_for(s1_step, A.count(S1, 5))
                        nc.gpsimd.tensor_tensor(r2, var2[:, A.slot, :], g.minus_half[0:RT, 0:NT], ALU.pow).then_inc(s1_step, 1)
                        wait_for(s1_step, A.count(S1, 6))
                        nc.gpsimd.tensor_tensor(rr, r1, r2, ALU.mult).then_inc(s1_step, 1)
                        wait_for(s1_step, A.count(S1, 7))
                        nc.gpsimd.tensor_tensor(mr, y_mv[:, :, 0], rr, ALU.mult).then_inc(s1_step, 1)
                        wait_for(s1_step, A.count(S1, 8))
                        nc.gpsimd.tensor_scalar(nb, mr, -1.0, None, ALU.mult).then_inc(s1_step, 1)
                    if C is not None:
                        wait_for(un_done, C.count(NT, 0))
                        wait_for(u_mv_done, C.count(NT, NT))
                        nc.gpsimd.tensor_scalar(u_var[:], u_mv[:, :, 1], LN_EPS * WS * WS, None, ALU.add).then_inc(u_step, 1)
                        wait_for(u_step, C.count(4, 1))
                        nc.gpsimd.tensor_tensor(u_rstd[:], u_var[:], g.minus_half[0:RT, 0:NT], ALU.pow).then_inc(u_step, 1)
                        wait_for(u_step, C.count(4, 2))
                        nc.gpsimd.tensor_tensor(small[:, 9, :], u_mv[:, :, 0], u_rstd[:], ALU.mult).then_inc(u_step, 1)
                        wait_for(u_step, C.count(4, 3))
                        nc.gpsimd.tensor_scalar(small[:, 10, :], small[:, 9, :], -1.0, None, ALU.mult).then_inc(u_step, 1)

                stages(pool, step)

            @block.scalar
            def _(act):
                def silu(c):
                    act.wait_ge(h2_loaded[c.slot], c.uses(16))
                    need(act, z_turned, c.count(NT, 0))
                    for k in range(KT):
                        nc.scalar.activation(z[:, k, :], h2_in[:, c.slot, k, :], ACT.Silu, bias=g.offset2[:, k:k + 1],
                                             scale=g.scale2[:, k:k + 1]).then_inc(z_done, 1)

                silu(Chunk(0, 0))

                def step(A, B, C, D, more):
                    def gelu_of(j):
                        act.wait_ge(f_done, B.count(NT, j + 1))
                        nc.scalar.activation(gelu[:, j, :], f_ps[0:RT, j % 2, 0:FH], ACT.Gelu_apprx_tanh,
                                             scale=1 / WS).then_inc(gelu_done, 1)

                    def turned_high(pair):
                        act.wait_ge(g_turned, C.count(2, pair + 1))
                        nc.scalar.copy(gt_hi[:, pair, :], turn_ps[:, pair, 0:4 * RT]).then_inc(gt_hi_done, 1)

                    def n2_high(j):
                        act.wait_ge(n2_turned, B.count(NT, j + 1))
                        nc.scalar.copy(nt_hi[:, j, :], turn_ps[:, j % 2, 0:KT * RT]).then_inc(nt_hi_done, 1)

                    def u_normalised(j):
                        nc.scalar.activation(u_n[:, j, :], u[:, j, :], ACT.Identity, bias=small[:, 10, j:j + 1],
                                             scale=u_rstd[:, j:j + 1]).then_inc(un_done, 1)

                    if B is not None:
                        need(act, f_done, B.count(NT, 0))
                        n2_high(0)
                        n2_high(1)
                    if D is not None:
                        need(act, ug_done, D.count(NT, 0))
                        act.wait_ge(u_step, D.count(4, 4))
                        u_normalised(0)
                        u_normalised(1)
                    if B is not None:
                        n2_high(2)
                    if D is not None:
                        u_normalised(2)
                        u_normalised(3)
                    if B is not None:
                        n2_high(3)
                        need(act, share_h_done, B.count(NT, 0))
                        gelu_of(0)
                        gelu_of(1)
                    if C is not None:
                        need(act, u_mm, C.count(NT, 0))
                        turned_high(0)
                    if B is not None:
                        gelu_of(2)
                    if C is not None:
                        turned_high(1)
                        act.wait_ge(s_turned, C.count(1, 1))
                        nc.scalar.copy(share_t[:].rearrange("p j n -> p (j n)"), turn_ps[:, 0, 0:NT * RT]).then_inc(share_t_done, 1)
                    if B is not None:
                        gelu_of(3)
                    if B is not None:
                        act.wait_ge(gap_done, B.count(1, 1))
                        nc.scalar.activation(e_gap[:], gap[:], ACT.Exp).then_inc(e_gap_done, 1)
                    if more:
                        silu(A.next())
                    if A is not None:
                        act.wait_ge(s1_step, A.count(S1, S1))
                        for j in range(NT):
                            need(act, u_done, A.count(NT, j + 1 - 2 * NT))
                            nc.scalar.activation(n2[:, A.slot, j, :], y[:, A.slot, j, :], ACT.Identity,
                                                 bias=small[:, 7, j:j + 1], scale=small[:, 5, j:j + 1]).then_inc(n2_done, 1)

                stages(act, step)

            @block.vector
            def _(dve):
                nc.vector.memset(share_parts[:], 0.0).then_inc(zeroed, 1)
                dve.wait_ge(zeroed, 1)
                wait_for = ticked(dve, g.dve_tick)

                def head_shares(t, k):
                    return t.unsqueeze(2).to_broadcast([RT, NT, k])

                def y_sum(c, j):
                    if j == 0:
                        dve.wait_ge(r_loaded[c.slot], c.uses(32))
                    need(dve, y_b_done, c.count(NT, j + 1 - 2 * NT))
                    dve.wait_ge(z_turned, c.count(NT, j + 1))
                    nc.vector.tensor_tensor(y[:, c.slot, j, :], z_ps[0:RT, j % 2, :], r_in[:, c.slot, j, :],
                                            ALU.add).then_inc(y_done, 1)

                for j in range(NT):
                    y_sum(Chunk(0, 0), j)

                def step(A, B, C, D, more):
                    S = 9

                    def y_stat(j):
                        dve.wait_ge(y_done, A.count(NT, j + 1))
                        nc.vector.bn_stats(y_stats[:, j, :], y[:, A.slot, j, :]).then_inc(y_stats_done, 1)

                    def n2_low(j):
                        dve.wait_ge(nt_hi_done, B.count(NT, j + 1))
                        nc.vector.tensor_tensor(nt_lo[:, j, :], turn_ps[:, j % 2, 0:KT * RT], nt_hi[:, j, :],
                                                ALU.subtract).then_inc(nt_lo_done, 1)

                    def g_low(pair):
                        dve.wait_ge(gt_hi_done, C.count(2, pair + 1))
                        nc.vector.tensor_tensor(gt_lo[:, pair, :], turn_ps[:, pair, 0:4 * RT], gt_hi[:, pair, :],
                                                ALU.subtract).then_inc(gt_lo_done, 1)

                    def logits_of(j):
                        dve.wait_ge(gelu_done, B.count(NT, j + 1))
                        nc.vector.tensor_scalar(logits[:, j, :], f_ps[0:RT, j % 2, FH:F1], 1 / WS, None,
                                                ALU.mult).then_inc(logits_done, 1)

                    def u_sum(j):
                        dve.wait_ge(u_mm, C.count(NT, j + 1))
                        need(dve, un_done, C.count(NT, 0))
                        nc.vector.scalar_tensor_tensor(u[:, j, :], n2[:, C.slot, j, :], inv2[:, C.slot, j:j + 1], u_ps[0:RT, j % 2, :],
                                                       ALU.mult, ALU.add).then_inc(u_done, 1)

                    def u_stat(j):
                        dve.wait_ge(u_done, C.count(NT, j + 1))
                        nc.vector.bn_stats(u_stats[:, j, :], u[:, j, :]).then_inc(u_stats_done, 1)

                    def finish(j):
                        dve.wait_ge(ug_done, D.count(NT, j + 1))
                        nc.vector.tensor_tensor(o[:, D.slot, j, :], ug[:, j, :], y_b[:, D.slot, j, :], ALU.add).then_inc(o_done, 1)

                    if B is not None:
                        n2_low(0)
                        n2_low(1)
                    if C is not None:
                        wait_for(share_step, C.count(S, 8))
                        nc.vector.tensor_copy(share_hi[:], shares[:]).then_inc(share_step, 1)
                        wait_for(g_turned, C.count(2, 0))
                        for j in range(NT):
                            dve.wait_ge(gelu_done, C.count(NT, j + 1))
                            nc.vector.tensor_tensor(share_h[:, j, :].rearrange("p (e h) -> p e h", e=NE),
                                                    gelu[:, j, :].rearrange("p (e h) -> p e h", e=NE),
                                                    shares[:, j, :].unsqueeze(2).to_broadcast([RT, NE, EH]),
                                                    ALU.mult).then_inc(share_h_done, 1)
                        wait_for(s_turned, C.count(1, 0))
                        wait_for(share_step, C.count(S, 9))
                        nc.vector.tensor_copy(share_parts[:, :, 0:NE], share_hi[:]).then_inc(parts_done, 1)
                        nc.vector.tensor_tensor(share_parts[:, :, NE:2 * NE], shares[:], share_hi[:],
                                                ALU.subtract).then_inc(parts_done, 1)
                        nc.vector.tensor_copy(share_parts[:, :, 2 * NE:3 * NE], share_hi[:]).then_inc(parts_done, 1)
                    if A is not None:
                        y_stat(0)
                    if B is not None:
                        n2_low(2)
                    if A is not None:
                        y_stat(1)
                        y_stat(2)
                    if B is not None:
                        n2_low(3)
                        logits_of(0)
                    if A is not None:
                        y_stat(3)
                    if B is not None:
                        logits_of(1)
                    if C is not None:
                        g_low(0)
                    if A is not None:
                        wait_for(s1_step, A.count(S1, 0))
                        wait_for(y_stats_done, A.count(NT, NT))
                        for j in range(NT):
                            nc.vector.bn_aggr(y_mv[:, j, :], y_stats[:, j, :]).then_inc(y_mv_done, 1)
                    if D is not None:
                        wait_for(y_b_done, D.count(NT, NT))
                        wait_for(stored[D.slot], D.uses(32))
                        finish(0)
                    if B is not None:
                        logits_of(2)
                    if C is not None:
                        g_low(1)
                    if D is not None:
                        finish(1)
                        finish(2)
                        finish(3)
                    if B is not None:
                        logits_of(3)
                        wait_for(logits_done, B.count(NT, NT))
                        for j in range(NT):
                            nc.vector.max(top[:, j, :], logits[:, j, :]).then_inc(s2_step, 1)
                        wait_for(s2_step, B.count(S2, NT))
                        nc.vector.tensor_tensor(gap[:], top[:, :, 1], top[:, :, 0], ALU.subtract).then_inc(gap_done, 1)
                        for j in range(NT):
                            nc.vector.max_index(top_i[:, j, :], top[:, j, :], logits[:, j, :]).then_inc(s2_step, 1)
                    if C is not None:
                        wait_for(inv2_done, C.count(1, 1))
                        u_sum(0)
                    if B is not None:
                        wait_for(s2_step, B.count(S2, 2 * NT))
                        nc.vector.tensor_copy(top_f[:], top_i[:, :, 0:2]).then_inc(s2_step, 2)
                    if C is not None:
                        u_stat(0)
                        u_sum(1)
                    if B is not None:
                        for t in range(2):
                            wait_for(s2_step, B.count(S2, S2))
                            nc.vector.tensor_tensor(is_top[:, t], g.expert[:], head_shares(top_f[:, :, t], NE),
                                                    ALU.is_equal).then_inc(share_step, 1)
                        wait_for(e_gap_done, B.count(1, 1))
                        nc.vector.tensor_scalar(e_one[:], e_gap[:], 1.0, None, ALU.add).then_inc(share_step, 1)
                    if C is not None:
                        u_stat(1)
                    if B is not None:
                        wait_for(share_step, B.count(S, 3))
                        nc.vector.reciprocal(share[:, 0, :], e_one[:]).then_inc(share_step, 1)
                    if C is not None:
                        u_sum(2)
                    if B is not None:
                        wait_for(share_step, B.count(S, 4))
                        nc.vector.tensor_tensor(share[:, 1, :], e_gap[:], share[:, 0, :], ALU.mult).then_inc(share_step, 1)
                    if C is not None:
                        u_stat(2)
                    if B is not None:
                        wait_for(share_step, B.count(S, 5))
                        for t in range(2):
                            nc.vector.tensor_tensor(by_top[:, t], is_top[:, t], head_shares(share[:, t, :], NE),
                                                    ALU.mult).then_inc(share_step, 1)
                    if C is not None:
                        u_sum(3)
                    if B is not None:
                        wait_for(share_step, B.count(S, 7))
                        nc.vector.tensor_tensor(shares[:], by_top[:, 0], by_top[:, 1], ALU.add).then_inc(share_step, 1)
                    if more:
                        y_sum(A.next(), 0)
                        y_sum(A.next(), 1)
                    if C is not None:
                        u_stat(3)
                        wait_for(u_step, C.count(4, 0))
                        wait_for(u_stats_done, C.count(NT, NT))
                        for j in range(NT):
                            nc.vector.bn_aggr(u_mv[:, j, :], u_stats[:, j, :]).then_inc(u_mv_done, 1)
                    if more:
                        y_sum(A.next(), 2)
                        y_sum(A.next(), 3)

                stages(dve, step)

            @block.tensor
            def _(pe):
                def step(A, B, C, D, more):
                    def turn_n2(j):
                        if j == 0:
                            need(pe, share_t_done, B.count(1, -1))
                        elif j == 1:
                            need(pe, gt_lo_done, B.count(2, -2))
                        else:
                            pe.wait_ge(nt_lo_done, B.count(NT, j - 1))
                        pe.wait_ge(n2_done, B.count(NT, j + 1))
                        for k in range(KT):
                            t = nc.tensor.transpose(turn_ps[:, j % 2, k * RT:(k + 1) * RT], n2[:, B.slot, j, k * P:(k + 1) * P],
                                                    g.ident[0:RT, 0:RT])
                        t.then_inc(n2_turned, 1)

                    def turn_hidden(pair):
                        if B is not None:
                            pe.wait_ge(nt_lo_done, B.count(NT, pair + 3))
                        elif pair == 0:
                            need(pe, share_t_done, C.count(1, 0))
                        else:
                            need(pe, gt_lo_done, C.count(2, 0))
                        for j in (2 * pair, 2 * pair + 1):
                            pe.wait_ge(share_h_done, C.count(NT, j + 1))
                            for b in range(2):
                                at = (j % 2 * 2 + b) * RT
                                t = nc.tensor.transpose(turn_ps[:, pair, at:at + RT], share_h[:, j, b * P:(b + 1) * P],
                                                        g.ident[0:RT, 0:RT])
                        t.then_inc(g_turned, 1)

                    def turn_shares():
                        pe.wait_ge(gt_lo_done, C.count(2, 1))
                        pe.wait_ge(parts_done, C.count(3, 3))
                        for j in range(NT):
                            t = nc.tensor.transpose(turn_ps[:, 0, j * RT:(j + 1) * RT], share_parts[:, j, :], g.ident[0:RT, 0:RT])
                        t.then_inc(s_turned, 1)

                    def hidden(j):
                        pe.wait_ge(nt_lo_done, B.count(NT, j + 1))
                        need(pe, logits_done, B.count(NT, j - 1))
                        for k in range(KT):
                            ks = slice(k * RT, (k + 1) * RT)
                            split3(nc, f_ps[0:RT, j % 2, 0:F1], nt_hi[:, j, ks], nt_lo[:, j, ks],
                                   g.f1_hi[:, k, :], g.f1_lo[:, k, :], k == 0, False)
                        nc.tensor.matmul(f_ps[0:RT, j % 2, 0:F1], g.ones_w[:], g.f1_bias[:], start=False, stop=True,
                                         skip_group_check=True).then_inc(f_done, 1)

                    def output(j):
                        pe.wait_ge(gt_lo_done, C.count(2, j // 2 + 1))
                        need(pe, u_done, C.count(NT, j - 1))
                        for b in range(2):
                            at = (j % 2 * 2 + b) * RT
                            split3(nc, u_ps[0:RT, j % 2, :], gt_hi[:, j // 2, at:at + RT], gt_lo[:, j // 2, at:at + RT],
                                   g.f2_hi[:, b, :], g.f2_lo[:, b, :], b == 0, False)
                        nc.tensor.matmul(u_ps[0:RT, j % 2, :], share_t[:, j, :], g.eb2[:], start=False, stop=True,
                                         skip_group_check=True).then_inc(u_mm, 1)

                    if A is not None:
                        pe.wait_ge(z_done, A.count(KT, KT))
                        for j in range(NT):
                            need(pe, y_done, A.count(NT, j - 1))
                            for k in range(KT):
                                t = nc.tensor.transpose(z_ps[0:RT, j % 2, k * P:(k + 1) * P], z[:, k, j * RT:(j + 1) * RT], g.ident[:])
                            t.then_inc(z_turned, 1)
                    if B is not None:
                        turn_n2(0)
                        turn_n2(1)
                        turn_n2(2)
                        hidden(0)
                        turn_n2(3)
                        hidden(1)
                    if C is not None:
                        turn_hidden(0)
                    if B is not None:
                        hidden(2)
                    if C is not None:
                        turn_hidden(1)
                        turn_shares()
                    if B is not None:
                        hidden(3)
                    if C is not None:
                        pe.wait_ge(share_t_done, C.count(1, 1))
                        for j in range(NT):
                            output(j)

                stages(pe, step)


def build(nc, a, out):
    with ExitStack() as ctx:
        g = Parts()

        def keep(name, shape, dt=F32):
            return ctx.enter_context(nc.sbuf_tensor(name, shape, dt))

        g.h_rows = nc.dram_tensor("h_rows", [N + RT, D], F32, kind="Internal").ap()
        g.q_t = nc.dram_tensor("q_t", [NCH, P, KT * CH], F32, kind="Internal").ap()
        g.r_rows = nc.dram_tensor("r_rows", [N, D], F32, kind="Internal").ap()
        g.h1_t = nc.dram_tensor("h1_t", [NCH, P, 2 * KT * CH], F32, kind="Internal").ap()
        g.h2_t = nc.dram_tensor("h2_t", [NCH, P, KT * CH], F32, kind="Internal").ap()
        g.ident = keep("ident", [P, P])
        g.ident_h = keep("ident_h", [P, P], F16)
        g.before = keep("before", [RT, RT])
        g.head_mask = keep("head_mask", [P, P])
        g.spread = keep("spread", [P, D], F16)
        g.trash = keep("trash", [RT, 1])
        g.expert = keep("expert", [RT, NT, NE])
        g.minus_half = keep("minus_half", [P, 2 * KT])
        g.half = keep("half", [P, 2 * KT])
        g.zeros_h = keep("zeros_h", [P, D], F16)
        g.ones_col = keep("ones_col", [P, 1], F16)
        g.ones_w = keep("ones_w", [P, RT], F16)
        g.ones_q = keep("ones_q", [P, RT], F16)
        g.eps = keep("eps", [RT, 1])
        g.one_eps = keep("one_eps", [RT, 1])
        g.gb1, g.g1, g.beta1 = (keep(n, [P, 2 * KT]) for n in ("gb1", "g1", "beta1"))
        g.gb2, g.g2, g.beta2 = (keep(n, [P, KT]) for n in ("gb2", "g2", "beta2"))
        g.we = keep("we", [ED + 1, D])
        g.out_g, g.out_b = (keep(n, [RT, D]) for n in ("out_g", "out_b"))
        g.f1_hi, g.f1_lo = (keep(n, [P, KT, F1], F16) for n in ("f1_hi", "f1_lo"))
        g.f2_hi, g.f2_lo = (keep(n, [P, 2, D], F16) for n in ("f2_hi", "f2_lo"))
        g.f1_bias = keep("f1_bias", [P, F1], F16)
        g.out_bias = keep("out_bias", [P, D], F16)
        g.eb2 = keep("eb2", [P, D], F16)
        g.scale1, g.offset1 = (keep(n, [P, 2 * KT]) for n in ("scale1", "offset1"))
        g.scale2, g.offset2 = (keep(n, [P, KT]) for n in ("scale2", "offset2"))
        g.rows_in = keep("rows_in", [RT, 2, NT, D])
        g.feat_in = keep("feat_in", [P, 2, KT, CH])
        g.q_loaded, g.x_loaded, g.h_loaded, g.h1_loaded, g.r_loaded, g.h2_loaded = (
            [ctx.enter_context(nc.semaphore(f"g_{name}{slot}")) for slot in range(2)]
            for name in ("q_loaded", "x_loaded", "h_loaded", "h1_loaded", "r_loaded", "h2_loaded"))
        g.sp_tick, g.pool_tick, g.dve_tick = (ctx.enter_context(nc.semaphore(n)) for n in ("sp_tick", "pool_tick", "dve_tick"))
        g.w_in = ctx.enter_context(nc.semaphore("w_in"))
        g.px_loaded, g.qkv_loaded = ([ctx.enter_context(nc.semaphore(f"{name}{n}")) for n in range(count)]
                                     for name, count in (("px_loaded", 2), ("qkv_loaded", 3)))
        g.ea_in, g.small_in = (ctx.enter_context(nc.semaphore(n)) for n in ("ea_in", "small_in"))
        g.b1_row, g.b1_sum = (keep(n, [1, F1]) for n in ("b1_row", "b1_sum"))
        with ExitStack() as messages:
            g.kv = messages.enter_context(nc.sbuf_tensor("kv", [P, KT, P], F32))
            g.k_sum = messages.enter_context(nc.sbuf_tensor("k_sum", [P, KT, TWICE], F32))
            g.totals = messages.enter_context(nc.sbuf_tensor("totals", [P, NCH, D], F32))
            g.qkv_f = g.totals[:, NCH - 3 * KT:NCH, :].rearrange("p (w k) n -> p w k n", w=3)
            g.ea = g.totals[0:RT, 4:NCH - 3 * KT, :].rearrange("p t d -> p (t d)")[:, 0:NCH * ED].rearrange("p (t f) -> p t f", f=ED)
            g.target = messages.enter_context(nc.sbuf_tensor("target", [RT, NCH], I32))
            with ExitStack() as first:
                g.zeros = first.enter_context(nc.sbuf_tensor("zeros", [RT, D], F32))
                g.ea_t = first.enter_context(nc.sbuf_tensor("ea_t", [ED + 1, E], F32))
                g.wqkv_hi, g.wqkv_lo = (first.enter_context(nc.sbuf_tensor(n, [P, KT, 3 * D], F16))
                                        for n in ("wqkv_hi", "wqkv_lo"))
                setup(nc, g, a)
                project(nc, g, a)
            g.w1_hi, g.w1_lo = (messages.enter_context(nc.sbuf_tensor(n, [P, KT, 2 * D], F16)) for n in ("w1_hi", "w1_lo"))
            g.w2_hi, g.w2_lo = (messages.enter_context(nc.sbuf_tensor(n, [P, 2 * KT, D], F16)) for n in ("w2_hi", "w2_lo"))
            attend(nc, g, a)
            gnn_up(nc, g, a)
            gnn_down(nc, g, a)
        feed(nc, g, a, out)


def constants():
    import numpy as np

    ident = np.eye(P, dtype=np.float32)
    p = np.arange(P)
    before = (p[:RT, None] < p[None, :RT]).astype(np.float32).T.copy()
    spread = np.zeros((P, D), np.float16)
    for at in (0, TWICE - HEADS):
        spread[at:at + HEADS] = np.kron(np.eye(HEADS), np.ones((1, HD)))
    return {
        "c_ident": ident,
        "c_ident_h": ident.astype(np.float16),
        "c_before": before,
        "c_head_mask": np.kron(np.eye(2), np.ones((HD, HD))).astype(np.float32),
        "c_spread": spread,
        "c_trash": (N + p[:RT, None]).astype(np.float32),
        "c_expert": np.tile(np.arange(NE, dtype=np.float32), (NT, 1)),
    }


def kernel(**inputs):
    import numpy as np
    import concourse.bacc as bacc
    from concourse.bass_utils import run_bass_kernel_spmd

    nc = bacc.Bacc("TRN2", target_bir_lowering=False, num_devices=1)
    arrays, a = {}, {}
    for name, value in [*inputs.items(), *constants().items()]:
        v = np.ascontiguousarray(value)
        if name == "L0_gnn_eps":
            v = v.reshape(1)
        arrays[f"in_{name}"] = v
        a[name] = nc.dram_tensor(f"in_{name}", v.shape, mybir.dt.from_np(v.dtype), kind="ExternalInput").ap()
    out = nc.dram_tensor("out", [N, D], F32, kind="ExternalOutput").ap()
    build(nc, a, out)
    r = run_bass_kernel_spmd(nc, [arrays], core_ids=[0])
    return r.results[0]["out"]
```
